# Optimizing a Trainium2 kernel written in Bass

```python
import numpy as np
import jax
import jax.numpy as jnp

def _softmax(x, axis=-1):
    return jax.nn.softmax(x, axis=axis)
def _gelu(x):
    return jax.nn.gelu(x, approximate=True)
def _silu(x):
    return jax.nn.silu(x)
def _sigmoid(x):
    return jax.nn.sigmoid(x)
def _layernorm(x, axis=-1, eps=1e-5):
    m = jnp.mean(x, axis=axis, keepdims=True)
    v = jnp.var(x, axis=axis, keepdims=True)
    return (x - m) / jnp.sqrt(v + eps)
def _scatter_add(tgt, idx, src, axis=0):
    return tgt.at[idx].add(src)
def _segment_sum(src, seg, n):
    return jax.ops.segment_sum(src, seg, n)

kernel_name = 'mk_conv_attn_hybrid_d2_conv_nhwc256_f9d7fa'

def setup_inputs(seed: int = 0):
    np.random.seed(seed)
    _w = jnp.asarray
    def _rec_inputs():
        import jax
        import jax.numpy as jnp
        _gk = jax.random.key(seed)
        x = -0.0005153 + 1.001 * jax.random.normal(jax.random.fold_in(_gk, 1), (4, 56, 56, 256), jnp.float32)
        return x
    x = _rec_inputs()
    def _L0_conv_setup():
        import jax, jax.numpy as jnp
        import numpy as np
        NUM_HEADS = 8
        KERNEL = 7
        LOW_RANK = 4
        key = jax.random.key(seed)
        ks = jax.random.split(key, 10)
        B, H, W, C = (4, 56, 56, 256)
        nh, K, lr = (NUM_HEADS, KERNEL, LOW_RANK)
        s = 0.02
        return {'x': jax.random.normal(ks[0], (B, H, W, C), jnp.float32), 'Wq': jax.random.normal(ks[1], (C, nh * lr), jnp.float32) * s, 'bq': jnp.zeros((nh * lr,), jnp.float32), 'Wk': jax.random.normal(ks[2], (C, nh * lr), jnp.float32) * s, 'bk': jnp.zeros((nh * lr,), jnp.float32), 'Wv': jax.random.normal(ks[3], (C, C), jnp.float32) * s, 'bv': jnp.zeros((C,), jnp.float32), 'rpb': jax.random.normal(ks[4], (nh, 2 * K - 1, 2 * K - 1), jnp.float32) * s, 'Wp': jax.random.normal(ks[5], (C, C), jnp.float32) * s, 'bp': jnp.zeros((C,), jnp.float32)}
    _L0_conv_all = _L0_conv_setup()
    _L0_conv_in = {k: v for k, v in _L0_conv_all.items() if k in ('Wq', 'bq', 'Wk', 'bk', 'Wv', 'bv', 'rpb', 'Wp', 'bp', )}
    del _L0_conv_all

    def _L1_attn_setup():
        import jax, jax.numpy as jnp
        import numpy as np
        HEADS = 8
        key = jax.random.key(seed)
        k1, k2, k3 = jax.random.split(key, 3)
        b, n, d = (4, 2048, 256)
        x = jax.random.normal(k1, (b, n, d), dtype=jnp.float32)
        w_qkv = jax.random.normal(k2, (d, 3 * d), dtype=jnp.float32) * d ** (-0.5)
        b_qkv = jnp.zeros((3 * d,), dtype=jnp.float32)
        w_out = jax.random.normal(k3, (d, d), dtype=jnp.float32) * d ** (-0.5)
        b_out = jnp.zeros((d,), dtype=jnp.float32)
        return {'x': x, 'w_qkv': w_qkv, 'b_qkv': b_qkv, 'w_out': w_out, 'b_out': b_out}
    _L1_attn_all = _L1_attn_setup()
    _L1_attn_in = {k: v for k, v in _L1_attn_all.items() if k in ('w_qkv', 'b_qkv', 'w_out', 'b_out', )}
    del _L1_attn_all

    def _L1_ffn_setup():
        import math
        import jax, jax.numpy as jnp
        import numpy as np
        CAPACITY_FACTOR = 1.25
        key = jax.random.key(seed)
        ks = jax.random.split(key, 5)
        B, L, D, F, E = (8, 8192, 256, 1024, 8)
        h = jax.random.normal(ks[0], (B, L, D), dtype=jnp.float32)
        gate_w = jax.random.normal(ks[1], (D, E), dtype=jnp.float32) * 0.02
        gate_b = jnp.zeros((E,), dtype=jnp.float32)
        w1 = jax.random.normal(ks[2], (E, D, F), dtype=jnp.float32) * (1.0 / math.sqrt(D))
        b1 = jnp.zeros((E, F), dtype=jnp.float32)
        w2 = jax.random.normal(ks[3], (E, F, D), dtype=jnp.float32) * (1.0 / math.sqrt(F))
        b2 = jnp.zeros((E, D), dtype=jnp.float32)
        return {'h': h, 'gate_w': gate_w, 'gate_b': gate_b, 'w1': w1, 'b1': b1, 'w2': w2, 'b2': b2}
    _L1_ffn_all = _L1_ffn_setup()
    _L1_ffn_in = {k: v for k, v in _L1_ffn_all.items() if k in ('gate_w', 'gate_b', 'w1', 'b1', 'w2', 'b2', )}
    del _L1_ffn_all

    return {
        "x": x,
        "L0_conv_Wq": _L0_conv_in["Wq"],
        "L0_conv_bq": _L0_conv_in["bq"],
        "L0_conv_Wk": _L0_conv_in["Wk"],
        "L0_conv_bk": _L0_conv_in["bk"],
        "L0_conv_Wv": _L0_conv_in["Wv"],
        "L0_conv_bv": _L0_conv_in["bv"],
        "L0_conv_rpb": _L0_conv_in["rpb"],
        "L0_conv_Wp": _L0_conv_in["Wp"],
        "L0_conv_bp": _L0_conv_in["bp"],
        "L1_attn_w_qkv": _L1_attn_in["w_qkv"],
        "L1_attn_b_qkv": _L1_attn_in["b_qkv"],
        "L1_attn_w_out": _L1_attn_in["w_out"],
        "L1_attn_b_out": _L1_attn_in["b_out"],
        "L1_ffn_gate_w": _L1_ffn_in["gate_w"],
        "L1_ffn_gate_b": _L1_ffn_in["gate_b"],
        "L1_ffn_w1": _L1_ffn_in["w1"],
        "L1_ffn_b1": _L1_ffn_in["b1"],
        "L1_ffn_w2": _L1_ffn_in["w2"],
        "L1_ffn_b2": _L1_ffn_in["b2"],
    }

def reference(x, L0_conv_Wq, L0_conv_bq, L0_conv_Wk, L0_conv_bk, L0_conv_Wv, L0_conv_bv, L0_conv_rpb, L0_conv_Wp, L0_conv_bp, L1_attn_w_qkv, L1_attn_b_qkv, L1_attn_w_out, L1_attn_b_out, L1_ffn_gate_w, L1_ffn_gate_b, L1_ffn_w1, L1_ffn_b1, L1_ffn_w2, L1_ffn_b2):
    import jax
    import jax.numpy as jnp
    def _L0_conv_ref(x, Wq, bq, Wk, bk, Wv, bv, rpb, Wp, bp):
        import jax, jax.numpy as jnp
        import numpy as np
        NUM_HEADS = 8
        KERNEL = 7
        LOW_RANK = 4
        B, H, W, C = x.shape
        nh, K, lr = (NUM_HEADS, KERNEL, LOW_RANK)
        hd = C // nh
        r = K // 2
        scale = hd ** (-0.5)
        q = (x @ Wq + bq).reshape(B, nh, H, W, lr) * scale
        k = (x @ Wk + bk).reshape(B, nh, H, W, lr)
        v = (x @ Wv + bv).reshape(B, nh, H, W, hd)
        start_h = jnp.clip(jnp.arange(H) - r, 0, H - K)
        start_w = jnp.clip(jnp.arange(W) - r, 0, W - K)
        idx_h = start_h[:, None] + jnp.arange(K)[None, :]
        idx_w = start_w[:, None] + jnp.arange(K)[None, :]
        k_win = k[:, :, idx_h][:, :, :, :, idx_w]
        v_win = v[:, :, idx_h][:, :, :, :, idx_w]
        attn = jnp.einsum('bhijc,bhikjlc->bhijkl', q, k_win)
        bi = idx_h - jnp.arange(H)[:, None] + (K - 1)
        bj = idx_w - jnp.arange(W)[:, None] + (K - 1)
        bias = rpb[:, bi][:, :, :, bj]
        attn = attn + bias.transpose(0, 1, 3, 2, 4)[None]
        attn = jax.nn.softmax(attn.reshape(B, nh, H, W, K * K), axis=-1)
        attn = attn.reshape(B, nh, H, W, K, K)
        out = jnp.einsum('bhijkl,bhikjld->bhijd', attn, v_win)
        out = out.transpose(0, 2, 3, 1, 4).reshape(B, H, W, C)
        return out @ Wp + bp

    def _L1_attn_ref(x, w_qkv, b_qkv, w_out, b_out):
        import jax, jax.numpy as jnp
        import numpy as np
        HEADS = 8
        b, n, d = x.shape
        h = HEADS
        dh = d // h
        scale = d ** (-0.5)
        qkv = x @ w_qkv + b_qkv
        q, k, v = jnp.split(qkv, 3, axis=-1)
        to_heads = lambda t: t.reshape(b, n, h, dh).transpose(0, 2, 1, 3)
        q, k, v = (to_heads(q), to_heads(k), to_heads(v))
        dots = jnp.einsum('bhid,bhjd->bhij', q, k) * scale
        attn = jax.nn.softmax(dots, axis=-1)
        out = jnp.einsum('bhij,bhjd->bhid', attn, v)
        out = out.transpose(0, 2, 1, 3).reshape(b, n, d)
        return out @ w_out + b_out

    def _L1_ffn_ref(h, gate_w, gate_b, w1, b1, w2, b2):
        import math
        import jax, jax.numpy as jnp
        import numpy as np
        CAPACITY_FACTOR = 1.25
        B, L, D = h.shape
        E = gate_w.shape[1]
        T = B * L
        C = max(1, math.ceil(CAPACITY_FACTOR * T / E))
        x = h.reshape(T, D)
        logits = x @ gate_w + gate_b
        probs = jax.nn.softmax(logits, axis=-1)
        idx = jnp.argmax(probs, axis=-1)
        prb = jnp.take_along_axis(probs, idx[:, None], axis=1)[:, 0]
        one_hot = jax.nn.one_hot(idx, E, dtype=jnp.float32)
        pos = (jnp.cumsum(one_hot, axis=0) * one_hot).sum(-1).astype(jnp.int32) - 1
        kept = pos < C
        pos_safe = jnp.where(kept, pos, C)
        buf = jnp.zeros((E, C, D), dtype=h.dtype).at[idx, pos_safe].set(x, mode='drop')
        hmid = jax.nn.relu(jnp.einsum('ecd,edf->ecf', buf, w1) + b1[:, None, :])
        ybuf = jnp.einsum('ecf,efd->ecd', hmid, w2) + b2[:, None, :]
        pos_g = jnp.minimum(pos, C - 1)
        y_tok = ybuf[idx, pos_g] * (prb * kept)[:, None]
        y = y_tok.reshape(B, L, D)
        y = jnp.nan_to_num(y, nan=0.0, posinf=10000.0, neginf=-10000.0)
        return y

    def _gn(v, G=32, eps=1e-5):
        B_, H_, W_, C_ = v.shape
        g = v.reshape(B_, H_, W_, G, C_ // G)
        m = jnp.mean(g, axis=(1, 2, 4), keepdims=True)
        s = jnp.var(g, axis=(1, 2, 4), keepdims=True)
        return ((g - m) / jnp.sqrt(s + eps)).reshape(v.shape)

    def _ln_c(v, eps=1e-6):
        m = jnp.mean(v, axis=-1, keepdims=True)
        s = jnp.var(v, axis=-1, keepdims=True)
        return (v - m) / jnp.sqrt(s + eps)

    def _ln_t(v, eps=1e-5):
        m = jnp.mean(v, axis=-1, keepdims=True)
        s = jnp.var(v, axis=-1, keepdims=True)
        return (v - m) / jnp.sqrt(s + eps)

    def _to_tokens(v):
        B_, H_, W_, C_ = v.shape
        return v.reshape(B_, H_ * W_, C_)
    def _from_tokens(t, like):
        return t.reshape(like.shape)

    x = x + _L0_conv_ref(_gn(x), L0_conv_Wq, L0_conv_bq, L0_conv_Wk, L0_conv_bk, L0_conv_Wv, L0_conv_bv, L0_conv_rpb, L0_conv_Wp, L0_conv_bp)
    t = _to_tokens(x)
    t = t + _L1_attn_ref(_ln_t(t), L1_attn_w_qkv, L1_attn_b_qkv, L1_attn_w_out, L1_attn_b_out)
    t = t + _L1_ffn_ref(_ln_t(t), L1_ffn_gate_w, L1_ffn_gate_b, L1_ffn_w1, L1_ffn_b1, L1_ffn_w2, L1_ffn_b2)
    x = _from_tokens(t, x)
    return x


_drawn_inputs = setup_inputs


def setup_inputs(seed=0):
    import zlib

    import numpy as np

    out = dict(_drawn_inputs(seed))
    spreads = {'L0_conv_bq': (0.0, 0.8),
     'L0_conv_bk': (0.0, 0.8),
     'L0_conv_bv': (0.0, 0.1),
     'L0_conv_bp': (0.0, 0.1),
     'L1_attn_b_qkv': (0.0, 0.1),
     'L1_attn_b_out': (0.0, 0.1),
     'L1_ffn_gate_b': (0.0, 0.1),
     'L1_ffn_b1': (0.0, 0.609),
     'L1_ffn_b2': (0.0, 0.426)}
    factors = {'L0_conv_Wq': 8.0, 'L0_conv_Wk': 8.0, 'L0_conv_Wv': 2.709, 'L0_conv_rpb': 21.483}
    for name, (base, spread) in spreads.items():
        noise = np.random.default_rng([zlib.crc32(name.encode()), seed]).standard_normal(out[name].shape)
        drawn = base * np.exp(spread * noise) if base else spread * noise
        out[name] = jnp.asarray(drawn.astype(out[name].dtype))
    for name, factor in factors.items():
        out[name] = (out[name] * factor).astype(out[name].dtype)
    return out
```

```python
from contextlib import ExitStack

import numpy as np
import concourse.bass as bass
from concourse import mybir

F32 = mybir.dt.float32
F32R = mybir.dt.float32r
U32 = mybir.dt.uint32
U8 = mybir.dt.uint8
ALU = mybir.AluOpType
ACT = mybir.ActivationFunctionType
AX_X = mybir.AxisListType.X

B, H, W, C = 4, 56, 56, 256
N = H * W
T = B * N
TT = 112
NT = N // TT
GW = 4 * TT
NG = N // GW
CC = C // 128
NH, HD, LR = 8, 32, 4
K7 = 7
RPB = 2 * K7 - 1
SUB = W // K7
HT = N // NH
TR = HT // H
QT = 29
CASES = (1, -1, -3, -5, -7)
EXP, FF = 8, 1024
CAP = -(-5 * T // (4 * EXP))
SLOTS = EXP * CAP
FAR = 1.0e30
KT = (N + 127) // 128
KTAIL = N - 128 * (KT - 1)


def first_key_row(r):
    return min(max(2 * r - 4, 0), H - 8)


def case_of(r):
    return CASES.index(first_key_row(r) - (2 * r - 1))


def window_start(i, n):
    return min(max(i - K7 // 2, 0), n - K7)


class Count:

    def __init__(self, eng, sem, base):
        self.eng, self.sem, self.base, self.n = eng, sem, base, 0

    def after(self, instruction):
        self.n += 1
        instruction.then_inc(self.sem, 1)
        self.eng.wait_ge(self.sem, self.base + self.n)


def inverse_root(dve, ch, out, variance, eps, spread, rooted, n):
    dve.tensor_scalar(out, variance, eps, None, ALU.add).then_inc(spread, 1)
    dve.wait_ge(rooted, n)
    ch.after(dve.reciprocal(out, out))


def root(act, out, spread, rooted, n):
    act.wait_ge(spread, n)
    act.activation(out, out, ACT.Sqrt).then_inc(rooted, 1)


def layer0_bias_tables(nc, A, S):
    with ExitStack() as ctx:
        far = ctx.enter_context(nc.sbuf_tensor("far", [128, 2 * GW * 5], F32))
        rp = ctx.enter_context(nc.sbuf_tensor("rp", [NH * RPB, RPB], F32))
        rn = ctx.enter_context(nc.sbuf_tensor("rn", [NH * RPB, RPB], F32))
        loaded = ctx.enter_context(nc.semaphore("rpb_loaded"))
        filled = ctx.enter_context(nc.semaphore("far_filled"))
        negated = ctx.enter_context(nc.semaphore("rpb_negated"))
        stored = ctx.enter_context(nc.semaphore("tables_filled"))
        placed = ctx.enter_context(nc.semaphore("rows_placed"))
        tiled = ctx.enter_context(nc.semaphore("tiles_placed"))
        block = ctx.enter_context(nc.Block())

        @block.vector
        def _(dve):
            dve.memset(far[:, :], FAR).then_inc(filled, 1)
            dve.wait_ge(loaded, 16)
            dve.tensor_scalar(rn[:, :], rp[:, :], -1.0, None, ALU.mult).then_inc(negated, 1)

        @block.sync
        def _(sp):
            sp.dma_start(rp[:, :], A["rpb"].rearrange("h a b -> (h a) b")).then_inc(loaded, 16)
            sp.wait_ge(filled, 1)
            for h in range(0, NH, 2):
                sp.dma_start(S["toeplitz"][:, h * RPB:(h + 2) * RPB, :].rearrange("j r c -> j (r c)"),
                             far[0:W, 0:2 * RPB * W]).then_inc(stored, 16)
            sp.dma_start(S["bias"].rearrange("h o p f -> p h o f")[:, 0:2],
                         far[0:TT, 0:2 * 5 * GW].rearrange("p (h o f) -> p h o f", h=2, o=5)).then_inc(stored, 16)
            for h in range(2, NH, 2):
                sp.dma_start(S["bias"].rearrange("h o p f -> p h o f")[:, h:h + 2],
                             far[0:TT, 0:2 * 5 * GW].rearrange("p (h o f) -> p h o f", h=2, o=5)).then_inc(stored, 16)
            sp.wait_ge(stored, 16 * NH)
            sp.wait_ge(negated, 1)
            for j in range(W):
                c0 = window_start(j, W)
                sp.dma_start(S["toeplitz"][j, :, c0:c0 + K7], rn[:, c0 - j + K7 - 1:c0 - j + 2 * K7 - 1]).then_inc(placed, 16)
            sp.wait_ge(placed, 16 * W)
            n = 0
            for o, off in enumerate(CASES):
                r = next(r for r in range(QT) if case_of(r) == o)
                for ri in range(2):
                    i = 2 * r - 1 + ri
                    if not 0 <= i < H:
                        continue
                    kk = window_start(i, H) - first_key_row(r)
                    dr = window_start(i, H) - i + K7 - 1
                    for h in range(NH):
                        src = S["toeplitz"][:, h * RPB + dr:h * RPB + dr + K7, :].rearrange("(t s) r c -> s t (r c)", s=SUB)
                        dst = S["bias"][h, o].rearrange("(s r t) f -> s r t f", s=SUB, r=2)[:, ri, :, kk * W:(kk + K7) * W]
                        sp.dma_start(dst, src).then_inc(tiled, 16)
                        n += 1
            sp.wait_ge(tiled, 16 * n)


def layer0_project(nc, A, S):
    with ExitStack() as ctx:
        def sb(name, shape, dt=F32):
            return ctx.enter_context(nc.sbuf_tensor("p0_" + name, shape, dt))

        def sem(name):
            return ctx.enter_context(nc.semaphore("p0_" + name))

        idn = sb("idn", [TT, TT])
        blk = sb("blk", [128, 128])
        wqk = sb("wqk", [128, CC, 64])
        wv = sb("wv", [128, CC, C])
        bqk = sb("bqk", [64, 1])
        sqk = sb("sqk", [64, 1])
        bvb = sb("bvb", [TT, C])
        xs = sb("xs", [TT, NT, C])
        xT = sb("xT", [128, CC, N])
        stats = sb("stats", [128, CC, NG, 6])
        mv = sb("mv", [128, CC, 2])
        gm = sb("gm", [128, CC])
        dd = sb("dd", [128, CC])
        vv = sb("vv", [128, CC])
        rstd = sb("rstd", [128, CC])
        tmp = sb("tmp", [64, 2, GW])
        qkh = sb("qkh", [64, N], F32R)
        qkl = sb("qkl", [64, N], F32R)
        vs = sb("vs", [TT, NT, C])
        idle = sb("idle", [128, 2])
        PS = ctx.enter_context(nc.psum_tensor("p0_ps", [128, 8, 512], F32))

        consts, loaded, turned, copied = sem("consts"), sem("loaded"), sem("turned"), sem("copied")
        stat, grouped, normed, chain = sem("stat"), sem("grouped"), sem("normed"), sem("chain")
        qk_made, qk_read, qk_split = sem("qk_made"), sem("qk_read"), sem("qk_split")
        v_made, v_read, stored, image_done = sem("v_made"), sem("v_read"), sem("stored"), sem("image_done")
        spread, rooted = sem("spread"), sem("rooted")
        CHAIN = 5 + NG

        block = ctx.enter_context(nc.Block())

        @block.sync
        def _(sp):
            for dst, src in ((idn[:, :], A["eye"][0:TT, 0:TT]), (blk[:, :], A["group_mean"]),
                             (wqk[:, :, 0:32], A["Wq0"].rearrange("(c p) n -> p c n", p=128)),
                             (wqk[:, :, 32:64], A["Wk0"].rearrange("(c p) n -> p c n", p=128)),
                             (wv[:, :, :], A["Wv0"].rearrange("(c p) n -> p c n", p=128)),
                             (bqk[0:32, :], A["bq0"].rearrange("(p a) -> p a", a=1)),
                             (bqk[32:64, :], A["bk0"].rearrange("(p a) -> p a", a=1)),
                             (sqk[:, :], A["qk_scale"]),
                             (bvb[:, :], A["bv0"].rearrange("(a n) -> a n", a=1).to_broadcast([TT, C]))):
                sp.dma_start(dst, src).then_inc(consts, 16)
            with sp.Fori(0, B) as b:
                sp.dma_start(xs[:, :, :], A["x"][b].rearrange("(j p) c -> p j c", p=TT)).then_inc(loaded, 16)
                sp.wait_ge(qk_split, (b + 1) * NG)
                sp.dma_start(S["qk0"][b, 0], qkh[:, :].bitcast(F32)).then_inc(stored, 16)
                sp.dma_start(S["qk0"][b, 1], qkl[:, :].bitcast(F32)).then_inc(stored, 16)
                sp.wait_ge(v_read, (b + 1) * NT)
                sp.dma_start(S["v0"][b].rearrange("(j p) c -> p j c", p=TT), vs[:, :, :]).then_inc(stored, 16)
                sp.wait_ge(stored, (b + 1) * 48)
                sp.sem_inc(image_done, 1)

        @block.tensor
        def _(pe):
            pe.wait_ge(consts, 144)
            with pe.Fori(0, B) as b:
                pe.wait_ge(loaded, (b + 1) * 16)
                for k in range(CC * NG):
                    g, c = divmod(k, CC)
                    if k >= 4:
                        pe.wait_ge(copied, b * (CC * NG) + k - 3)
                    for u in range(4):
                        last = pe.transpose(PS[:, k % 4, TT * u:TT * u + TT], xs[:, 4 * g + u, 128 * c:128 * c + 128],
                                            idn[:, :])
                    last.then_inc(turned, 1)
                for w, what in enumerate((mv[:, :, 0], vv[:, :])):
                    pe.wait_ge(stat, b * 2 + w + 1)
                    pe.matmul(PS[:, 4 + w, 0:CC], blk[:, :], what, start=True, stop=True).then_inc(grouped, 1)
                pe.wait_ge(normed, (b + 1) * CC)
                for g in range(NG):
                    if g >= 4:
                        pe.wait_ge(qk_read, b * NG + g - 3)
                    for c in range(CC):
                        last = pe.matmul(PS[0:64, g % 4, 0:GW], wqk[:, c, :], xT[:, c, GW * g:GW * g + GW],
                                         start=(c == 0), stop=(c == CC - 1))
                    last.then_inc(qk_made, 1)
                for j in range(NT):
                    if j >= 4:
                        pe.wait_ge(v_read, b * NT + j - 3)
                    for c in range(CC):
                        last = pe.matmul(PS[0:TT, 4 + j % 4, 0:C], xT[:, c, TT * j:TT * j + TT], wv[:, c, :],
                                         start=(c == 0), stop=(c == CC - 1))
                    last.then_inc(v_made, 1)
                pe.wait_ge(image_done, b + 1)

        @block.scalar
        def _(act):
            with act.Fori(0, B) as b:
                for k in range(CC * NG):
                    g, c = divmod(k, CC)
                    act.wait_ge(turned, b * (CC * NG) + k + 1)
                    act.activation(xT[:, c, GW * g:GW * g + GW], PS[:, k % 4, 0:GW], ACT.Copy).then_inc(copied, 1)
                root(act, rstd[:, :], spread, rooted, b + 1)
                act.wait_ge(image_done, b + 1)

        @block.vector
        def _(dve):
            dve.memset(idle[:, :], 0.0)
            dve.wait_ge(consts, 144)
            with dve.Fori(0, B) as b:
                ch = Count(dve, chain, b * CHAIN)
                for k in range(CC * NG):
                    g, c = divmod(k, CC)
                    dve.wait_ge(copied, b * (CC * NG) + k + 1)
                    last = dve.bn_stats(stats[:, c, g, :], xT[:, c, GW * g:GW * g + GW])
                ch.after(last)
                dve.tensor_copy(idle[:, 1:2], idle[:, 0:1])
                for c in range(CC):
                    last = dve.bn_aggr(mv[:, c, :], stats[:, c, :, :].rearrange("p g s -> p (g s)"))
                last.then_inc(stat, 1)
                dve.wait_ge(grouped, b * 2 + 1)
                ch.after(dve.tensor_copy(gm[:, :], PS[:, 4, 0:CC]))
                ch.after(dve.tensor_tensor(dd[:, :], mv[:, :, 0], gm[:, :], ALU.subtract))
                ch.after(dve.tensor_tensor(dd[:, :], dd[:, :], dd[:, :], ALU.mult))
                dve.tensor_tensor(vv[:, :], dd[:, :], mv[:, :, 1], ALU.add).then_inc(stat, 1)
                dve.wait_ge(grouped, b * 2 + 2)
                inverse_root(dve, ch, rstd[:, :], PS[:, 5, 0:CC], 1e-5, spread, rooted, b + 1)
                for c in range(CC):
                    dve.tensor_scalar(xT[:, c, :], xT[:, c, :], gm[:, c:c + 1], rstd[:, c:c + 1],
                                      ALU.subtract, ALU.mult).then_inc(normed, 1)
                for g in range(NG):
                    dve.wait_ge(qk_made, b * NG + g + 1)
                    t = tmp[:, g % 2, :]
                    dve.tensor_scalar(t, PS[0:64, g % 4, 0:GW], bqk[:, 0:1], sqk[:, 0:1], ALU.add, ALU.mult)\
                       .then_inc(qk_read, 1)
                    dve.wait_ge(qk_read, b * NG + g + 1)
                    ch.after(dve.tensor_copy(qkh[:, GW * g:GW * g + GW], t))
                    dve.tensor_tensor(qkl[:, GW * g:GW * g + GW], t, qkh[:, GW * g:GW * g + GW].bitcast(F32),
                                      ALU.subtract).then_inc(qk_split, 1)
                for j in range(NT):
                    dve.wait_ge(v_made, b * NT + j + 1)
                    dve.tensor_tensor(vs[:, j, :], PS[0:TT, 4 + j % 4, 0:C], bvb[:, :], ALU.add).then_inc(v_read, 1)
                assert ch.n == CHAIN
                dve.wait_ge(image_done, b + 1)


def layer0_attend(nc, A, S):
    with ExitStack() as ctx:
        def sb(name, shape, dt=F32):
            return ctx.enter_context(nc.sbuf_tensor("n0_" + name, shape, dt))

        def sem(name):
            return ctx.enter_context(nc.semaphore("n0_" + name))

        PAD = TR
        KW = 8 * W
        idn = sb("idn", [TT, TT])
        bias = sb("bias", [TT, 4, 5, KW])
        bnat = sb("bnat", [TT, 2, KW])
        qn = sb("qn", [128, SUB, HT + 2 * PAD])
        qp = sb("qp", [128, QT * TT], F32R)
        kn = sb("kn", [128, SUB, HT], F32R)
        vt = sb("vt", [TT, 4 * NT, HD])
        sm = sb("sm", [TT, 3, KW])
        P = sb("P", [TT, 3, KW])
        PTs = sb("PTs", [TT, 2, KW])
        mx = sb("mx", [TT, 8])
        rs = sb("rs", [TT, 8])
        rc = sb("rc", [TT, 8])
        yT = sb("yT", [128, N])
        inverted = sem("inverted")
        PS = ctx.enter_context(nc.psum_tensor("n0_ps", [128, 8, 512], F32))

        consts, zeroed, bias_loaded, bias_done = sem("consts"), sem("zeroed"), sem("bias_loaded"), sem("bias_done")
        loaded, tiled, scored, maxed = sem("loaded"), sem("tiled"), sem("scored"), sem("maxed")
        exped, normed, turned = sem("exped"), sem("normed"), sem("turned")
        copied, mixed, out_read, stored = sem("copied"), sem("mixed"), sem("out_read"), sem("stored")
        quad_done = sem("quad_done")
        steps = sem("steps")
        U = 4 * QT
        NLOAD = 16 * (16 + 16 + SUB)
        kv = [first_key_row(r) for r in range(QT)]

        def read_out(dve, it, r):
            dve.wait_ge(mixed, it * U + 4 * r + 4)
            t0, t1 = (7, 14) if r == 0 else (0, 7) if r == QT - 1 else (0, 14)
            p0 = W * (2 * r - 1) + SUB * t0
            dve.tensor_copy(yT[:, p0:p0 + SUB * (t1 - t0)].rearrange("p (t s) -> p s t", s=SUB),
                            PS[:, 5 + r % 2, 0:TT].rearrange("p (s t) -> p s t", s=SUB)[:, :, t0:t1])\
               .then_inc(out_read, 1)

        block = ctx.enter_context(nc.Block())

        @block.sync
        def _(sp):
            sp.dma_start(idn[:, :], A["eye"][0:TT, 0:TT]).then_inc(consts, 16)
            sp.wait_ge(zeroed, 2)
            with sp.Fori(0, 2) as g:
                for n in range(20):
                    if n >= 2:
                        sp.wait_ge(bias_done, g * 20 + n - 1)
                    if n >= 1:
                        sp.wait_ge(bias_loaded, (g * 20 + n) * 16)
                    h, o = divmod(n, 5)
                    sp.dma_start(bnat[:, n % 2, :], S["bias"][g * 4 + h, o]).then_inc(bias_loaded, 16)
                with sp.Fori(0, B) as b:
                    it = g * B + b
                    for hh in range(4):
                        tok = g * (4 * HT) + hh * HT
                        for term in range(4):
                            rows = slice(32 * hh + 4 * term, 32 * hh + 4 * term + 4)
                            sp.dma_start(qn[rows, :, PAD:PAD + HT],
                                         S["qk0"][b, term // 2, 0:32, bass.ds(tok, HT)].rearrange("(s c) t -> c s t", c=LR))\
                              .then_inc(loaded, 16)
                            sp.dma_start(kn[rows, :, :].bitcast(F32),
                                         S["qk0"][b, (0, 1, 1, 0)[term], 32:64, bass.ds(tok, HT)]
                                         .rearrange("(s c) t -> c s t", c=LR)).then_inc(loaded, 16)
                    for s in range(SUB):
                        src = S["v0"][b, bass.ds(g * (4 * HT), 4 * HT), HD * s:HD * s + HD]
                        sp.dma_start(vt[14 * s:14 * s + 14, :, :], src.rearrange("(m t) d -> t m d", t=14))\
                          .then_inc(loaded, 16)
                    sp.wait_ge(out_read, (it + 1) * QT)
                    sp.dma_start(S["y0T"][b * 2 + g], yT[:, :]).then_inc(stored, 16)
                    sp.wait_ge(stored, (it + 1) * 16)
                    sp.sem_inc(quad_done, 1)

        @block.tensor
        def _(pe):
            pe.wait_ge(consts, 16)
            with pe.Fori(0, 2 * B) as it:
                pe.wait_ge(loaded, (it + 1) * NLOAD)
                pe.wait_ge(tiled, it + 1)
                for n in range(U + 3):
                    if n < U:
                        r, hh = divmod(n, 4)
                        if n >= 3:
                            pe.wait_ge(maxed, it * U + n - 2)
                        rows = slice(32 * hh, 32 * hh + 16)
                        pe.matmul(PS[0:TT, n % 3, 0:KW].rearrange("p (c s t) -> p c s t", c=4, s=SUB),
                                  qp[rows, TT * r:TT * r + TT],
                                  kn[rows, :, TR * kv[r]:TR * kv[r] + 56].rearrange("p s (c t) -> p c s t", c=4),
                                  start=True, stop=True).then_inc(scored, 1)
                    if 2 <= n < U + 2:
                        m = n - 2
                        pe.wait_ge(normed, it * U + m + 1)
                        if m >= 2:
                            pe.wait_ge(copied, it * U + m - 1)
                        for c in range(4):
                            last = pe.transpose(PS[0:TT, 3 + m % 2, TT * c:TT * c + TT],
                                                P[:, m % 3, TT * c:TT * c + TT], idn[:, :])
                        last.then_inc(turned, 1)
                    if n >= 3:
                        m = n - 3
                        r, hh = divmod(m, 4)
                        pe.wait_ge(copied, it * U + m + 1)
                        if hh == 0 and r >= 2:
                            pe.wait_ge(out_read, it * QT + r - 1)
                        for c in range(4):
                            last = pe.matmul(PS[32 * hh:32 * hh + 32, 5 + r % 2, 0:TT],
                                             vt[:, NT * hh + kv[r] // 2 + c, :],
                                             PTs[:, m % 2, TT * c:TT * c + TT], start=(c == 0), stop=(c == 3))
                        last.then_inc(mixed, 1)
                pe.wait_ge(quad_done, it + 1)

        @block.vector
        def _(dve):
            dve.memset(qn[:, :, :], 0.0).then_inc(zeroed, 1)
            dve.memset(kn[:, :, :].bitcast(F32), 0.0).then_inc(zeroed, 1)
            with dve.Fori(0, 2) as g:
                for n in range(20):
                    h, o = divmod(n, 5)
                    dve.wait_ge(bias_loaded, (g * 20 + n + 1) * 16)
                    dve.tensor_copy(bias[:, h, o, :].rearrange("p (c s t) -> p c s t", c=4, s=SUB),
                                    bnat[:, n % 2, :].rearrange("p (c t s) -> p c s t", c=4, s=SUB))\
                       .then_inc(bias_done, 1)
                dve.wait_ge(bias_done, (g + 1) * 20)
                dve.sem_inc(steps, 1)
                with dve.Fori(0, B) as b:
                    it = g * B + b
                    dve.wait_ge(loaded, (it + 1) * NLOAD)
                    dve.tensor_copy(qp[:, :].rearrange("p (r s t) -> p r s t", r=QT, s=SUB),
                                    qn[:, :, :].rearrange("p s (r t) -> p r s t", r=QT)).then_inc(tiled, 1)
                    for n in range(U + 4):
                        if n < U:
                            r, hh = divmod(n, 4)
                            if n >= 3:
                                dve.wait_ge(exped, it * U + n - 2)
                            dve.wait_ge(scored, it * U + n + 1)
                            dve.sem_inc(steps, 1)
                            dve.tensor_tensor_reduce(out=sm[:, n % 3, :], in0=PS[0:TT, n % 3, 0:KW],
                                                     in1=bias[:, hh, case_of(r), :], scale=1.0, scalar=3.0e38,
                                                     op0=ALU.add, op1=ALU.min, accum_out=mx[:, n % 8:n % 8 + 1])\
                               .then_inc(maxed, 1)
                        if 1 <= n < U + 1:
                            m = n - 1
                            dve.wait_ge(exped, it * U + m + 1)
                            dve.reciprocal(rc[:, m % 8:m % 8 + 1], rs[:, m % 8:m % 8 + 1]).then_inc(inverted, 1)
                            dve.wait_ge(inverted, it * U + m + 1)
                            dve.tensor_scalar(P[:, m % 3, :], P[:, m % 3, :], rc[:, m % 8:m % 8 + 1], None,
                                              ALU.mult).then_inc(normed, 1)
                        if n >= 8 and n % 4 == 0:
                            read_out(dve, it, n // 4 - 2)
                    read_out(dve, it, QT - 1)
                    dve.wait_ge(quad_done, it + 1)

        @block.scalar
        def _(act):
            with act.Fori(0, 2 * B) as it:
                for n in range(U + 2):
                    if n < U:
                        act.wait_ge(maxed, it * U + n + 1)
                        if n >= 3:
                            act.wait_ge(turned, it * U + n - 2)
                        act.activation(P[:, n % 3, :], sm[:, n % 3, :], ACT.Exp, bias=mx[:, n % 8:n % 8 + 1],
                                       scale=-1.0, accum_out=rs[:, n % 8:n % 8 + 1]).then_inc(exped, 1)
                    if n >= 2:
                        m = n - 2
                        act.wait_ge(turned, it * U + m + 1)
                        if m >= 2:
                            act.wait_ge(mixed, it * U + m - 1)
                        act.activation(PTs[:, m % 2, :], PS[0:TT, 3 + m % 2, 0:KW], ACT.Copy).then_inc(copied, 1)
                act.wait_ge(quad_done, it + 1)


def layer0_output(nc, A, S):
    with ExitStack() as ctx:
        def sb(name, shape, dt=F32):
            return ctx.enter_context(nc.sbuf_tensor("o0_" + name, shape, dt))

        def sem(name):
            return ctx.enter_context(nc.semaphore("o0_" + name))

        QB = 4
        idn = sb("idn", [TT, TT])
        wp = sb("wp", [128, CC, C])
        wqkv = sb("wqkv", [128, CC, 3 * C])
        bqk = sb("bqk", [128, QB])
        bpb = sb("bpb", [TT, C])
        bvb = sb("bvb", [128, C])
        yT = sb("yT", [128, CC, N])
        ts = sb("ts", [TT, NT, C])
        xn = sb("xn", [TT, 4, C])
        xT = sb("xT", [128, CC, N])
        stats = sb("stats", [TT, NT, 6])
        mv = sb("mv", [TT, NT, 2])
        rstd = sb("rstd", [TT, NT])
        tmp = sb("tmp", [128, 2, GW])
        high = sb("high", [128, 2, N], F32R)
        low = sb("low", [128, 2, N], F32R)
        vs = sb("vs", [128, KT, C])
        idle = sb("idle", [TT, 2])
        spread, rooted = sem("spread"), sem("rooted")
        steps = sem("steps")
        PS = ctx.enter_context(nc.psum_tensor("o0_ps", [128, 8, 512], F32))

        consts, loaded, made, summed, normed = sem("consts"), sem("loaded"), sem("made"), sem("summed"), sem("normed")
        turned, copied, chain = sem("turned"), sem("copied"), sem("chain")
        qk_made, qk_read, qk_split = sem("qk_made"), sem("qk_read"), sem("qk_split")
        v_made, v_read = sem("v_made"), sem("v_read")
        part_stored = [sem("part_stored0"), sem("part_stored1")]
        v_stored, t_stored, image_done = sem("v_stored"), sem("t_stored"), sem("image_done")
        CHAIN = 4 + QB * NG
        block = ctx.enter_context(nc.Block())

        @block.sync
        def _(sp):
            sp.dma_start(bqk[:, :], A["b_qkv"][0:2 * C].rearrange("(q p) -> p q", p=128),
                         allow_slow_non_contiguous=True).then_inc(consts, 16)
            for dst, src in ((idn[:, :], A["eye"][0:TT, 0:TT]),
                             (wp[:, :, :], A["Wp0"].rearrange("(c p) n -> p c n", p=128)),
                             (wqkv[:, :, :], A["w_qkv"].rearrange("(c p) n -> p c n", p=128)),
                             (bpb[:, :], A["bp0"].rearrange("(a n) -> a n", a=1).to_broadcast([TT, C])),
                             (bvb[:, :], A["b_qkv"][2 * C:3 * C].rearrange("(a n) -> a n", a=1).to_broadcast([128, C]))):
                sp.dma_start(dst, src).then_inc(consts, 16)
            with sp.Fori(0, B) as b:
                sp.dma_start(yT[:, :, :], S["y0T"][bass.ds(b * 2, 2)].rearrange("c p n -> p c n")).then_inc(loaded, 16)
                sp.dma_start(ts[:, :, :], A["x"][b].rearrange("(j p) c -> p j c", p=TT)).then_inc(loaded, 16)
                sp.wait_ge(summed, (b + 1) * NT)
                sp.dma_start(S["t0"][b].rearrange("(j p) c -> p j c", p=TT), ts[:, :, :]).then_inc(t_stored, 16)
                for q in range(QB):
                    sp.wait_ge(qk_split, b * (QB * NG) + (q + 1) * NG)
                    sp.sem_inc(steps, 1)
                    for part, src in ((0, high), (1, low)):
                        sp.dma_start(S["q1" if q < 2 else "k1"][part, b * 2 + q % 2],
                                     src[:, q % 2, :].bitcast(F32)).then_inc(part_stored[q % 2], 16)
                sp.wait_ge(v_read, (b + 1) * KT)
                sp.sem_inc(steps, 1)
                for g in range(2):
                    sp.dma_start(S["v1"][b * 2 + g, :, 0:KT - 1, :], vs[:, 0:KT - 1, 128 * g:128 * g + 128])\
                      .then_inc(v_stored, 16)
                    sp.dma_start(S["v1"][b * 2 + g, 0:KTAIL, KT - 1, :],
                                 vs[0:KTAIL, KT - 1, 128 * g:128 * g + 128]).then_inc(v_stored, 16)
                for w in range(2):
                    sp.wait_ge(part_stored[w], (b + 1) * (QB * 16))
                    sp.sem_inc(steps, 1)
                sp.wait_ge(v_stored, (b + 1) * 64)
                sp.sem_inc(steps, 1)
                sp.wait_ge(t_stored, (b + 1) * 16)
                sp.sem_inc(image_done, 1)

        @block.tensor
        def _(pe):
            pe.wait_ge(consts, 96)
            with pe.Fori(0, B) as b:
                pe.wait_ge(loaded, (b + 1) * 32)
                for j in range(NT):
                    if j >= 4:
                        pe.wait_ge(summed, b * NT + j - 3)
                    for c in range(CC):
                        last = pe.matmul(PS[0:TT, j % 4, 0:C], yT[:, c, TT * j:TT * j + TT], wp[:, c, :],
                                         start=(c == 0), stop=(c == CC - 1))
                    last.then_inc(made, 1)
                for g in range(NG):
                    pe.wait_ge(normed, b * NT + 4 * g + 4)
                    if g >= 2:
                        pe.wait_ge(copied, b * (CC * NG) + 2 * g - 2)
                    for c in range(CC):
                        for u in range(4):
                            last = pe.transpose(PS[:, 4 + (2 * g + c) % 4, TT * u:TT * u + TT],
                                                xn[:, u, 128 * c:128 * c + 128], idn[:, :])
                        last.then_inc(turned, 1)
                pe.wait_ge(copied, (b + 1) * (CC * NG))
                for n in range(QB * NG):
                    q, g = divmod(n, NG)
                    if n >= 4:
                        pe.wait_ge(qk_read, b * (QB * NG) + n - 3)
                    for c in range(CC):
                        last = pe.matmul(PS[:, n % 4, 0:GW], wqkv[:, c, 128 * q:128 * q + 128],
                                         xT[:, c, GW * g:GW * g + GW], start=(c == 0), stop=(c == CC - 1))
                    last.then_inc(qk_made, 1)
                for j in range(KT):
                    rows = 128 if j < KT - 1 else KTAIL
                    if j >= 4:
                        pe.wait_ge(v_read, b * KT + j - 3)
                    for c in range(CC):
                        last = pe.matmul(PS[0:rows, 4 + j % 4, 0:C], xT[:, c, 128 * j:128 * j + rows],
                                         wqkv[:, c, 2 * C:3 * C], start=(c == 0), stop=(c == CC - 1))
                    last.then_inc(v_made, 1)
                pe.wait_ge(image_done, b + 1)

        @block.scalar
        def _(act):
            with act.Fori(0, B) as b:
                root(act, rstd[:, :], spread, rooted, b + 1)
                for k in range(CC * NG):
                    g, c = divmod(k, CC)
                    act.wait_ge(turned, b * (CC * NG) + k + 1)
                    act.activation(xT[:, c, GW * g:GW * g + GW], PS[:, 4 + k % 4, 0:GW], ACT.Copy).then_inc(copied, 1)
                act.wait_ge(image_done, b + 1)

        @block.vector
        def _(dve):
            dve.memset(idle[:, :], 0.0)
            dve.wait_ge(consts, 96)
            with dve.Fori(0, B) as b:
                ch = Count(dve, chain, b * CHAIN)
                dve.wait_ge(loaded, (b + 1) * 32)
                for j in range(NT):
                    last = dve.tensor_tensor(ts[:, j, :], ts[:, j, :], bpb[:, :], ALU.add)
                ch.after(last)
                for j in range(NT):
                    dve.wait_ge(made, b * NT + j + 1)
                    dve.tensor_tensor(ts[:, j, :], PS[0:TT, j % 4, 0:C], ts[:, j, :], ALU.add).then_inc(summed, 1)
                    if j >= 1:
                        dve.wait_ge(summed, b * NT + j)
                        dve.bn_stats(stats[:, j - 1, :], ts[:, j - 1, :])
                dve.wait_ge(summed, (b + 1) * NT)
                ch.after(dve.bn_stats(stats[:, NT - 1, :], ts[:, NT - 1, :]))
                dve.tensor_copy(idle[:, 1:2], idle[:, 0:1])
                for j in range(NT):
                    last = dve.bn_aggr(mv[:, j, :], stats[:, j, :])
                ch.after(last)
                inverse_root(dve, ch, rstd[:, :], mv[:, :, 1], 1e-5, spread, rooted, b + 1)
                for j in range(NT):
                    if j >= 4:
                        dve.wait_ge(turned, b * (CC * NG) + 2 * (j // 4))
                    dve.tensor_scalar(xn[:, j % 4, :], ts[:, j, :], mv[:, j, 0:1], rstd[:, j:j + 1],
                                      ALU.subtract, ALU.mult).then_inc(normed, 1)
                for n in range(QB * NG):
                    q, g = divmod(n, NG)
                    dve.wait_ge(qk_made, b * (QB * NG) + n + 1)
                    t = tmp[:, n % 2, :]
                    dve.tensor_scalar(t, PS[:, n % 4, 0:GW], bqk[:, q:q + 1], float(C) ** -0.5 if q < 2 else 1.0,
                                      ALU.add, ALU.mult).then_inc(qk_read, 1)
                    if q >= 2 and g == 0:
                        dve.wait_ge(part_stored[q % 2], b * (QB * 16) + 32)
                    dve.wait_ge(qk_read, b * (QB * NG) + n + 1)
                    at = slice(GW * g, GW * g + GW)
                    ch.after(dve.tensor_copy(high[:, q % 2, at], t))
                    dve.tensor_tensor(low[:, q % 2, at], t, high[:, q % 2, at].bitcast(F32), ALU.subtract)\
                       .then_inc(qk_split, 1)
                for j in range(KT):
                    rows = 128 if j < KT - 1 else KTAIL
                    dve.wait_ge(v_made, b * KT + j + 1)
                    dve.tensor_tensor(vs[0:rows, j, :], PS[0:rows, 4 + j % 4, 0:C], bvb[0:rows, :], ALU.add)\
                       .then_inc(v_read, 1)
                assert ch.n == CHAIN
                dve.wait_ge(image_done, b + 1)


def layer1_attend(nc, A, S):
    with ExitStack() as ctx:
        def sb(name, shape, dt=F32):
            return ctx.enter_context(nc.sbuf_tensor("a1_" + name, shape, dt))

        def sem(name):
            return ctx.enter_context(nc.semaphore("a1_" + name))

        idn = sb("idn", [128, 128])
        ones = sb("ones", [128, HD])
        qp = sb("qp", [98, 4, N], F32R)
        kp = sb("kp", [98, 4, N], F32R)
        vt = sb("vt", [128, KT, 128])
        tops = sb("tops", [128, 4 * KT, 2])
        top = sb("top", [128, 4 * KT])
        neg = sb("neg", [4 * KT, 128])
        negh = sb("negh", [4 * KT, 128], F32R)
        negl = sb("negl", [4 * KT, 128], F32R)
        P = sb("P", [128, 6, 2, GW])
        rec = sb("rec", [128, GW])
        yo = sb("yo", [128, N])
        PS = ctx.enter_context(nc.psum_tensor("a1_ps", [128, 8, 512], F32))

        consts, cleared, loaded = sem("consts"), sem("cleared"), sem("loaded")
        keyed, topped, chain, top_turned = sem("keyed"), sem("topped"), sem("chain"), sem("top_turned")
        neg_stored, neg_loaded = sem("neg_stored"), sem("neg_loaded")
        scored, exped, mixed, divided = sem("scored"), sem("exped"), sem("mixed"), sem("divided")
        chain2, stored, quad_done = sem("chain2"), sem("stored"), sem("quad_done")
        steps = sem("steps")
        CHAIN = 5
        HALVES = ((0, 4), (4, 3))
        block = ctx.enter_context(nc.Block())

        @block.sync
        def _(sp):
            sp.dma_start(idn[:, :], A["eye"]).then_inc(consts, 16)
            sp.wait_ge(cleared, 3)
            with sp.Fori(0, 2 * B) as q:
                for term in range(3):
                    rows = slice(32 * term, 32 * term + 32)
                    sp.dma_start(qp[rows, :, :].bitcast(F32),
                                 S["q1"][(0, 0, 1)[term], q].rearrange("(h d) n -> d h n", d=HD)).then_inc(loaded, 16)
                    sp.dma_start(kp[rows, :, :].bitcast(F32),
                                 S["k1"][(0, 1, 0)[term], q].rearrange("(h d) n -> d h n", d=HD)).then_inc(loaded, 16)
                sp.dma_start(vt[:, 0:KT - 1, :], S["v1"][q, :, 0:KT - 1, :]).then_inc(loaded, 16)
                sp.dma_start(vt[0:KTAIL, KT - 1, :], S["v1"][q, 0:KTAIL, KT - 1, :]).then_inc(loaded, 16)
                sp.wait_ge(chain, (q + 1) * CHAIN)
                sp.dma_start(S["neg"][0], negh[:, :].bitcast(F32)).then_inc(neg_stored, 16)
                sp.dma_start(S["neg"][1], negl[:, :].bitcast(F32)).then_inc(neg_stored, 16)
                sp.wait_ge(neg_stored, (q + 1) * 32)
                sp.dma_start(qp[96:98, :, :].bitcast(F32),
                             S["neg"].rearrange("u (h t) p -> u h (t p)", h=4)[:, :, 0:N]).then_inc(neg_loaded, 16)
                sp.wait_ge(divided, (q + 1) * NG)
                sp.dma_start(S["y1T"][q], yo[:, :]).then_inc(stored, 16)
                sp.wait_ge(stored, (q + 1) * 16)
                sp.sem_inc(quad_done, 1)

        @block.tensor
        def _(pe):
            pe.wait_ge(consts, 16)
            with pe.Fori(0, 2 * B) as q:
                pe.wait_ge(loaded, (q + 1) * 128)
                for n in range(4 * KT):
                    hh, t = divmod(n, KT)
                    rows = 128 if t < KT - 1 else KTAIL
                    for half, (k0, nk) in enumerate(HALVES):
                        if n >= 1:
                            pe.wait_ge(topped, q * (8 * KT) + 2 * n + half - 1)
                        for k in range(k0, k0 + nk):
                            last = pe.matmul(PS[0:rows, k, 0:GW], qp[0:96, hh, 128 * t:128 * t + rows],
                                             kp[0:96, hh, GW * k:GW * k + GW], start=True, stop=True)
                        last.then_inc(keyed, 1)
                pe.wait_ge(chain, q * CHAIN + 2)
                pe.transpose(PS[0:4 * KT, 7, 0:128], top[:, :], idn[:, :]).then_inc(top_turned, 1)
                pe.wait_ge(neg_loaded, (q + 1) * 16)
                STEPS = NG * KT
                for n in range(STEPS + 1):
                    if n < STEPS:
                        j, t = divmod(n, KT)
                        rows = 128 if t < KT - 1 else KTAIL
                        for pair in range(2):
                            slot = 2 * n + pair
                            if slot >= 2:
                                pe.wait_ge(exped, q * (2 * STEPS) + slot - 1)
                            for e in range(2):
                                last = pe.matmul(PS[0:rows, 2 * pair + e, 0:GW],
                                                 kp[0:98, 2 * pair + e, 128 * t:128 * t + rows],
                                                 qp[0:98, 2 * pair + e, GW * j:GW * j + GW], start=True, stop=True)
                            last.then_inc(scored, 1)
                    if n >= 1:
                        m = n - 1
                        j, t = divmod(m, KT)
                        rows = 128 if t < KT - 1 else KTAIL
                        pe.wait_ge(exped, q * (2 * STEPS) + 2 * m + 2)
                        if t == 0 and j >= 2:
                            pe.wait_ge(divided, q * NG + j - 1)
                        if rows < 128:
                            pe.sem_inc(steps, 1)
                        for bank, what in ((4, None), (6, ones)):
                            for hh in range(4):
                                w = vt[0:rows, t, HD * hh:HD * hh + HD] if what is None else ones[0:rows, :]
                                last = pe.matmul(PS[HD * hh:HD * hh + HD, bank + j % 2, 0:GW], w,
                                                 P[0:rows, (2 * m + hh // 2) % 6, hh % 2, :],
                                                 start=(t == 0), stop=(t == KT - 1))
                        last.then_inc(mixed, 1)
                pe.wait_ge(quad_done, q + 1)

        @block.vector
        def _(dve):
            dve.memset(tops[:, :, :], 0.0).then_inc(cleared, 1)
            dve.memset(ones[:, :], 1.0).then_inc(cleared, 1)
            dve.memset(kp[96:98, :, :].bitcast(F32), 1.0).then_inc(cleared, 1)
            with dve.Fori(0, 2 * B) as q:
                ch = Count(dve, chain, q * CHAIN)
                for n in range(4 * KT):
                    rows = 128 if n % KT < KT - 1 else KTAIL
                    for half, (k0, nk) in enumerate(HALVES):
                        dve.wait_ge(keyed, q * (8 * KT) + 2 * n + half + 1)
                        dve.tensor_reduce(tops[0:rows, n, half:half + 1], PS[0:rows, k0:k0 + nk, 0:GW],
                                          mybir.AxisListType.XY, ALU.max).then_inc(topped, 1)
                dve.wait_ge(topped, (q + 1) * (8 * KT))
                ch.after(dve.tensor_reduce(top[:, :], tops[:, :, :], AX_X, ALU.max))
                ch.after(dve.tensor_scalar(top[:, :], top[:, :], -1.0, None, ALU.mult))
                dve.wait_ge(top_turned, q + 1)
                ch.after(dve.tensor_copy(neg[:, :], PS[0:4 * KT, 7, 0:128]))
                ch.after(dve.tensor_copy(negh[:, :], neg[:, :]))
                ch.after(dve.tensor_tensor(negl[:, :], neg[:, :], negh[:, :].bitcast(F32), ALU.subtract))
                assert ch.n == CHAIN
                for j in range(NG):
                    dve.wait_ge(mixed, q * (NG * KT) + (j + 1) * KT)
                    if j >= 1:
                        dve.wait_ge(divided, q * NG + j)
                    dve.reciprocal(rec[:, :], PS[:, 6 + j % 2, 0:GW]).then_inc(chain2, 1)
                    dve.wait_ge(chain2, q * NG + j + 1)
                    dve.tensor_tensor(yo[:, GW * j:GW * j + GW], PS[:, 4 + j % 2, 0:GW], rec[:, :], ALU.mult)\
                       .then_inc(divided, 1)
                dve.wait_ge(quad_done, q + 1)

        @block.scalar
        def _(act):
            with act.Fori(0, 2 * B) as q:
                for slot in range(2 * NG * KT):
                    t = slot // 2 % KT
                    rows = 128 if t < KT - 1 else KTAIL
                    act.wait_ge(scored, q * (2 * NG * KT) + slot + 1)
                    if slot >= 6:
                        act.wait_ge(mixed, q * (NG * KT) + slot // 2 - 2)
                    act.activation(P[0:rows, slot % 6, :, :], PS[0:rows, 2 * (slot % 2):2 * (slot % 2) + 2, 0:GW],
                                   ACT.Exp).then_inc(exped, 1)
                act.wait_ge(quad_done, q + 1)


def layer1_output(nc, A, S):
    with ExitStack() as ctx:
        def sb(name, shape, dt=F32):
            return ctx.enter_context(nc.sbuf_tensor("o1_" + name, shape, dt))

        def sem(name):
            return ctx.enter_context(nc.semaphore("o1_" + name))

        idn = sb("idn", [TT, TT])
        wo = sb("wo", [128, CC, C])
        gw = sb("gw", [128, CC, EXP])
        bob = sb("bob", [TT, C])
        gbb = sb("gbb", [TT, EXP])
        yT = sb("yT", [128, CC, N])
        ts = sb("ts", [TT, NT, C])
        xn = sb("xn", [TT, 4, C])
        xT = sb("xT", [128, CC, N])
        stats = sb("stats", [TT, NT, 6])
        mv = sb("mv", [TT, NT, 2])
        rstd = sb("rstd", [TT, NT])
        lg = sb("lg", [TT, NT, EXP])
        zero = sb("zero", [1, C])
        idle = sb("idle", [TT, 2])
        spread, rooted = sem("spread"), sem("rooted")
        PS = ctx.enter_context(nc.psum_tensor("o1_ps", [128, 8, 512], F32))

        consts, loaded, made, summed, normed = sem("consts"), sem("loaded"), sem("made"), sem("summed"), sem("normed")
        turned, copied, chain, gated, gate_read = sem("turned"), sem("copied"), sem("chain"), sem("gated"), sem("gate_read")
        zeroed, zero_stored, stored, image_done = sem("zeroed"), sem("zero_stored"), sem("stored"), sem("image_done")
        CHAIN = 4
        block = ctx.enter_context(nc.Block())

        @block.sync
        def _(sp):
            for dst, src in ((idn[:, :], A["eye"][0:TT, 0:TT]),
                             (wo[:, :, :], A["w_out"].rearrange("(c p) n -> p c n", p=128)),
                             (gw[:, :, :], A["gate_w"].rearrange("(c p) n -> p c n", p=128)),
                             (bob[:, :], A["b_out"].rearrange("(a n) -> a n", a=1).to_broadcast([TT, C])),
                             (gbb[:, :], A["gate_b"].rearrange("(a n) -> a n", a=1).to_broadcast([TT, EXP]))):
                sp.dma_start(dst, src).then_inc(consts, 16)
            sp.wait_ge(zeroed, 1)
            sp.dma_start(S["t1"][T:T + 1, :], zero[:, :]).then_inc(zero_stored, 16)
            sp.wait_ge(zero_stored, 16)
            with sp.Fori(0, B) as b:
                sp.dma_start(yT[:, :, :], S["y1T"][bass.ds(b * 2, 2)].rearrange("c p n -> p c n")).then_inc(loaded, 16)
                sp.dma_start(ts[:, :, :], S["t0"][b].rearrange("(j p) c -> p j c", p=TT)).then_inc(loaded, 16)
                sp.wait_ge(summed, (b + 1) * NT)
                sp.dma_start(S["t1"][bass.ds(b * N, N), :].rearrange("(j p) c -> p j c", p=TT), ts[:, :, :])\
                  .then_inc(stored, 16)
                sp.dma_start(A["out"][b].rearrange("(j p) c -> p j c", p=TT), ts[:, :, :]).then_inc(stored, 16)
                sp.wait_ge(gate_read, (b + 1) * NT)
                sp.dma_start(S["logits"][:, bass.ds(b * NT, NT), :], lg[:, :, :]).then_inc(stored, 16)
                sp.wait_ge(stored, (b + 1) * 48)
                sp.sem_inc(image_done, 1)

        @block.tensor
        def _(pe):
            pe.wait_ge(consts, 80)
            with pe.Fori(0, B) as b:
                pe.wait_ge(loaded, (b + 1) * 32)
                for j in range(NT):
                    if j >= 4:
                        pe.wait_ge(summed, b * NT + j - 3)
                    for c in range(CC):
                        last = pe.matmul(PS[0:TT, j % 4, 0:C], yT[:, c, TT * j:TT * j + TT], wo[:, c, :],
                                         start=(c == 0), stop=(c == CC - 1))
                    last.then_inc(made, 1)
                for g in range(NG):
                    pe.wait_ge(normed, b * NT + 4 * g + 4)
                    if g >= 2:
                        pe.wait_ge(copied, b * (CC * NG) + 2 * g - 2)
                    for c in range(CC):
                        for u in range(4):
                            last = pe.transpose(PS[:, 4 + (2 * g + c) % 4, TT * u:TT * u + TT],
                                                xn[:, u, 128 * c:128 * c + 128], idn[:, :])
                        last.then_inc(turned, 1)
                pe.wait_ge(copied, (b + 1) * (CC * NG))
                for j in range(NT):
                    if j >= 4:
                        pe.wait_ge(gate_read, b * NT + j - 3)
                    for c in range(CC):
                        last = pe.matmul(PS[0:TT, j % 4, 0:EXP], xT[:, c, TT * j:TT * j + TT], gw[:, c, :],
                                         start=(c == 0), stop=(c == CC - 1))
                    last.then_inc(gated, 1)
                pe.wait_ge(image_done, b + 1)

        @block.scalar
        def _(act):
            with act.Fori(0, B) as b:
                root(act, rstd[:, :], spread, rooted, b + 1)
                for k in range(CC * NG):
                    g, c = divmod(k, CC)
                    act.wait_ge(turned, b * (CC * NG) + k + 1)
                    act.activation(xT[:, c, GW * g:GW * g + GW], PS[:, 4 + k % 4, 0:GW], ACT.Copy).then_inc(copied, 1)
                act.wait_ge(image_done, b + 1)

        @block.vector
        def _(dve):
            dve.memset(zero[:, :], 0.0).then_inc(zeroed, 1)
            dve.memset(idle[:, :], 0.0)
            dve.wait_ge(consts, 80)
            with dve.Fori(0, B) as b:
                ch = Count(dve, chain, b * CHAIN)
                dve.wait_ge(loaded, (b + 1) * 32)
                for j in range(NT):
                    last = dve.tensor_tensor(ts[:, j, :], ts[:, j, :], bob[:, :], ALU.add)
                ch.after(last)
                for j in range(NT):
                    dve.wait_ge(made, b * NT + j + 1)
                    dve.tensor_tensor(ts[:, j, :], PS[0:TT, j % 4, 0:C], ts[:, j, :], ALU.add).then_inc(summed, 1)
                    if j >= 1:
                        dve.wait_ge(summed, b * NT + j)
                        dve.bn_stats(stats[:, j - 1, :], ts[:, j - 1, :])
                dve.wait_ge(summed, (b + 1) * NT)
                ch.after(dve.bn_stats(stats[:, NT - 1, :], ts[:, NT - 1, :]))
                dve.tensor_copy(idle[:, 1:2], idle[:, 0:1])
                for j in range(NT):
                    last = dve.bn_aggr(mv[:, j, :], stats[:, j, :])
                ch.after(last)
                inverse_root(dve, ch, rstd[:, :], mv[:, :, 1], 1e-5, spread, rooted, b + 1)
                for j in range(NT):
                    if j >= 4:
                        dve.wait_ge(turned, b * (CC * NG) + 2 * (j // 4))
                    dve.tensor_scalar(xn[:, j % 4, :], ts[:, j, :], mv[:, j, 0:1], rstd[:, j:j + 1],
                                      ALU.subtract, ALU.mult).then_inc(normed, 1)
                for j in range(NT):
                    dve.wait_ge(gated, b * NT + j + 1)
                    dve.tensor_tensor(lg[:, j, :], PS[0:TT, j % 4, 0:EXP], gbb[:, :], ALU.add).then_inc(gate_read, 1)
                assert ch.n == CHAIN
                dve.wait_ge(image_done, b + 1)


def route(nc, A, S):
    with ExitStack() as ctx:
        def sb(name, shape, dt=F32):
            return ctx.enter_context(nc.sbuf_tensor("r_" + name, shape, dt))

        def sem(name):
            return ctx.enter_context(nc.semaphore("r_" + name))

        J = B * NT
        HALF = J // 2 * EXP
        lg = sb("lg", [TT, J, EXP])
        e1 = sb("e1", [TT, J, EXP])
        e2 = sb("e2", [TT, J, EXP])
        hot = sb("hot", [TT, J, EXP])
        back = sb("back", [TT, EXP])
        first = sb("first", [TT, EXP])
        upper = sb("upper", [TT, TT])
        ones = sb("ones", [TT, TT])
        top = sb("top", [TT, J])
        place = sb("place", [TT, J])
        prob = sb("prob", [TT, J])
        pos = sb("pos", [TT, J])
        kept = sb("kept", [TT, J])
        slot = sb("slot", [TT, J])
        slotu = sb("slotu", [TT, J], U32)
        before = sb("before", [TT, EXP, J])
        zeros = sb("zeros", [TT, J])
        token = sb("token", [TT, J])
        rows = sb("rows", [TT, J, 2])
        empty = sb("empty", [112, SLOTS // 112, 2])
        PS = ctx.enter_context(nc.psum_tensor("r_ps", [128, 4, 512], F32))
        loaded, chain, told, counted, shifted = sem("loaded"), sem("chain"), sem("told"), sem("counted"), sem("shifted")
        exped, table_cleared, scattered = sem("exped"), sem("table_cleared"), sem("scattered")
        emptied, placed = sem("emptied"), sem("placed")
        block = ctx.enter_context(nc.Block())

        def over_experts(x):
            return x.unsqueeze(2).to_broadcast([TT, J, EXP])

        def over_tokens(x):
            return x.unsqueeze(1).to_broadcast([TT, J, EXP])

        @block.sync
        def _(sp):
            for dst, src in ((lg[:, :, :], S["logits"]), (back[:, :], A["back"]), (first[:, :], A["first"]),
                             (upper[:, :], A["upper"]), (token[:, :], A["token"])):
                sp.dma_start(dst, src).then_inc(loaded, 16)
            sp.wait_ge(emptied, 2)
            sp.dma_start(S["table"].rearrange("(p a) b -> p a b", p=112), empty[:, :, :]).then_inc(table_cleared, 16)
            sp.wait_ge(table_cleared, 16)

        @block.gpsimd
        def _(pool):
            pool.memset(empty[:, :, 0], float(T)).then_inc(emptied, 1)
            pool.memset(empty[:, :, 1], 0.0).then_inc(emptied, 1)
            pool.wait_ge(table_cleared, 16)
            pool.wait_ge(placed, 1)
            for j in range(J):
                pool.indirect_dma_start(out=S["table"], out_offset=bass.IndirectOffsetOnAxis(ap=slotu[:, j:j + 1], axis=0),
                                        in_=rows[:, j, :], in_offset=None, bounds_check=SLOTS - 1,
                                        oob_is_err=False).then_inc(scattered, 16)
            pool.wait_ge(scattered, 16 * J)

        @block.scalar
        def _(act):
            act.wait_ge(shifted, 1)
            act.activation(e2[:, :, :], e2[:, :, :], ACT.Exp).then_inc(exped, 1)

        @block.tensor
        def _(pe):
            pe.wait_ge(told, 1)
            for half in range(2):
                cols = hot[:, :, :].rearrange("p j e -> p (j e)")[:, half * HALF:half * HALF + HALF]
                pe.matmul(PS[0:TT, half, 0:HALF], upper[:, :], cols, start=True, stop=True).then_inc(counted, 1)
                pe.matmul(PS[0:TT, 2 + half, 0:HALF], ones[:, :], cols, start=True, stop=True).then_inc(counted, 1)

        @block.vector
        def _(dve):
            ch = Count(dve, chain, 0)
            ch.after(dve.memset(ones[:, :], 1.0))
            ch.after(dve.memset(zeros[:, :], 0.0))
            dve.wait_ge(loaded, 80)
            ch.after(dve.tensor_reduce(top[:, :], lg[:, :, :], AX_X, ALU.max))
            ch.after(dve.tensor_tensor(e2[:, :, :], lg[:, :, :], over_experts(top[:, :]), ALU.subtract))
            ch.after(dve.tensor_scalar(e1[:, :, :], e2[:, :, :], 0.0, None, ALU.is_ge))
            dve.sem_inc(shifted, 1)
            ch.after(dve.tensor_tensor(e1[:, :, :], e1[:, :, :], over_tokens(back[:, :]), ALU.mult))
            ch.after(dve.tensor_reduce(place[:, :], e1[:, :, :], AX_X, ALU.max))
            dve.tensor_tensor(hot[:, :, :], over_tokens(back[:, :]), over_experts(place[:, :]), ALU.is_equal)\
               .then_inc(told, 1)
            dve.wait_ge(exped, 1)
            ch.after(dve.tensor_reduce(prob[:, :], e2[:, :, :], AX_X, ALU.add))
            dve.wait_ge(counted, 4)
            for half in range(2):
                last = dve.tensor_copy(e1[:, half * (J // 2):(half + 1) * (J // 2), :],
                                       PS[0:TT, 2 + half, 0:HALF].rearrange("p (j e) -> p j e", e=EXP))
            ch.after(last)
            for e in range(EXP):
                last = dve.tensor_tensor_scan(out=before[:, e, :], data0=e1[:, :, e], data1=zeros[:, :], initial=0.0,
                                              op0=ALU.add, op1=ALU.add)
            ch.after(last)
            ch.after(dve.tensor_tensor(e1[:, :, :], before[:, :, :].rearrange("p e j -> p j e"), e1[:, :, :],
                                       ALU.subtract))
            for half in range(2):
                part = e1[:, half * (J // 2):(half + 1) * (J // 2), :]
                last = dve.tensor_tensor(part, PS[0:TT, half, 0:HALF].rearrange("p (j e) -> p j e", e=EXP), part,
                                         ALU.add)
            ch.after(last)
            ch.after(dve.tensor_tensor(e2[:, :, :], e1[:, :, :], hot[:, :, :], ALU.mult))
            ch.after(dve.tensor_reduce(pos[:, :], e2[:, :, :], AX_X, ALU.add))
            ch.after(dve.tensor_tensor(e2[:, :, :], hot[:, :, :], over_tokens(first[:, :]), ALU.mult))
            ch.after(dve.tensor_reduce(slot[:, :], e2[:, :, :], AX_X, ALU.add))
            ch.after(dve.tensor_scalar(kept[:, :], pos[:, :], float(CAP), float(2 * SLOTS), ALU.is_gt, ALU.mult))
            ch.after(dve.tensor_tensor(slot[:, :], slot[:, :], pos[:, :], ALU.add))
            ch.after(dve.tensor_tensor(slot[:, :], slot[:, :], kept[:, :], ALU.add))
            ch.after(dve.tensor_scalar(slotu[:, :], slot[:, :], -1.0, None, ALU.add))
            ch.after(dve.reciprocal(rows[:, :, 1], prob[:, :]))
            dve.tensor_copy(rows[:, :, 0], token[:, :]).then_inc(placed, 1)


def experts(nc, A, S):
    with ExitStack() as ctx:
        def sb(name, shape, dt=F32):
            return ctx.enter_context(nc.sbuf_tensor("e_" + name, shape, dt))

        def sem(name):
            return ctx.enter_context(nc.semaphore("e_" + name))

        FB = FF // 128
        ST = (CAP + 127) // 128
        STAIL = CAP - 128 * (ST - 1)
        SG = (ST + 3) // 4
        idn = sb("idn", [128, 128])
        w1 = sb("w1", [128, CC, FF])
        w2 = sb("w2", [128, FB, C])
        b1 = sb("b1", [128, FB])
        b2b = sb("b2b", [128, C])
        tab = sb("tab", [128, ST, 2])
        tok = sb("tok", [128, ST], U32)
        xg = sb("xg", [128, ST, C])
        xn = sb("xn", [128, 4, C])
        stats = sb("stats", [128, ST, 6])
        mv = sb("mv", [128, ST, 2])
        rstd = sb("rstd", [128, ST])
        xT = sb("xT", [128, 2, CC, 512])
        hT = sb("hT", [128, FB, 512])
        y = sb("y", [128, 2, C])
        none = sb("none", [128, C])
        fin = sb("fin", [128, 2, C], U8)
        nan = sb("nan", [128, 2, C], U8)
        yf = sb("yf", [128, 2, C])
        idle = sb("idle", [128, 2])
        spread, rooted = sem("spread"), sem("rooted")
        PS = ctx.enter_context(nc.psum_tensor("e_ps", [128, 8, 512], F32))
        consts, cleared, loaded, told, gathered = sem("consts"), sem("cleared"), sem("loaded"), sem("told"), sem("gathered")
        chain, normed, turned, copied = sem("chain"), sem("normed"), sem("turned"), sem("copied")
        hidden, relued, made, finished = sem("hidden"), sem("relued"), sem("made"), sem("finished")
        read, expert_done = sem("read"), sem("expert_done")
        scattered = [sem("scattered0"), sem("scattered1")]
        steps = sem("steps")
        CHAIN = 3 * SG + 4 * ST

        def size(t):
            return 128 if t < ST - 1 else STAIL

        def width(g):
            return min(512, CAP - 512 * g)

        block = ctx.enter_context(nc.Block())

        @block.sync
        def _(sp):
            sp.dma_start(idn[:, :], A["eye"]).then_inc(consts, 16)
            sp.wait_ge(cleared, 1)
            with sp.Fori(0, EXP) as e:
                sp.dma_start(tab[:, 0:ST - 1, :],
                             S["table"][bass.ds(e * CAP, 128 * (ST - 1)), :].rearrange("(t p) b -> p t b", p=128))\
                  .then_inc(loaded, 16)
                sp.dma_start(tab[0:STAIL, ST - 1, :], S["table"][bass.ds(e * CAP + 128 * (ST - 1), STAIL), :])\
                  .then_inc(loaded, 16)
                sp.dma_start(w1[:, :, :], A["w1"][e].rearrange("(c p) n -> p c n", p=128)).then_inc(loaded, 16)
                sp.dma_start(w2[:, :, :], A["w2"][e].rearrange("(c p) n -> p c n", p=128)).then_inc(loaded, 16)
                sp.dma_start(b1[:, :], A["b1"][e].rearrange("(c p) -> p c", p=128),
                             allow_slow_non_contiguous=True).then_inc(loaded, 16)
                sp.dma_start(b2b[:, :], A["b2"][bass.ds(e, 1), :].to_broadcast([128, C])).then_inc(loaded, 16)
                for w in scattered:
                    sp.wait_ge(w, (e + 1) * (8 * ST))
                sp.sem_inc(expert_done, 1)

        @block.gpsimd
        def _(pool):
            with pool.Fori(0, EXP) as e:
                pool.wait_ge(told, e + 1)
                pool.sem_inc(steps, 1)
                for t in range(ST):
                    pool.indirect_dma_start(out=xg[0:size(t), t, :], out_offset=None, in_=S["t1"],
                                            in_offset=bass.IndirectOffsetOnAxis(ap=tok[0:size(t), t:t + 1], axis=0))\
                        .then_inc(gathered, 16)
                for t in range(ST):
                    pool.wait_ge(finished, e * ST + t + 1)
                    pool.sem_inc(steps, 1)
                    pool.indirect_dma_start(out=A["out_rows"],
                                            out_offset=bass.IndirectOffsetOnAxis(ap=tok[0:size(t), t:t + 1], axis=0),
                                            in_=yf[0:size(t), t % 2, :], in_offset=None, bounds_check=T - 1,
                                            oob_is_err=False).then_inc(scattered[t % 2], 16)
                pool.wait_ge(expert_done, e + 1)

        @block.tensor
        def _(pe):
            pe.wait_ge(consts, 16)
            with pe.Fori(0, EXP) as e:
                pe.wait_ge(loaded, (e + 1) * 96)
                for g in range(SG):
                    tiles = range(4 * g, min(4 * g + 4, ST))
                    pe.wait_ge(normed, e * ST + tiles[-1] + 1)
                    for c in range(CC):
                        if g >= 1:
                            pe.wait_ge(copied, e * (CC * SG) + (g - 1) * CC + c + 1)
                        for t in tiles:
                            last = pe.transpose(PS[:, c, 128 * (t % 4):128 * (t % 4) + size(t)],
                                                xn[0:size(t), t % 4, 128 * c:128 * c + 128],
                                                idn[0:size(t), 0:size(t)])
                        last.then_inc(turned, 1)
                    pe.wait_ge(copied, e * (CC * SG) + (g + 1) * CC)
                    for f in range(FB):
                        n = g * FB + f
                        if n >= 3:
                            pe.wait_ge(relued, e * (SG * FB) + n - 2)
                        for c in range(CC):
                            last = pe.matmul(PS[:, 2 + n % 3, 0:width(g)], w1[:, c, 128 * f:128 * f + 128],
                                             xT[:, g % 2, c, 0:width(g)], start=(c == 0), stop=(c == CC - 1))
                        last.then_inc(hidden, 1)
                    pe.wait_ge(relued, e * (SG * FB) + (g + 1) * FB)
                    for t in tiles:
                        if t >= 2:
                            pe.wait_ge(read, e * ST + t - 1)
                        for f in range(FB):
                            last = pe.matmul(PS[0:size(t), 5 + t % 2, 0:C],
                                             hT[:, f, 128 * (t % 4):128 * (t % 4) + size(t)], w2[:, f, :],
                                             start=(f == 0), stop=(f == FB - 1))
                        last.then_inc(made, 1)
                pe.wait_ge(expert_done, e + 1)

        @block.scalar
        def _(act):
            with act.Fori(0, EXP) as e:
                act.wait_ge(loaded, (e + 1) * 96)
                for g in range(SG):
                    root(act, rstd[:, 4 * g:min(4 * g + 4, ST)], spread, rooted, e * SG + g + 1)
                    for c in range(CC):
                        act.wait_ge(turned, e * (CC * SG) + g * CC + c + 1)
                        act.activation(xT[:, g % 2, c, 0:width(g)], PS[:, c, 0:width(g)], ACT.Copy).then_inc(copied, 1)
                    if g >= 1:
                        act.wait_ge(made, e * ST + 4 * g)
                    for f in range(FB):
                        n = g * FB + f
                        act.wait_ge(hidden, e * (SG * FB) + n + 1)
                        act.activation(hT[:, f, 0:width(g)], PS[:, 2 + n % 3, 0:width(g)], ACT.Relu,
                                       bias=b1[:, f:f + 1]).then_inc(relued, 1)
                act.wait_ge(expert_done, e + 1)

        @block.vector
        def _(dve):
            dve.memset(idle[:, :], 0.0)
            dve.memset(mv[:, :, :], 0.0)
            dve.memset(none[:, :], 0.0)
            dve.memset(tab[:, ST - 1, :], float(T)).then_inc(cleared, 1)
            with dve.Fori(0, EXP) as e:
                ch = Count(dve, chain, e * CHAIN)
                dve.wait_ge(loaded, (e + 1) * 96)
                dve.tensor_copy(tok[:, :], tab[:, :, 0]).then_inc(told, 1)

                def finish(t):
                    s = size(t)
                    y_, f_, n_, o_ = (v[0:s, t % 2, :] for v in (y, fin, nan, yf))
                    dve.wait_ge(made, e * ST + t + 1)
                    dve.tensor_tensor(y_, PS[0:s, 5 + t % 2, 0:C], b2b[0:s, :], ALU.add).then_inc(read, 1)
                    dve.wait_ge(read, e * ST + t + 1)
                    ch.after(dve.tensor_scalar(y_, y_, tab[0:s, t, 1:2], None, ALU.mult))
                    dve.tensor_scalar(f_, y_, 0.0, 0.0, ALU.mult, ALU.is_equal)
                    dve.tensor_tensor(n_, y_, y_, ALU.not_equal)
                    if t >= 2:
                        dve.wait_ge(scattered[t % 2], e * (8 * ST) + 16 * (t // 2))
                    ch.after(dve.tensor_scalar(o_, y_, -1.0e4, 1.0e4, ALU.max, ALU.min))
                    dve.tensor_copy(idle[:, 1:2], idle[:, 0:1])
                    ch.after(dve.copy_predicated(o_, n_, none[0:s, :]))
                    dve.tensor_copy(idle[:, 1:2], idle[:, 0:1])
                    ch.after(dve.copy_predicated(o_, f_, y_))
                    dve.tensor_tensor(o_, o_, xg[0:s, t, :], ALU.add).then_inc(finished, 1)

                for g in range(SG):
                    tiles = range(4 * g, min(4 * g + 4, ST))
                    for t in tiles:
                        s = size(t)
                        if t == 0:
                            dve.wait_ge(gathered, (e + 1) * (16 * ST))
                        last = dve.bn_stats(stats[0:s, t, :], xg[0:s, t, :])
                    ch.after(last)
                    dve.tensor_copy(idle[:, 1:2], idle[:, 0:1])
                    for t in tiles:
                        last = dve.bn_aggr(mv[0:size(t), t, :], stats[0:size(t), t, :])
                    ch.after(last)
                    inverse_root(dve, ch, rstd[:, 4 * g:tiles[-1] + 1], mv[:, 4 * g:tiles[-1] + 1, 1], 1e-5,
                                 spread, rooted, e * SG + g + 1)
                    for t in tiles:
                        s = size(t)
                        if g >= 1:
                            dve.wait_ge(turned, e * (CC * SG) + g * CC)
                        dve.tensor_scalar(xn[0:s, t % 4, :], xg[0:s, t, :], mv[0:s, t, 0:1], rstd[0:s, t:t + 1],
                                          ALU.subtract, ALU.mult).then_inc(normed, 1)
                    if g >= 1:
                        for t in range(4 * g - 4, 4 * g):
                            finish(t)
                for t in range(4 * SG - 4, ST):
                    finish(t)
                assert ch.n == CHAIN, ch.n
                dve.wait_ge(expert_done, e + 1)


STAGES = (layer0_bias_tables, layer0_project, layer0_attend, layer0_output, layer1_attend, layer1_output, route, experts)

SCRATCH = {
    "toeplitz": [W, NH * RPB, W],
    "bias": [NH, 5, TT, 8 * W],
    "qk0": [B, 2, 64, N],
    "v0": [B, N, C],
    "y0T": [2 * B, 128, N],
    "t0": [B, N, C],
    "q1": [2, 2 * B, 128, N],
    "k1": [2, 2 * B, 128, N],
    "v1": [2 * B, 128, KT, 128],
    "neg": [2, 4 * KT, 128],
    "y1T": [2 * B, 128, N],
    "t1": [T + 1, C],
    "logits": [TT, B * NT, EXP],
    "table": [SLOTS, 2],
}

INPUTS = {
    "x": "x", "L0_conv_Wq": "Wq0", "L0_conv_bq": "bq0", "L0_conv_Wk": "Wk0", "L0_conv_bk": "bk0",
    "L0_conv_Wv": "Wv0", "L0_conv_bv": "bv0", "L0_conv_rpb": "rpb", "L0_conv_Wp": "Wp0", "L0_conv_bp": "bp0",
    "L1_attn_w_qkv": "w_qkv", "L1_attn_b_qkv": "b_qkv", "L1_attn_w_out": "w_out", "L1_attn_b_out": "b_out",
    "L1_ffn_gate_w": "gate_w", "L1_ffn_gate_b": "gate_b", "L1_ffn_w1": "w1", "L1_ffn_b1": "b1",
    "L1_ffn_w2": "w2", "L1_ffn_b2": "b2",
}


def shape_constants():
    one = np.ones((128, 1), np.float32)
    group = C // 32
    return {
        "eye": np.eye(128, dtype=np.float32),
        "group_mean": np.kron(np.eye(128 // group, dtype=np.float32), np.full((group, group), 1.0 / group, np.float32)),
        "qk_scale": np.concatenate([one[:32] * np.float32(-HD ** -0.5), one[:32]]),
        "upper": np.triu(np.ones((TT, TT), np.float32)),
        "back": np.tile(np.arange(EXP, 0, -1, dtype=np.float32), (TT, 1)),
        "first": np.tile(np.arange(EXP, dtype=np.float32) * CAP, (TT, 1)),
        "token": np.arange(T, dtype=np.float32).reshape(B * NT, TT).T.copy(),
    }


def build(nc, A, S):
    A = dict(A)
    A["x"] = A["x"].rearrange("b h w c -> b (h w) c")
    A["out_rows"] = A["out"].rearrange("b h w c -> (b h w) c")
    A["out"] = A["out"].rearrange("b h w c -> b (h w) c")
    for stage in STAGES:
        stage(nc, A, S)


def kernel(**inputs):
    import concourse.bacc as bacc
    from concourse.bass_utils import run_bass_kernel_spmd

    nc = bacc.Bacc("TRN2", target_bir_lowering=False, num_devices=1)
    arrays, A = {}, {}
    given = {short: np.ascontiguousarray(inputs[name]) for name, short in INPUTS.items()}
    for short, a in {**given, **shape_constants()}.items():
        arrays["in_" + short] = a
        A[short] = nc.dram_tensor("in_" + short, a.shape, mybir.dt.from_np(a.dtype), kind="ExternalInput").ap()
    A["out"] = nc.dram_tensor("result", (B, H, W, C), F32, kind="ExternalOutput").ap()
    S = {n: nc.dram_tensor("scratch_" + n, s, F32, kind="Internal").ap() for n, s in SCRATCH.items()}
    build(nc, A, S)
    r = run_bass_kernel_spmd(nc, [arrays], core_ids=[0])
    return r.results[0]["result"]
```

```python
from contextlib import ExitStack

import numpy as np
import concourse.bass as bass
from concourse import mybir

F32 = mybir.dt.float32
F32R = mybir.dt.float32r
U32 = mybir.dt.uint32
U8 = mybir.dt.uint8
ALU = mybir.AluOpType
ACT = mybir.ActivationFunctionType
AX_X = mybir.AxisListType.X

B, H, W, C = 4, 56, 56, 256
N = H * W
T = B * N
TT = 112
NT = N // TT
GW = 4 * TT
NG = N // GW
CC = C // 128
NH, HD, LR = 8, 32, 4
K7 = 7
RPB = 2 * K7 - 1
SUB = W // K7
HT = N // NH
TR = HT // H
QT = 29
CASES = (1, -1, -3, -5, -7)
EXP, FF = 8, 1024
CAP = -(-5 * T // (4 * EXP))
SLOTS = EXP * CAP
FAR = 1.0e30
KT = (N + 127) // 128
KTAIL = N - 128 * (KT - 1)


def first_key_row(r):
    return min(max(2 * r - 4, 0), H - 8)


def case_of(r):
    return CASES.index(first_key_row(r) - (2 * r - 1))


def window_start(i, n):
    return min(max(i - K7 // 2, 0), n - K7)


class Count:

    def __init__(self, eng, sem, base):
        self.eng, self.sem, self.base, self.n = eng, sem, base, 0

    def after(self, instruction):
        self.n += 1
        instruction.then_inc(self.sem, 1)
        self.eng.wait_ge(self.sem, self.base + self.n)


def inverse_root(dve, ch, out, variance, eps, spread, rooted, n):
    dve.tensor_scalar(out, variance, eps, None, ALU.add).then_inc(spread, 1)
    dve.wait_ge(rooted, n)
    ch.after(dve.reciprocal(out, out))


def root(act, out, spread, rooted, n):
    act.wait_ge(spread, n)
    act.activation(out, out, ACT.Sqrt).then_inc(rooted, 1)


def layer0_bias_tables(nc, A, S):
    with ExitStack() as ctx:
        far = ctx.enter_context(nc.sbuf_tensor("far", [128, 2 * GW * 5], F32))
        rp = ctx.enter_context(nc.sbuf_tensor("rp", [NH * RPB, RPB], F32))
        rn = ctx.enter_context(nc.sbuf_tensor("rn", [NH * RPB, RPB], F32))
        loaded = ctx.enter_context(nc.semaphore("rpb_loaded"))
        filled = ctx.enter_context(nc.semaphore("far_filled"))
        negated = ctx.enter_context(nc.semaphore("rpb_negated"))
        stored = ctx.enter_context(nc.semaphore("tables_filled"))
        placed = ctx.enter_context(nc.semaphore("rows_placed"))
        tiled = ctx.enter_context(nc.semaphore("tiles_placed"))
        block = ctx.enter_context(nc.Block())

        @block.vector
        def _(dve):
            dve.memset(far[:, :], FAR).then_inc(filled, 1)
            dve.wait_ge(loaded, 16)
            dve.tensor_scalar(rn[:, :], rp[:, :], -1.0, None, ALU.mult).then_inc(negated, 1)

        @block.sync
        def _(sp):
            sp.dma_start(rp[:, :], A["rpb"].rearrange("h a b -> (h a) b")).then_inc(loaded, 16)
            sp.wait_ge(filled, 1)
            for h in range(0, NH, 2):
                sp.dma_start(S["toeplitz"][:, h * RPB:(h + 2) * RPB, :].rearrange("j r c -> j (r c)"),
                             far[0:W, 0:2 * RPB * W]).then_inc(stored, 16)
            sp.dma_start(S["bias"].rearrange("h o p f -> p h o f")[:, 0:2],
                         far[0:TT, 0:2 * 5 * GW].rearrange("p (h o f) -> p h o f", h=2, o=5)).then_inc(stored, 16)
            for h in range(2, NH, 2):
                sp.dma_start(S["bias"].rearrange("h o p f -> p h o f")[:, h:h + 2],
                             far[0:TT, 0:2 * 5 * GW].rearrange("p (h o f) -> p h o f", h=2, o=5)).then_inc(stored, 16)
            sp.wait_ge(stored, 16 * NH)
            sp.wait_ge(negated, 1)
            for j in range(W):
                c0 = window_start(j, W)
                sp.dma_start(S["toeplitz"][j, :, c0:c0 + K7], rn[:, c0 - j + K7 - 1:c0 - j + 2 * K7 - 1]).then_inc(placed, 16)
            sp.wait_ge(placed, 16 * W)
            n = 0
            for o, off in enumerate(CASES):
                r = next(r for r in range(QT) if case_of(r) == o)
                for ri in range(2):
                    i = 2 * r - 1 + ri
                    if not 0 <= i < H:
                        continue
                    kk = window_start(i, H) - first_key_row(r)
                    dr = window_start(i, H) - i + K7 - 1
                    for h in range(NH):
                        src = S["toeplitz"][:, h * RPB + dr:h * RPB + dr + K7, :].rearrange("(t s) r c -> s t (r c)", s=SUB)
                        dst = S["bias"][h, o].rearrange("(s r t) f -> s r t f", s=SUB, r=2)[:, ri, :, kk * W:(kk + K7) * W]
                        sp.dma_start(dst, src).then_inc(tiled, 16)
                        n += 1
            sp.wait_ge(tiled, 16 * n)


def layer0_project(nc, A, S):
    with ExitStack() as ctx:
        def sb(name, shape, dt=F32):
            return ctx.enter_context(nc.sbuf_tensor("p0_" + name, shape, dt))

        def sem(name):
            return ctx.enter_context(nc.semaphore("p0_" + name))

        idn = sb("idn", [TT, TT])
        blk = sb("blk", [128, 128])
        wqk = sb("wqk", [128, CC, 64])
        wv = sb("wv", [128, CC, C])
        bqk = sb("bqk", [64, 1])
        sqk = sb("sqk", [64, 1])
        bvb = sb("bvb", [TT, C])
        xs = sb("xs", [TT, NT, C])
        xT = sb("xT", [128, CC, N])
        stats = sb("stats", [128, CC, NG, 6])
        mv = sb("mv", [128, CC, 2])
        gm = sb("gm", [128, CC])
        dd = sb("dd", [128, CC])
        vv = sb("vv", [128, CC])
        rstd = sb("rstd", [128, CC])
        tmp = sb("tmp", [64, 2, GW])
        qkh = sb("qkh", [64, N], F32R)
        qkl = sb("qkl", [64, N], F32R)
        vs = sb("vs", [TT, NT, C])
        idle = sb("idle", [128, 2])
        PS = ctx.enter_context(nc.psum_tensor("p0_ps", [128, 8, 512], F32))

        consts, loaded, turned, copied = sem("consts"), sem("loaded"), sem("turned"), sem("copied")
        stat, grouped, normed, chain = sem("stat"), sem("grouped"), sem("normed"), sem("chain")
        qk_made, qk_read, qk_split = sem("qk_made"), sem("qk_read"), sem("qk_split")
        v_made, v_read, stored, image_done = sem("v_made"), sem("v_read"), sem("stored"), sem("image_done")
        spread, rooted = sem("spread"), sem("rooted")
        CHAIN = 5 + NG

        block = ctx.enter_context(nc.Block())

        @block.sync
        def _(sp):
            for dst, src in ((idn[:, :], A["eye"][0:TT, 0:TT]), (blk[:, :], A["group_mean"]),
                             (wqk[:, :, 0:32], A["Wq0"].rearrange("(c p) n -> p c n", p=128)),
                             (wqk[:, :, 32:64], A["Wk0"].rearrange("(c p) n -> p c n", p=128)),
                             (wv[:, :, :], A["Wv0"].rearrange("(c p) n -> p c n", p=128)),
                             (bqk[0:32, :], A["bq0"].rearrange("(p a) -> p a", a=1)),
                             (bqk[32:64, :], A["bk0"].rearrange("(p a) -> p a", a=1)),
                             (sqk[:, :], A["qk_scale"]),
                             (bvb[:, :], A["bv0"].rearrange("(a n) -> a n", a=1).to_broadcast([TT, C]))):
                sp.dma_start(dst, src).then_inc(consts, 16)
            with sp.Fori(0, B) as b:
                sp.dma_start(xs[:, :, :], A["x"][b].rearrange("(j p) c -> p j c", p=TT)).then_inc(loaded, 16)
                sp.wait_ge(qk_split, (b + 1) * NG)
                sp.dma_start(S["qk0"][b, 0], qkh[:, :].bitcast(F32)).then_inc(stored, 16)
                sp.dma_start(S["qk0"][b, 1], qkl[:, :].bitcast(F32)).then_inc(stored, 16)
                sp.wait_ge(v_read, (b + 1) * NT)
                sp.dma_start(S["v0"][b].rearrange("(j p) c -> p j c", p=TT), vs[:, :, :]).then_inc(stored, 16)
                sp.wait_ge(stored, (b + 1) * 48)
                sp.sem_inc(image_done, 1)

        @block.tensor
        def _(pe):
            pe.wait_ge(consts, 144)
            with pe.Fori(0, B) as b:
                pe.wait_ge(loaded, (b + 1) * 16)
                for k in range(CC * NG):
                    g, c = divmod(k, CC)
                    if k >= 4:
                        pe.wait_ge(copied, b * (CC * NG) + k - 3)
                    for u in range(4):
                        last = pe.transpose(PS[:, k % 4, TT * u:TT * u + TT], xs[:, 4 * g + u, 128 * c:128 * c + 128],
                                            idn[:, :])
                    last.then_inc(turned, 1)
                for w, what in enumerate((mv[:, :, 0], vv[:, :])):
                    pe.wait_ge(stat, b * 2 + w + 1)
                    pe.matmul(PS[:, 4 + w, 0:CC], blk[:, :], what, start=True, stop=True).then_inc(grouped, 1)
                pe.wait_ge(normed, (b + 1) * CC)
                for g in range(NG):
                    if g >= 4:
                        pe.wait_ge(qk_read, b * NG + g - 3)
                    for c in range(CC):
                        last = pe.matmul(PS[0:64, g % 4, 0:GW], wqk[:, c, :], xT[:, c, GW * g:GW * g + GW],
                                         start=(c == 0), stop=(c == CC - 1))
                    last.then_inc(qk_made, 1)
                for j in range(NT):
                    if j >= 4:
                        pe.wait_ge(v_read, b * NT + j - 3)
                    for c in range(CC):
                        last = pe.matmul(PS[0:TT, 4 + j % 4, 0:C], xT[:, c, TT * j:TT * j + TT], wv[:, c, :],
                                         start=(c == 0), stop=(c == CC - 1))
                    last.then_inc(v_made, 1)
                pe.wait_ge(image_done, b + 1)

        @block.scalar
        def _(act):
            with act.Fori(0, B) as b:
                for k in range(CC * NG):
                    g, c = divmod(k, CC)
                    act.wait_ge(turned, b * (CC * NG) + k + 1)
                    act.activation(xT[:, c, GW * g:GW * g + GW], PS[:, k % 4, 0:GW], ACT.Copy).then_inc(copied, 1)
                root(act, rstd[:, :], spread, rooted, b + 1)
                act.wait_ge(image_done, b + 1)

        @block.vector
        def _(dve):
            dve.memset(idle[:, :], 0.0)
            dve.wait_ge(consts, 144)
            with dve.Fori(0, B) as b:
                ch = Count(dve, chain, b * CHAIN)
                for k in range(CC * NG):
                    g, c = divmod(k, CC)
                    dve.wait_ge(copied, b * (CC * NG) + k + 1)
                    last = dve.bn_stats(stats[:, c, g, :], xT[:, c, GW * g:GW * g + GW])
                ch.after(last)
                dve.tensor_copy(idle[:, 1:2], idle[:, 0:1])
                for c in range(CC):
                    last = dve.bn_aggr(mv[:, c, :], stats[:, c, :, :].rearrange("p g s -> p (g s)"))
                last.then_inc(stat, 1)
                dve.wait_ge(grouped, b * 2 + 1)
                ch.after(dve.tensor_copy(gm[:, :], PS[:, 4, 0:CC]))
                ch.after(dve.tensor_tensor(dd[:, :], mv[:, :, 0], gm[:, :], ALU.subtract))
                ch.after(dve.tensor_tensor(dd[:, :], dd[:, :], dd[:, :], ALU.mult))
                dve.tensor_tensor(vv[:, :], dd[:, :], mv[:, :, 1], ALU.add).then_inc(stat, 1)
                dve.wait_ge(grouped, b * 2 + 2)
                inverse_root(dve, ch, rstd[:, :], PS[:, 5, 0:CC], 1e-5, spread, rooted, b + 1)
                for c in range(CC):
                    dve.tensor_scalar(xT[:, c, :], xT[:, c, :], gm[:, c:c + 1], rstd[:, c:c + 1],
                                      ALU.subtract, ALU.mult).then_inc(normed, 1)
                for g in range(NG):
                    dve.wait_ge(qk_made, b * NG + g + 1)
                    t = tmp[:, g % 2, :]
                    dve.tensor_scalar(t, PS[0:64, g % 4, 0:GW], bqk[:, 0:1], sqk[:, 0:1], ALU.add, ALU.mult)\
                       .then_inc(qk_read, 1)
                    dve.wait_ge(qk_read, b * NG + g + 1)
                    ch.after(dve.tensor_copy(qkh[:, GW * g:GW * g + GW], t))
                    dve.tensor_tensor(qkl[:, GW * g:GW * g + GW], t, qkh[:, GW * g:GW * g + GW].bitcast(F32),
                                      ALU.subtract).then_inc(qk_split, 1)
                for j in range(NT):
                    dve.wait_ge(v_made, b * NT + j + 1)
                    dve.tensor_tensor(vs[:, j, :], PS[0:TT, 4 + j % 4, 0:C], bvb[:, :], ALU.add).then_inc(v_read, 1)
                assert ch.n == CHAIN
                dve.wait_ge(image_done, b + 1)


def layer0_attend(nc, A, S):
    with ExitStack() as ctx:
        def sb(name, shape, dt=F32):
            return ctx.enter_context(nc.sbuf_tensor("n0_" + name, shape, dt))

        def sem(name):
            return ctx.enter_context(nc.semaphore("n0_" + name))

        PAD = TR
        KW = 8 * W
        idn = sb("idn", [TT, TT])
        bias = sb("bias", [TT, 4, 5, KW])
        bnat = sb("bnat", [TT, 2, KW])
        qn = sb("qn", [128, SUB, HT + 2 * PAD])
        qp = sb("qp", [128, QT * TT], F32R)
        kn = sb("kn", [128, SUB, HT], F32R)
        vt = sb("vt", [TT, 4 * NT, HD])
        sm = sb("sm", [TT, 3, KW])
        P = sb("P", [TT, 3, KW])
        PTs = sb("PTs", [TT, 2, KW])
        mx = sb("mx", [TT, 8])
        rs = sb("rs", [TT, 8])
        rc = sb("rc", [TT, 8])
        yT = sb("yT", [128, N])
        inverted = sem("inverted")
        PS = ctx.enter_context(nc.psum_tensor("n0_ps", [128, 8, 512], F32))

        consts, zeroed, bias_loaded, bias_done = sem("consts"), sem("zeroed"), sem("bias_loaded"), sem("bias_done")
        loaded, tiled, scored, maxed = sem("loaded"), sem("tiled"), sem("scored"), sem("maxed")
        exped, normed, turned = sem("exped"), sem("normed"), sem("turned")
        copied, mixed, out_read, stored = sem("copied"), sem("mixed"), sem("out_read"), sem("stored")
        quad_done = sem("quad_done")
        steps = sem("steps")
        U = 4 * QT
        NLOAD = 16 * (16 + 16 + SUB)
        kv = [first_key_row(r) for r in range(QT)]

        def read_out(dve, it, r):
            dve.wait_ge(mixed, it * U + 4 * r + 4)
            t0, t1 = (7, 14) if r == 0 else (0, 7) if r == QT - 1 else (0, 14)
            p0 = W * (2 * r - 1) + SUB * t0
            dve.tensor_copy(yT[:, p0:p0 + SUB * (t1 - t0)].rearrange("p (t s) -> p s t", s=SUB),
                            PS[:, 5 + r % 2, 0:TT].rearrange("p (s t) -> p s t", s=SUB)[:, :, t0:t1])\
               .then_inc(out_read, 1)

        block = ctx.enter_context(nc.Block())

        @block.sync
        def _(sp):
            sp.dma_start(idn[:, :], A["eye"][0:TT, 0:TT]).then_inc(consts, 16)
            sp.wait_ge(zeroed, 2)
            with sp.Fori(0, 2) as g:
                for n in range(20):
                    if n >= 2:
                        sp.wait_ge(bias_done, g * 20 + n - 1)
                    if n >= 1:
                        sp.wait_ge(bias_loaded, (g * 20 + n) * 16)
                    h, o = divmod(n, 5)
                    sp.dma_start(bnat[:, n % 2, :], S["bias"][g * 4 + h, o]).then_inc(bias_loaded, 16)
                with sp.Fori(0, B) as b:
                    it = g * B + b
                    for hh in range(4):
                        tok = g * (4 * HT) + hh * HT
                        for term in range(4):
                            rows = slice(32 * hh + 4 * term, 32 * hh + 4 * term + 4)
                            sp.dma_start(qn[rows, :, PAD:PAD + HT],
                                         S["qk0"][b, term // 2, 0:32, bass.ds(tok, HT)].rearrange("(s c) t -> c s t", c=LR))\
                              .then_inc(loaded, 16)
                            sp.dma_start(kn[rows, :, :].bitcast(F32),
                                         S["qk0"][b, (0, 1, 1, 0)[term], 32:64, bass.ds(tok, HT)]
                                         .rearrange("(s c) t -> c s t", c=LR)).then_inc(loaded, 16)
                    for s in range(SUB):
                        src = S["v0"][b, bass.ds(g * (4 * HT), 4 * HT), HD * s:HD * s + HD]
                        sp.dma_start(vt[14 * s:14 * s + 14, :, :], src.rearrange("(m t) d -> t m d", t=14))\
                          .then_inc(loaded, 16)
                    sp.wait_ge(out_read, (it + 1) * QT)
                    sp.dma_start(S["y0T"][b * 2 + g], yT[:, :]).then_inc(stored, 16)
                    sp.wait_ge(stored, (it + 1) * 16)
                    sp.sem_inc(quad_done, 1)

        @block.tensor
        def _(pe):
            pe.wait_ge(consts, 16)
            with pe.Fori(0, 2 * B) as it:
                pe.wait_ge(loaded, (it + 1) * NLOAD)
                pe.wait_ge(tiled, it + 1)
                for n in range(U + 3):
                    if n < U:
                        r, hh = divmod(n, 4)
                        if n >= 3:
                            pe.wait_ge(maxed, it * U + n - 2)
                        rows = slice(32 * hh, 32 * hh + 16)
                        pe.matmul(PS[0:TT, n % 3, 0:KW].rearrange("p (c s t) -> p c s t", c=4, s=SUB),
                                  qp[rows, TT * r:TT * r + TT],
                                  kn[rows, :, TR * kv[r]:TR * kv[r] + 56].rearrange("p s (c t) -> p c s t", c=4),
                                  start=True, stop=True).then_inc(scored, 1)
                    if 2 <= n < U + 2:
                        m = n - 2
                        pe.wait_ge(normed, it * U + m + 1)
                        if m >= 2:
                            pe.wait_ge(copied, it * U + m - 1)
                        for c in range(4):
                            last = pe.transpose(PS[0:TT, 3 + m % 2, TT * c:TT * c + TT],
                                                P[:, m % 3, TT * c:TT * c + TT], idn[:, :])
                        last.then_inc(turned, 1)
                    if n >= 3:
                        m = n - 3
                        r, hh = divmod(m, 4)
                        pe.wait_ge(copied, it * U + m + 1)
                        if hh == 0 and r >= 2:
                            pe.wait_ge(out_read, it * QT + r - 1)
                        for c in range(4):
                            last = pe.matmul(PS[32 * hh:32 * hh + 32, 5 + r % 2, 0:TT],
                                             vt[:, NT * hh + kv[r] // 2 + c, :],
                                             PTs[:, m % 2, TT * c:TT * c + TT], start=(c == 0), stop=(c == 3))
                        last.then_inc(mixed, 1)
                pe.wait_ge(quad_done, it + 1)

        @block.vector
        def _(dve):
            dve.memset(qn[:, :, :], 0.0).then_inc(zeroed, 1)
            dve.memset(kn[:, :, :].bitcast(F32), 0.0).then_inc(zeroed, 1)
            with dve.Fori(0, 2) as g:
                for n in range(20):
                    h, o = divmod(n, 5)
                    dve.wait_ge(bias_loaded, (g * 20 + n + 1) * 16)
                    dve.tensor_copy(bias[:, h, o, :].rearrange("p (c s t) -> p c s t", c=4, s=SUB),
                                    bnat[:, n % 2, :].rearrange("p (c t s) -> p c s t", c=4, s=SUB))\
                       .then_inc(bias_done, 1)
                dve.wait_ge(bias_done, (g + 1) * 20)
                dve.sem_inc(steps, 1)
                with dve.Fori(0, B) as b:
                    it = g * B + b
                    dve.wait_ge(loaded, (it + 1) * NLOAD)
                    dve.tensor_copy(qp[:, :].rearrange("p (r s t) -> p r s t", r=QT, s=SUB),
                                    qn[:, :, :].rearrange("p s (r t) -> p r s t", r=QT)).then_inc(tiled, 1)
                    for n in range(U + 4):
                        if n < U:
                            r, hh = divmod(n, 4)
                            if n >= 3:
                                dve.wait_ge(exped, it * U + n - 2)
                            dve.wait_ge(scored, it * U + n + 1)
                            dve.sem_inc(steps, 1)
                            dve.tensor_tensor_reduce(out=sm[:, n % 3, :], in0=PS[0:TT, n % 3, 0:KW],
                                                     in1=bias[:, hh, case_of(r), :], scale=1.0, scalar=3.0e38,
                                                     op0=ALU.add, op1=ALU.min, accum_out=mx[:, n % 8:n % 8 + 1])\
                               .then_inc(maxed, 1)
                        if 1 <= n < U + 1:
                            m = n - 1
                            dve.wait_ge(exped, it * U + m + 1)
                            dve.reciprocal(rc[:, m % 8:m % 8 + 1], rs[:, m % 8:m % 8 + 1]).then_inc(inverted, 1)
                            dve.wait_ge(inverted, it * U + m + 1)
                            dve.tensor_scalar(P[:, m % 3, :], P[:, m % 3, :], rc[:, m % 8:m % 8 + 1], None,
                                              ALU.mult).then_inc(normed, 1)
                        if n >= 8 and n % 4 == 0:
                            read_out(dve, it, n // 4 - 2)
                    read_out(dve, it, QT - 1)
                    dve.wait_ge(quad_done, it + 1)

        @block.scalar
        def _(act):
            with act.Fori(0, 2 * B) as it:
                for n in range(U + 2):
                    if n < U:
                        act.wait_ge(maxed, it * U + n + 1)
                        if n >= 3:
                            act.wait_ge(turned, it * U + n - 2)
                        act.activation(P[:, n % 3, :], sm[:, n % 3, :], ACT.Exp, bias=mx[:, n % 8:n % 8 + 1],
                                       scale=-1.0, accum_out=rs[:, n % 8:n % 8 + 1]).then_inc(exped, 1)
                    if n >= 2:
                        m = n - 2
                        act.wait_ge(turned, it * U + m + 1)
                        if m >= 2:
                            act.wait_ge(mixed, it * U + m - 1)
                        act.activation(PTs[:, m % 2, :], PS[0:TT, 3 + m % 2, 0:KW], ACT.Copy).then_inc(copied, 1)
                act.wait_ge(quad_done, it + 1)


def layer0_output(nc, A, S):
    with ExitStack() as ctx:
        def sb(name, shape, dt=F32):
            return ctx.enter_context(nc.sbuf_tensor("o0_" + name, shape, dt))

        def sem(name):
            return ctx.enter_context(nc.semaphore("o0_" + name))

        QB = 4
        idn = sb("idn", [TT, TT])
        wp = sb("wp", [128, CC, C])
        wqkv = sb("wqkv", [128, CC, 3 * C])
        bqk = sb("bqk", [128, QB])
        bpb = sb("bpb", [TT, C])
        bvb = sb("bvb", [128, C])
        yT = sb("yT", [128, CC, N])
        ts = sb("ts", [TT, NT, C])
        xn = sb("xn", [TT, 4, C])
        xT = sb("xT", [128, CC, N])
        stats = sb("stats", [TT, NT, 6])
        mv = sb("mv", [TT, NT, 2])
        rstd = sb("rstd", [TT, NT])
        tmp = sb("tmp", [128, 2, GW])
        high = sb("high", [128, 2, N], F32R)
        low = sb("low", [128, 2, N], F32R)
        vs = sb("vs", [128, KT, C])
        idle = sb("idle", [TT, 2])
        spread, rooted = sem("spread"), sem("rooted")
        steps = sem("steps")
        PS = ctx.enter_context(nc.psum_tensor("o0_ps", [128, 8, 512], F32))

        consts, loaded, made, summed, normed = sem("consts"), sem("loaded"), sem("made"), sem("summed"), sem("normed")
        turned, copied, chain = sem("turned"), sem("copied"), sem("chain")
        qk_made, qk_read, qk_split = sem("qk_made"), sem("qk_read"), sem("qk_split")
        v_made, v_read = sem("v_made"), sem("v_read")
        part_stored = [sem("part_stored0"), sem("part_stored1")]
        v_stored, t_stored, image_done = sem("v_stored"), sem("t_stored"), sem("image_done")
        CHAIN = 4 + QB * NG
        block = ctx.enter_context(nc.Block())

        @block.sync
        def _(sp):
            sp.dma_start(bqk[:, :], A["b_qkv"][0:2 * C].rearrange("(q p) -> p q", p=128),
                         allow_slow_non_contiguous=True).then_inc(consts, 16)
            for dst, src in ((idn[:, :], A["eye"][0:TT, 0:TT]),
                             (wp[:, :, :], A["Wp0"].rearrange("(c p) n -> p c n", p=128)),
                             (wqkv[:, :, :], A["w_qkv"].rearrange("(c p) n -> p c n", p=128)),
                             (bpb[:, :], A["bp0"].rearrange("(a n) -> a n", a=1).to_broadcast([TT, C])),
                             (bvb[:, :], A["b_qkv"][2 * C:3 * C].rearrange("(a n) -> a n", a=1).to_broadcast([128, C]))):
                sp.dma_start(dst, src).then_inc(consts, 16)
            with sp.Fori(0, B) as b:
                sp.dma_start(yT[:, :, :], S["y0T"][bass.ds(b * 2, 2)].rearrange("c p n -> p c n")).then_inc(loaded, 16)
                sp.dma_start(ts[:, :, :], A["x"][b].rearrange("(j p) c -> p j c", p=TT)).then_inc(loaded, 16)
                sp.wait_ge(summed, (b + 1) * NT)
                sp.dma_start(S["t0"][b].rearrange("(j p) c -> p j c", p=TT), ts[:, :, :]).then_inc(t_stored, 16)
                for q in range(QB):
                    sp.wait_ge(qk_split, b * (QB * NG) + (q + 1) * NG)
                    sp.sem_inc(steps, 1)
                    for part, src in ((0, high), (1, low)):
                        sp.dma_start(S["q1" if q < 2 else "k1"][part, b * 2 + q % 2],
                                     src[:, q % 2, :].bitcast(F32)).then_inc(part_stored[q % 2], 16)
                sp.wait_ge(v_read, (b + 1) * KT)
                sp.sem_inc(steps, 1)
                for g in range(2):
                    sp.dma_start(S["v1"][b * 2 + g, :, 0:KT - 1, :], vs[:, 0:KT - 1, 128 * g:128 * g + 128])\
                      .then_inc(v_stored, 16)
                    sp.dma_start(S["v1"][b * 2 + g, 0:KTAIL, KT - 1, :],
                                 vs[0:KTAIL, KT - 1, 128 * g:128 * g + 128]).then_inc(v_stored, 16)
                for w in range(2):
                    sp.wait_ge(part_stored[w], (b + 1) * (QB * 16))
                    sp.sem_inc(steps, 1)
                sp.wait_ge(v_stored, (b + 1) * 64)
                sp.sem_inc(steps, 1)
                sp.wait_ge(t_stored, (b + 1) * 16)
                sp.sem_inc(image_done, 1)

        @block.tensor
        def _(pe):
            pe.wait_ge(consts, 96)
            with pe.Fori(0, B) as b:
                pe.wait_ge(loaded, (b + 1) * 32)
                for j in range(NT):
                    if j >= 4:
                        pe.wait_ge(summed, b * NT + j - 3)
                    for c in range(CC):
                        last = pe.matmul(PS[0:TT, j % 4, 0:C], yT[:, c, TT * j:TT * j + TT], wp[:, c, :],
                                         start=(c == 0), stop=(c == CC - 1))
                    last.then_inc(made, 1)
                for g in range(NG):
                    pe.wait_ge(normed, b * NT + 4 * g + 4)
                    if g >= 2:
                        pe.wait_ge(copied, b * (CC * NG) + 2 * g - 2)
                    for c in range(CC):
                        for u in range(4):
                            last = pe.transpose(PS[:, 4 + (2 * g + c) % 4, TT * u:TT * u + TT],
                                                xn[:, u, 128 * c:128 * c + 128], idn[:, :])
                        last.then_inc(turned, 1)
                pe.wait_ge(copied, (b + 1) * (CC * NG))
                for n in range(QB * NG):
                    q, g = divmod(n, NG)
                    if n >= 4:
                        pe.wait_ge(qk_read, b * (QB * NG) + n - 3)
                    for c in range(CC):
                        last = pe.matmul(PS[:, n % 4, 0:GW], wqkv[:, c, 128 * q:128 * q + 128],
                                         xT[:, c, GW * g:GW * g + GW], start=(c == 0), stop=(c == CC - 1))
                    last.then_inc(qk_made, 1)
                for j in range(KT):
                    rows = 128 if j < KT - 1 else KTAIL
                    if j >= 4:
                        pe.wait_ge(v_read, b * KT + j - 3)
                    for c in range(CC):
                        last = pe.matmul(PS[0:rows, 4 + j % 4, 0:C], xT[:, c, 128 * j:128 * j + rows],
                                         wqkv[:, c, 2 * C:3 * C], start=(c == 0), stop=(c == CC - 1))
                    last.then_inc(v_made, 1)
                pe.wait_ge(image_done, b + 1)

        @block.scalar
        def _(act):
            with act.Fori(0, B) as b:
                root(act, rstd[:, :], spread, rooted, b + 1)
                for k in range(CC * NG):
                    g, c = divmod(k, CC)
                    act.wait_ge(turned, b * (CC * NG) + k + 1)
                    act.activation(xT[:, c, GW * g:GW * g + GW], PS[:, 4 + k % 4, 0:GW], ACT.Copy).then_inc(copied, 1)
                act.wait_ge(image_done, b + 1)

        @block.vector
        def _(dve):
            dve.memset(idle[:, :], 0.0)
            dve.wait_ge(consts, 96)
            with dve.Fori(0, B) as b:
                ch = Count(dve, chain, b * CHAIN)
                dve.wait_ge(loaded, (b + 1) * 32)
                for j in range(NT):
                    last = dve.tensor_tensor(ts[:, j, :], ts[:, j, :], bpb[:, :], ALU.add)
                ch.after(last)
                for j in range(NT):
                    dve.wait_ge(made, b * NT + j + 1)
                    dve.tensor_tensor(ts[:, j, :], PS[0:TT, j % 4, 0:C], ts[:, j, :], ALU.add).then_inc(summed, 1)
                    if j >= 1:
                        dve.wait_ge(summed, b * NT + j)
                        dve.bn_stats(stats[:, j - 1, :], ts[:, j - 1, :])
                dve.wait_ge(summed, (b + 1) * NT)
                ch.after(dve.bn_stats(stats[:, NT - 1, :], ts[:, NT - 1, :]))
                dve.tensor_copy(idle[:, 1:2], idle[:, 0:1])
                for j in range(NT):
                    last = dve.bn_aggr(mv[:, j, :], stats[:, j, :])
                ch.after(last)
                inverse_root(dve, ch, rstd[:, :], mv[:, :, 1], 1e-5, spread, rooted, b + 1)
                for j in range(NT):
                    if j >= 4:
                        dve.wait_ge(turned, b * (CC * NG) + 2 * (j // 4))
                    dve.tensor_scalar(xn[:, j % 4, :], ts[:, j, :], mv[:, j, 0:1], rstd[:, j:j + 1],
                                      ALU.subtract, ALU.mult).then_inc(normed, 1)
                for n in range(QB * NG):
                    q, g = divmod(n, NG)
                    dve.wait_ge(qk_made, b * (QB * NG) + n + 1)
                    t = tmp[:, n % 2, :]
                    dve.tensor_scalar(t, PS[:, n % 4, 0:GW], bqk[:, q:q + 1], float(C) ** -0.5 if q < 2 else 1.0,
                                      ALU.add, ALU.mult).then_inc(qk_read, 1)
                    if q >= 2 and g == 0:
                        dve.wait_ge(part_stored[q % 2], b * (QB * 16) + 32)
                    dve.wait_ge(qk_read, b * (QB * NG) + n + 1)
                    at = slice(GW * g, GW * g + GW)
                    ch.after(dve.tensor_copy(high[:, q % 2, at], t))
                    dve.tensor_tensor(low[:, q % 2, at], t, high[:, q % 2, at].bitcast(F32), ALU.subtract)\
                       .then_inc(qk_split, 1)
                for j in range(KT):
                    rows = 128 if j < KT - 1 else KTAIL
                    dve.wait_ge(v_made, b * KT + j + 1)
                    dve.tensor_tensor(vs[0:rows, j, :], PS[0:rows, 4 + j % 4, 0:C], bvb[0:rows, :], ALU.add)\
                       .then_inc(v_read, 1)
                assert ch.n == CHAIN
                dve.wait_ge(image_done, b + 1)


def layer1_attend(nc, A, S):
    with ExitStack() as ctx:
        def sb(name, shape, dt=F32):
            return ctx.enter_context(nc.sbuf_tensor("a1_" + name, shape, dt))

        def sem(name):
            return ctx.enter_context(nc.semaphore("a1_" + name))

        QUADS = 2 * B
        STEPS = NG * KT
        MX = 4 * KT * NG
        HMX = KT * NG
        PAIRS = KT // 2
        SUMS = PAIRS + 1
        HEAD_STEPS = 42
        idn = sb("idn", [128, 128])
        ones = sb("ones", [128, HD])
        qp = sb("qp", [98, 4, N], F32R)
        kp = sb("kp", [98, 4, N], F32R)
        hq = sb("hq", [96, N], F32R)
        hk = sb("hk", [96, N], F32R)
        vt = sb("vt", [128, KT, 128])
        tops = sb("tops", [128, 4 * KT, NG])
        top = sb("top", [128, 4 * KT])
        neg = sb("neg", [4 * KT, 128])
        negh = sb("negh", [4 * KT, 128], F32R)
        negl = sb("negl", [4 * KT, 128], F32R)
        P = sb("P", [128, 8, 2, GW])
        added2 = sb("added2", [128, 4, 2, GW])
        rec = sb("rec", [128, GW])
        y = sb("y", [128, 2, GW])
        yo = sb("yo", [128, 2, GW])
        PS = ctx.enter_context(nc.psum_tensor("a1_ps", [128, 8, 512], F32))
        MIX, SUM, MAX = 4, 5, 6

        consts, cleared, loaded, head_loaded = sem("consts"), sem("cleared"), sem("loaded"), sem("head_loaded")
        keyed, topped, chain, top_turned = sem("keyed"), sem("topped"), sem("chain"), sem("top_turned")
        neg_stored, neg_loaded = sem("neg_stored"), sem("neg_loaded")
        scored, exped, added, mixed, summed = sem("scored"), sem("exped"), sem("added"), sem("mixed"), sem("summed")
        taken, inverted, divided = sem("taken"), sem("inverted"), sem("divided")
        stored = [sem("stored0"), sem("stored1")]
        steps = sem("steps")
        CHAIN = 5
        KGROUPS = [(5 * u, min(5 * u + 5, KT)) for u in range(KT // 5)]
        LOADS = 3 * NG + 3 * len(KGROUPS) + len(KGROUPS) + 1

        def rows_of(t):
            return 128 if t < KT - 1 else KTAIL

        def sum_number(j, u):
            return SUMS * j + (u + 1 if u < PAIRS - 1 else SUMS)

        def maxima_by(n):
            hh = min(n // HEAD_STEPS, 3)
            within = min(max(n - HEAD_STEPS * hh - 1, 0), HEAD_STEPS - 4)
            return HMX * hh + HMX * within // (HEAD_STEPS - 4)

        block = ctx.enter_context(nc.Block())

        @block.sync
        def _(sp):
            def load_q(m, j):
                for term in range(3):
                    sp.dma_start(qp[32 * term:32 * term + 32, :, GW * j:GW * j + GW].bitcast(F32),
                                 S["q1"][(0, 0, 1)[term], m].rearrange("(h d) n -> d h n", d=HD)
                                 [:, :, GW * j:GW * j + GW]).then_inc(loaded, 16)

            def load_kv(m, u):
                t0, t1 = KGROUPS[u]
                c0, c1 = 128 * t0, min(128 * t1, N)
                for term in range(3):
                    sp.dma_start(kp[32 * term:32 * term + 32, :, c0:c1].bitcast(F32),
                                 S["k1"][(0, 1, 0)[term], m].rearrange("(h d) n -> d h n", d=HD)[:, :, c0:c1])\
                      .then_inc(loaded, 16)
                full = min(t1, KT - 1)
                sp.dma_start(vt[:, t0:full, :], S["v1"][m, :, t0:full, :]).then_inc(loaded, 16)
                if t1 == KT:
                    sp.dma_start(vt[0:KTAIL, KT - 1, :], S["v1"][m, 0:KTAIL, KT - 1, :]).then_inc(loaded, 16)

            def move_neg(m):
                sp.wait_ge(chain, (m + 1) * CHAIN)
                sp.dma_start(S["neg"][0], negh[:, :].bitcast(F32)).then_inc(neg_stored, 16)
                sp.dma_start(S["neg"][1], negl[:, :].bitcast(F32)).then_inc(neg_stored, 16)
                sp.wait_ge(neg_stored, (m + 1) * 32)
                sp.dma_start(qp[96:98, :, :].bitcast(F32),
                             S["neg"].rearrange("u (h t) p -> u h (t p)", h=4)[:, :, 0:N]).then_inc(neg_loaded, 16)

            def store_y(q, j):
                sp.wait_ge(divided, q * NG + j + 1)
                sp.dma_start(S["y1T"][q, :, GW * j:GW * j + GW], yo[:, j % 2, :]).then_inc(stored[j % 2], 16)

            def quad(q, more):
                m = q + 1
                for n in range(STEPS + 1):
                    if more and n in (1, HEAD_STEPS, 2 * HEAD_STEPS, 3 * HEAD_STEPS):
                        hh = n // HEAD_STEPS
                        sp.wait_ge(keyed, m * MX + HMX * hh)
                        for term in range(3):
                            rows = slice(32 * term, 32 * term + 32)
                            head = slice(HD * hh, HD * hh + HD)
                            sp.dma_start(hq[rows, :].bitcast(F32), S["q1"][(0, 0, 1)[term], m, head, :])\
                              .then_inc(head_loaded, 16)
                            sp.dma_start(hk[rows, :].bitcast(F32), S["k1"][(0, 1, 0)[term], m, head, :])\
                              .then_inc(head_loaded, 16)
                    if more and n > 0 and n % KT == 0:
                        sp.wait_ge(scored, q * (2 * STEPS) + 2 * n)
                        load_q(m, n // KT - 1)
                    if n > KT and n % KT == 3:
                        store_y(q, n // KT - 1)
                    if more and n > STEPS - KT and n % 5 == 0:
                        sp.wait_ge(mixed, q * STEPS + n)
                        load_kv(m, (n - (STEPS - KT)) // 5 - 1)
                if more:
                    move_neg(m)
                store_y(q, NG - 1)

            sp.dma_start(idn[:, :], A["eye"]).then_inc(consts, 16)
            for j in range(NG):
                load_q(0, j)
            for u in range(len(KGROUPS)):
                load_kv(0, u)
            move_neg(0)
            with sp.Fori(0, QUADS - 1) as q:
                quad(q, True)
            quad(QUADS - 1, False)
            for w in range(2):
                sp.wait_ge(stored[w], QUADS * 16 * ((NG + 1 - w) // 2))

        @block.tensor
        def _(pe):
            def product_for_maximum(m, i, q_of, k_of):
                hh, t, k = i // HMX, i // NG % KT, i % NG
                if i >= 2:
                    pe.wait_ge(topped, m * MX + i - 1)
                if q_of(0) is hq and i % HMX == 0:
                    pe.wait_ge(head_loaded, (m - 1) * (4 * 96) + (hh + 1) * 96)
                pe.matmul(PS[0:rows_of(t), MAX + i % 2, 0:GW], q_of(hh)[:, 128 * t:128 * t + rows_of(t)],
                          k_of(hh)[:, GW * k:GW * k + GW], start=True, stop=True).then_inc(keyed, 1)

            def turn_maxima(m):
                pe.wait_ge(chain, m * CHAIN + 2)
                pe.transpose(PS[0:4 * KT, MAX + 1, 0:128], top[:, :], idn[:, :]).then_inc(top_turned, 1)

            def mix(q, n):
                j, t = divmod(n, KT)
                rows = rows_of(t)
                pe.wait_ge(exped, q * (2 * STEPS) + 2 * n + 2)
                if t == 0 and j >= 1:
                    pe.wait_ge(taken, q * NG + j)
                if rows < 128:
                    pe.sem_inc(steps, 1)
                for hh in range(4):
                    last = pe.matmul(PS[HD * hh:HD * hh + HD, MIX, 0:GW], vt[0:rows, t, HD * hh:HD * hh + HD],
                                     P[0:rows, (2 * n + hh // 2) % 8, hh % 2, :], start=(t == 0), stop=(t == KT - 1))
                last.then_inc(mixed, 1)
                if t == KT - 1:
                    for hh in range(4):
                        last = pe.matmul(PS[HD * hh:HD * hh + HD, SUM, 0:GW], ones[0:rows, :],
                                         P[0:rows, (2 * n + hh // 2) % 8, hh % 2, :], start=False, stop=False)
                    last.then_inc(summed, 1)

            def sum_pair(q, j, u):
                pe.wait_ge(added, q * (2 * PAIRS * NG) + 2 * (PAIRS * j + u) + 2)
                if u == 0 and j >= 1:
                    pe.wait_ge(inverted, q * NG + j)
                for hh in range(4):
                    last = pe.matmul(PS[HD * hh:HD * hh + HD, SUM, 0:GW], ones[:, :],
                                     added2[:, (2 * (PAIRS * j + u) + hh // 2) % 4, hh % 2, :],
                                     start=(u == 0), stop=(u == PAIRS - 1))
                last.then_inc(summed, 1)

            def quad(q, more):
                m = q + 1
                pe.wait_ge(loaded, m * (16 * LOADS))
                pe.wait_ge(neg_loaded, m * 16)
                i = 0
                for n in range(STEPS + 3):
                    due = maxima_by(n) if more else 0
                    parts = []
                    if n < STEPS:
                        parts += [("score", 0), ("score", 1)]
                    if 1 <= n < STEPS + 1:
                        parts += [("mix", 0)]
                    if n >= 3 and (n - 3) % KT % 2 == 1:
                        parts += [("sum", 0)]
                    for at, (what, pair) in enumerate(parts):
                        if what == "score":
                            j, t = divmod(n, KT)
                            slot = 2 * n + pair
                            if slot >= 2:
                                pe.wait_ge(exped, q * (2 * STEPS) + slot - 1)
                            for e in range(2):
                                last = pe.matmul(PS[0:rows_of(t), 2 * pair + e, 0:GW],
                                                 kp[0:98, 2 * pair + e, 128 * t:128 * t + rows_of(t)],
                                                 qp[0:98, 2 * pair + e, GW * j:GW * j + GW], start=True, stop=True)
                            last.then_inc(scored, 1)
                        elif what == "mix":
                            mix(q, n - 1)
                        else:
                            sum_pair(q, (n - 3) // KT, (n - 3) % KT // 2)
                        until = i + (due - i + len(parts) - 1 - at) // (len(parts) - at)
                        while i < until:
                            product_for_maximum(m, i, lambda hh: hq, lambda hh: hk)
                            i += 1
                    if more and n == STEPS - 5:
                        assert i == MX
                        turn_maxima(m)
                pe.wait_ge(taken, m * NG)
                pe.wait_ge(inverted, m * NG)

            pe.wait_ge(consts, 16)
            pe.wait_ge(cleared, 3)
            pe.wait_ge(loaded, 16 * LOADS)
            for i in range(MX):
                product_for_maximum(0, i, lambda hh: qp[0:96, hh, :], lambda hh: kp[0:96, hh, :])
            turn_maxima(0)
            with pe.Fori(0, QUADS - 1) as q:
                quad(q, True)
            quad(QUADS - 1, False)

        @block.vector
        def _(dve):
            def maximum(m, i):
                hh, t, k = i // HMX, i // NG % KT, i % NG
                dve.wait_ge(keyed, m * MX + i + 1)
                dve.tensor_reduce(tops[0:rows_of(t), KT * hh + t, k:k + 1], PS[0:rows_of(t), MAX + i % 2, 0:GW],
                                  AX_X, ALU.max).then_inc(topped, 1)

            def negate(m):
                ch = Count(dve, chain, m * CHAIN)
                dve.wait_ge(topped, (m + 1) * MX)
                ch.after(dve.tensor_reduce(top[:, :], tops[:, :, :], AX_X, ALU.max))
                ch.after(dve.tensor_scalar(top[:, :], top[:, :], -1.0, None, ALU.mult))

            def split(m):
                ch = Count(dve, chain, m * CHAIN + 2)
                dve.wait_ge(top_turned, m + 1)
                ch.after(dve.tensor_copy(neg[:, :], PS[0:4 * KT, MAX + 1, 0:128]))
                ch.after(dve.tensor_copy(negh[:, :], neg[:, :]))
                ch.after(dve.tensor_tensor(negl[:, :], neg[:, :], negh[:, :].bitcast(F32), ALU.subtract))

            def divide(q, j):
                dve.wait_ge(summed, q * (SUMS * NG) + SUMS * (j + 1))
                if j >= 1:
                    dve.wait_ge(divided, q * NG + j)
                dve.reciprocal(rec[:, :], PS[:, SUM, 0:GW]).then_inc(inverted, 1)
                dve.wait_ge(taken, q * NG + j + 1)
                if j >= 2:
                    dve.wait_ge(stored[j % 2], q * (16 * ((NG + 1 - j % 2) // 2)) + 16 * (j // 2))
                dve.wait_ge(inverted, q * NG + j + 1)
                dve.tensor_tensor(yo[:, j % 2, :], y[:, j % 2, :], rec[:, :], ALU.mult).then_inc(divided, 1)

            def quad(q, more):
                m = q + 1
                i = 0
                for n in range(STEPS):
                    while more and i < maxima_by(n):
                        maximum(m, i)
                        i += 1
                    if more and i == MX and n == STEPS - 6:
                        negate(m)
                    if more and n == STEPS - 4:
                        split(m)
                    if n > KT and n % KT == 3:
                        divide(q, n // KT - 1)
                divide(q, NG - 1)
                for w in range(2):
                    dve.wait_ge(stored[w], m * (16 * ((NG + 1 - w) // 2)))
                dve.wait_ge(divided, m * NG)

            dve.memset(tops[:, :, :], 0.0).then_inc(cleared, 1)
            dve.memset(ones[:, :], 1.0).then_inc(cleared, 1)
            dve.memset(kp[96:98, :, :].bitcast(F32), 1.0).then_inc(cleared, 1)
            for i in range(MX):
                maximum(0, i)
            negate(0)
            split(0)
            with dve.Fori(0, QUADS - 1) as q:
                quad(q, True)
            quad(QUADS - 1, False)

        @block.scalar
        def _(act):
            def take(q, j):
                act.wait_ge(mixed, q * STEPS + KT * (j + 1))
                if j >= 2:
                    act.wait_ge(divided, q * NG + j - 1)
                act.activation(y[:, j % 2, :], PS[:, MIX, 0:GW], ACT.Copy).then_inc(taken, 1)

            def quad(q):
                for n in range(STEPS):
                    t = n % KT
                    for pair in range(2):
                        slot = 2 * n + pair
                        if n >= 4:
                            j0, t0 = divmod(n - 4, KT)
                            if pair == 0:
                                act.wait_ge(mixed, q * STEPS + n - 3)
                                if t0 == KT - 1:
                                    act.wait_ge(summed, q * (SUMS * NG) + SUMS * j0 + PAIRS)
                            if t0 < KT - 1:
                                act.wait_ge(added, q * (2 * PAIRS * NG) + 2 * (PAIRS * j0 + t0 // 2) + pair + 1)
                        act.wait_ge(scored, q * (2 * STEPS) + slot + 1)
                        act.activation(P[0:rows_of(t), slot % 8, :, :], PS[0:rows_of(t), 2 * pair:2 * pair + 2, 0:GW],
                                       ACT.Exp).then_inc(exped, 1)
                    if t == 0 and n > 0:
                        take(q, n // KT - 1)
                take(q, NG - 1)
                act.wait_ge(mixed, (q + 1) * STEPS)
                act.wait_ge(summed, (q + 1) * (SUMS * NG))
                act.wait_ge(divided, (q + 1) * NG)

            with act.Fori(0, QUADS) as q:
                quad(q)

        @block.gpsimd
        def _(pool):
            with pool.Fori(0, QUADS) as q:
                for j in range(NG):
                    for u in range(PAIRS):
                        for pair in range(2):
                            n = KT * j + 2 * u
                            a = 2 * (PAIRS * j + u) + pair
                            if pair == 0 and a >= 4:
                                before = PAIRS * j + u - 2
                                pool.wait_ge(summed, q * (SUMS * NG) + sum_number(before // PAIRS, before % PAIRS))
                            pool.wait_ge(exped, q * (2 * STEPS) + 2 * (n + 1) + pair + 1)
                            pool.tensor_tensor(added2[:, a % 4, :, :], P[:, (2 * n + pair) % 8, :, :],
                                               P[:, (2 * n + 2 + pair) % 8, :, :], ALU.add).then_inc(added, 1)
                pool.wait_ge(summed, (q + 1) * (SUMS * NG))


def layer1_output(nc, A, S):
    with ExitStack() as ctx:
        def sb(name, shape, dt=F32):
            return ctx.enter_context(nc.sbuf_tensor("o1_" + name, shape, dt))

        def sem(name):
            return ctx.enter_context(nc.semaphore("o1_" + name))

        idn = sb("idn", [TT, TT])
        wo = sb("wo", [128, CC, C])
        gw = sb("gw", [128, CC, EXP])
        bob = sb("bob", [TT, C])
        gbb = sb("gbb", [TT, EXP])
        yT = sb("yT", [128, CC, N])
        ts = sb("ts", [TT, NT, C])
        xn = sb("xn", [TT, 4, C])
        xT = sb("xT", [128, CC, N])
        stats = sb("stats", [TT, NT, 6])
        mv = sb("mv", [TT, NT, 2])
        rstd = sb("rstd", [TT, NT])
        lg = sb("lg", [TT, NT, EXP])
        zero = sb("zero", [1, C])
        idle = sb("idle", [TT, 2])
        spread, rooted = sem("spread"), sem("rooted")
        PS = ctx.enter_context(nc.psum_tensor("o1_ps", [128, 8, 512], F32))

        consts, loaded, made, summed, normed = sem("consts"), sem("loaded"), sem("made"), sem("summed"), sem("normed")
        turned, copied, chain, gated, gate_read = sem("turned"), sem("copied"), sem("chain"), sem("gated"), sem("gate_read")
        zeroed, zero_stored, stored, image_done = sem("zeroed"), sem("zero_stored"), sem("stored"), sem("image_done")
        CHAIN = 4
        block = ctx.enter_context(nc.Block())

        @block.sync
        def _(sp):
            for dst, src in ((idn[:, :], A["eye"][0:TT, 0:TT]),
                             (wo[:, :, :], A["w_out"].rearrange("(c p) n -> p c n", p=128)),
                             (gw[:, :, :], A["gate_w"].rearrange("(c p) n -> p c n", p=128)),
                             (bob[:, :], A["b_out"].rearrange("(a n) -> a n", a=1).to_broadcast([TT, C])),
                             (gbb[:, :], A["gate_b"].rearrange("(a n) -> a n", a=1).to_broadcast([TT, EXP]))):
                sp.dma_start(dst, src).then_inc(consts, 16)
            sp.wait_ge(zeroed, 1)
            sp.dma_start(S["t1"][T:T + 1, :], zero[:, :]).then_inc(zero_stored, 16)
            sp.wait_ge(zero_stored, 16)
            with sp.Fori(0, B) as b:
                sp.dma_start(yT[:, :, :], S["y1T"][bass.ds(b * 2, 2)].rearrange("c p n -> p c n")).then_inc(loaded, 16)
                sp.dma_start(ts[:, :, :], S["t0"][b].rearrange("(j p) c -> p j c", p=TT)).then_inc(loaded, 16)
                sp.wait_ge(summed, (b + 1) * NT)
                sp.dma_start(S["t1"][bass.ds(b * N, N), :].rearrange("(j p) c -> p j c", p=TT), ts[:, :, :])\
                  .then_inc(stored, 16)
                sp.dma_start(A["out"][b].rearrange("(j p) c -> p j c", p=TT), ts[:, :, :]).then_inc(stored, 16)
                sp.wait_ge(gate_read, (b + 1) * NT)
                sp.dma_start(S["logits"][:, bass.ds(b * NT, NT), :], lg[:, :, :]).then_inc(stored, 16)
                sp.wait_ge(stored, (b + 1) * 48)
                sp.sem_inc(image_done, 1)

        @block.tensor
        def _(pe):
            pe.wait_ge(consts, 80)
            with pe.Fori(0, B) as b:
                pe.wait_ge(loaded, (b + 1) * 32)
                for j in range(NT):
                    if j >= 4:
                        pe.wait_ge(summed, b * NT + j - 3)
                    for c in range(CC):
                        last = pe.matmul(PS[0:TT, j % 4, 0:C], yT[:, c, TT * j:TT * j + TT], wo[:, c, :],
                                         start=(c == 0), stop=(c == CC - 1))
                    last.then_inc(made, 1)
                for g in range(NG):
                    pe.wait_ge(normed, b * NT + 4 * g + 4)
                    if g >= 2:
                        pe.wait_ge(copied, b * (CC * NG) + 2 * g - 2)
                    for c in range(CC):
                        for u in range(4):
                            last = pe.transpose(PS[:, 4 + (2 * g + c) % 4, TT * u:TT * u + TT],
                                                xn[:, u, 128 * c:128 * c + 128], idn[:, :])
                        last.then_inc(turned, 1)
                pe.wait_ge(copied, (b + 1) * (CC * NG))
                for j in range(NT):
                    if j >= 4:
                        pe.wait_ge(gate_read, b * NT + j - 3)
                    for c in range(CC):
                        last = pe.matmul(PS[0:TT, j % 4, 0:EXP], xT[:, c, TT * j:TT * j + TT], gw[:, c, :],
                                         start=(c == 0), stop=(c == CC - 1))
                    last.then_inc(gated, 1)
                pe.wait_ge(image_done, b + 1)

        @block.scalar
        def _(act):
            with act.Fori(0, B) as b:
                root(act, rstd[:, :], spread, rooted, b + 1)
                for k in range(CC * NG):
                    g, c = divmod(k, CC)
                    act.wait_ge(turned, b * (CC * NG) + k + 1)
                    act.activation(xT[:, c, GW * g:GW * g + GW], PS[:, 4 + k % 4, 0:GW], ACT.Copy).then_inc(copied, 1)
                act.wait_ge(image_done, b + 1)

        @block.vector
        def _(dve):
            dve.memset(zero[:, :], 0.0).then_inc(zeroed, 1)
            dve.memset(idle[:, :], 0.0)
            dve.wait_ge(consts, 80)
            with dve.Fori(0, B) as b:
                ch = Count(dve, chain, b * CHAIN)
                dve.wait_ge(loaded, (b + 1) * 32)
                for j in range(NT):
                    last = dve.tensor_tensor(ts[:, j, :], ts[:, j, :], bob[:, :], ALU.add)
                ch.after(last)
                for j in range(NT):
                    dve.wait_ge(made, b * NT + j + 1)
                    dve.tensor_tensor(ts[:, j, :], PS[0:TT, j % 4, 0:C], ts[:, j, :], ALU.add).then_inc(summed, 1)
                    if j >= 1:
                        dve.wait_ge(summed, b * NT + j)
                        dve.bn_stats(stats[:, j - 1, :], ts[:, j - 1, :])
                dve.wait_ge(summed, (b + 1) * NT)
                ch.after(dve.bn_stats(stats[:, NT - 1, :], ts[:, NT - 1, :]))
                dve.tensor_copy(idle[:, 1:2], idle[:, 0:1])
                for j in range(NT):
                    last = dve.bn_aggr(mv[:, j, :], stats[:, j, :])
                ch.after(last)
                inverse_root(dve, ch, rstd[:, :], mv[:, :, 1], 1e-5, spread, rooted, b + 1)
                for j in range(NT):
                    if j >= 4:
                        dve.wait_ge(turned, b * (CC * NG) + 2 * (j // 4))
                    dve.tensor_scalar(xn[:, j % 4, :], ts[:, j, :], mv[:, j, 0:1], rstd[:, j:j + 1],
                                      ALU.subtract, ALU.mult).then_inc(normed, 1)
                for j in range(NT):
                    dve.wait_ge(gated, b * NT + j + 1)
                    dve.tensor_tensor(lg[:, j, :], PS[0:TT, j % 4, 0:EXP], gbb[:, :], ALU.add).then_inc(gate_read, 1)
                assert ch.n == CHAIN
                dve.wait_ge(image_done, b + 1)


def route(nc, A, S):
    with ExitStack() as ctx:
        def sb(name, shape, dt=F32):
            return ctx.enter_context(nc.sbuf_tensor("r_" + name, shape, dt))

        def sem(name):
            return ctx.enter_context(nc.semaphore("r_" + name))

        J = B * NT
        HALF = J // 2 * EXP
        lg = sb("lg", [TT, J, EXP])
        e1 = sb("e1", [TT, J, EXP])
        e2 = sb("e2", [TT, J, EXP])
        hot = sb("hot", [TT, J, EXP])
        back = sb("back", [TT, EXP])
        first = sb("first", [TT, EXP])
        upper = sb("upper", [TT, TT])
        ones = sb("ones", [TT, TT])
        top = sb("top", [TT, J])
        place = sb("place", [TT, J])
        prob = sb("prob", [TT, J])
        pos = sb("pos", [TT, J])
        kept = sb("kept", [TT, J])
        slot = sb("slot", [TT, J])
        slotu = sb("slotu", [TT, J], U32)
        before = sb("before", [TT, EXP, J])
        zeros = sb("zeros", [TT, J])
        token = sb("token", [TT, J])
        rows = sb("rows", [TT, J, 2])
        empty = sb("empty", [112, SLOTS // 112, 2])
        PS = ctx.enter_context(nc.psum_tensor("r_ps", [128, 4, 512], F32))
        loaded, chain, told, counted, shifted = sem("loaded"), sem("chain"), sem("told"), sem("counted"), sem("shifted")
        exped, table_cleared, scattered = sem("exped"), sem("table_cleared"), sem("scattered")
        emptied, placed = sem("emptied"), sem("placed")
        block = ctx.enter_context(nc.Block())

        def over_experts(x):
            return x.unsqueeze(2).to_broadcast([TT, J, EXP])

        def over_tokens(x):
            return x.unsqueeze(1).to_broadcast([TT, J, EXP])

        @block.sync
        def _(sp):
            for dst, src in ((lg[:, :, :], S["logits"]), (back[:, :], A["back"]), (first[:, :], A["first"]),
                             (upper[:, :], A["upper"]), (token[:, :], A["token"])):
                sp.dma_start(dst, src).then_inc(loaded, 16)
            sp.wait_ge(emptied, 2)
            sp.dma_start(S["table"].rearrange("(p a) b -> p a b", p=112), empty[:, :, :]).then_inc(table_cleared, 16)
            sp.wait_ge(table_cleared, 16)

        @block.gpsimd
        def _(pool):
            pool.memset(empty[:, :, 0], float(T)).then_inc(emptied, 1)
            pool.memset(empty[:, :, 1], 0.0).then_inc(emptied, 1)
            pool.wait_ge(table_cleared, 16)
            pool.wait_ge(placed, 1)
            for j in range(J):
                pool.indirect_dma_start(out=S["table"], out_offset=bass.IndirectOffsetOnAxis(ap=slotu[:, j:j + 1], axis=0),
                                        in_=rows[:, j, :], in_offset=None, bounds_check=SLOTS - 1,
                                        oob_is_err=False).then_inc(scattered, 16)
            pool.wait_ge(scattered, 16 * J)

        @block.scalar
        def _(act):
            act.wait_ge(shifted, 1)
            act.activation(e2[:, :, :], e2[:, :, :], ACT.Exp).then_inc(exped, 1)

        @block.tensor
        def _(pe):
            pe.wait_ge(told, 1)
            for half in range(2):
                cols = hot[:, :, :].rearrange("p j e -> p (j e)")[:, half * HALF:half * HALF + HALF]
                pe.matmul(PS[0:TT, half, 0:HALF], upper[:, :], cols, start=True, stop=True).then_inc(counted, 1)
                pe.matmul(PS[0:TT, 2 + half, 0:HALF], ones[:, :], cols, start=True, stop=True).then_inc(counted, 1)

        @block.vector
        def _(dve):
            ch = Count(dve, chain, 0)
            ch.after(dve.memset(ones[:, :], 1.0))
            ch.after(dve.memset(zeros[:, :], 0.0))
            dve.wait_ge(loaded, 80)
            ch.after(dve.tensor_reduce(top[:, :], lg[:, :, :], AX_X, ALU.max))
            ch.after(dve.tensor_tensor(e2[:, :, :], lg[:, :, :], over_experts(top[:, :]), ALU.subtract))
            ch.after(dve.tensor_scalar(e1[:, :, :], e2[:, :, :], 0.0, None, ALU.is_ge))
            dve.sem_inc(shifted, 1)
            ch.after(dve.tensor_tensor(e1[:, :, :], e1[:, :, :], over_tokens(back[:, :]), ALU.mult))
            ch.after(dve.tensor_reduce(place[:, :], e1[:, :, :], AX_X, ALU.max))
            dve.tensor_tensor(hot[:, :, :], over_tokens(back[:, :]), over_experts(place[:, :]), ALU.is_equal)\
               .then_inc(told, 1)
            dve.wait_ge(exped, 1)
            ch.after(dve.tensor_reduce(prob[:, :], e2[:, :, :], AX_X, ALU.add))
            dve.wait_ge(counted, 4)
            for half in range(2):
                last = dve.tensor_copy(e1[:, half * (J // 2):(half + 1) * (J // 2), :],
                                       PS[0:TT, 2 + half, 0:HALF].rearrange("p (j e) -> p j e", e=EXP))
            ch.after(last)
            for e in range(EXP):
                last = dve.tensor_tensor_scan(out=before[:, e, :], data0=e1[:, :, e], data1=zeros[:, :], initial=0.0,
                                              op0=ALU.add, op1=ALU.add)
            ch.after(last)
            ch.after(dve.tensor_tensor(e1[:, :, :], before[:, :, :].rearrange("p e j -> p j e"), e1[:, :, :],
                                       ALU.subtract))
            for half in range(2):
                part = e1[:, half * (J // 2):(half + 1) * (J // 2), :]
                last = dve.tensor_tensor(part, PS[0:TT, half, 0:HALF].rearrange("p (j e) -> p j e", e=EXP), part,
                                         ALU.add)
            ch.after(last)
            ch.after(dve.tensor_tensor(e2[:, :, :], e1[:, :, :], hot[:, :, :], ALU.mult))
            ch.after(dve.tensor_reduce(pos[:, :], e2[:, :, :], AX_X, ALU.add))
            ch.after(dve.tensor_tensor(e2[:, :, :], hot[:, :, :], over_tokens(first[:, :]), ALU.mult))
            ch.after(dve.tensor_reduce(slot[:, :], e2[:, :, :], AX_X, ALU.add))
            ch.after(dve.tensor_scalar(kept[:, :], pos[:, :], float(CAP), float(2 * SLOTS), ALU.is_gt, ALU.mult))
            ch.after(dve.tensor_tensor(slot[:, :], slot[:, :], pos[:, :], ALU.add))
            ch.after(dve.tensor_tensor(slot[:, :], slot[:, :], kept[:, :], ALU.add))
            ch.after(dve.tensor_scalar(slotu[:, :], slot[:, :], -1.0, None, ALU.add))
            ch.after(dve.reciprocal(rows[:, :, 1], prob[:, :]))
            dve.tensor_copy(rows[:, :, 0], token[:, :]).then_inc(placed, 1)


def experts(nc, A, S):
    with ExitStack() as ctx:
        def sb(name, shape, dt=F32):
            return ctx.enter_context(nc.sbuf_tensor("e_" + name, shape, dt))

        def sem(name):
            return ctx.enter_context(nc.semaphore("e_" + name))

        FB = FF // 128
        ST = (CAP + 127) // 128
        STAIL = CAP - 128 * (ST - 1)
        SG = (ST + 3) // 4
        idn = sb("idn", [128, 128])
        w1 = sb("w1", [128, CC, FF])
        w2 = sb("w2", [128, FB, C])
        b1 = sb("b1", [128, FB])
        b2b = sb("b2b", [128, C])
        tab = sb("tab", [128, ST, 2])
        tok = sb("tok", [128, ST], U32)
        xg = sb("xg", [128, ST, C])
        xn = sb("xn", [128, 4, C])
        stats = sb("stats", [128, ST, 6])
        mv = sb("mv", [128, ST, 2])
        rstd = sb("rstd", [128, ST])
        xT = sb("xT", [128, 2, CC, 512])
        hT = sb("hT", [128, FB, 512])
        y = sb("y", [128, 2, C])
        none = sb("none", [128, C])
        fin = sb("fin", [128, 2, C], U8)
        nan = sb("nan", [128, 2, C], U8)
        yf = sb("yf", [128, 2, C])
        idle = sb("idle", [128, 2])
        spread, rooted = sem("spread"), sem("rooted")
        PS = ctx.enter_context(nc.psum_tensor("e_ps", [128, 8, 512], F32))
        consts, cleared, loaded, told, gathered = sem("consts"), sem("cleared"), sem("loaded"), sem("told"), sem("gathered")
        chain, normed, turned, copied = sem("chain"), sem("normed"), sem("turned"), sem("copied")
        hidden, relued, made, finished = sem("hidden"), sem("relued"), sem("made"), sem("finished")
        read, expert_done = sem("read"), sem("expert_done")
        scattered = [sem("scattered0"), sem("scattered1")]
        steps = sem("steps")
        CHAIN = 3 * SG + 4 * ST

        def size(t):
            return 128 if t < ST - 1 else STAIL

        def width(g):
            return min(512, CAP - 512 * g)

        block = ctx.enter_context(nc.Block())

        @block.sync
        def _(sp):
            sp.dma_start(idn[:, :], A["eye"]).then_inc(consts, 16)
            sp.wait_ge(cleared, 1)
            with sp.Fori(0, EXP) as e:
                sp.dma_start(tab[:, 0:ST - 1, :],
                             S["table"][bass.ds(e * CAP, 128 * (ST - 1)), :].rearrange("(t p) b -> p t b", p=128))\
                  .then_inc(loaded, 16)
                sp.dma_start(tab[0:STAIL, ST - 1, :], S["table"][bass.ds(e * CAP + 128 * (ST - 1), STAIL), :])\
                  .then_inc(loaded, 16)
                sp.dma_start(w1[:, :, :], A["w1"][e].rearrange("(c p) n -> p c n", p=128)).then_inc(loaded, 16)
                sp.dma_start(w2[:, :, :], A["w2"][e].rearrange("(c p) n -> p c n", p=128)).then_inc(loaded, 16)
                sp.dma_start(b1[:, :], A["b1"][e].rearrange("(c p) -> p c", p=128),
                             allow_slow_non_contiguous=True).then_inc(loaded, 16)
                sp.dma_start(b2b[:, :], A["b2"][bass.ds(e, 1), :].to_broadcast([128, C])).then_inc(loaded, 16)
                for w in scattered:
                    sp.wait_ge(w, (e + 1) * (8 * ST))
                sp.sem_inc(expert_done, 1)

        @block.gpsimd
        def _(pool):
            with pool.Fori(0, EXP) as e:
                pool.wait_ge(told, e + 1)
                pool.sem_inc(steps, 1)
                for t in range(ST):
                    pool.indirect_dma_start(out=xg[0:size(t), t, :], out_offset=None, in_=S["t1"],
                                            in_offset=bass.IndirectOffsetOnAxis(ap=tok[0:size(t), t:t + 1], axis=0))\
                        .then_inc(gathered, 16)
                for t in range(ST):
                    pool.wait_ge(finished, e * ST + t + 1)
                    pool.sem_inc(steps, 1)
                    pool.indirect_dma_start(out=A["out_rows"],
                                            out_offset=bass.IndirectOffsetOnAxis(ap=tok[0:size(t), t:t + 1], axis=0),
                                            in_=yf[0:size(t), t % 2, :], in_offset=None, bounds_check=T - 1,
                                            oob_is_err=False).then_inc(scattered[t % 2], 16)
                pool.wait_ge(expert_done, e + 1)

        @block.tensor
        def _(pe):
            pe.wait_ge(consts, 16)
            with pe.Fori(0, EXP) as e:
                pe.wait_ge(loaded, (e + 1) * 96)
                for g in range(SG):
                    tiles = range(4 * g, min(4 * g + 4, ST))
                    pe.wait_ge(normed, e * ST + tiles[-1] + 1)
                    for c in range(CC):
                        if g >= 1:
                            pe.wait_ge(copied, e * (CC * SG) + (g - 1) * CC + c + 1)
                        for t in tiles:
                            last = pe.transpose(PS[:, c, 128 * (t % 4):128 * (t % 4) + size(t)],
                                                xn[0:size(t), t % 4, 128 * c:128 * c + 128],
                                                idn[0:size(t), 0:size(t)])
                        last.then_inc(turned, 1)
                    pe.wait_ge(copied, e * (CC * SG) + (g + 1) * CC)
                    for f in range(FB):
                        n = g * FB + f
                        if n >= 3:
                            pe.wait_ge(relued, e * (SG * FB) + n - 2)
                        for c in range(CC):
                            last = pe.matmul(PS[:, 2 + n % 3, 0:width(g)], w1[:, c, 128 * f:128 * f + 128],
                                             xT[:, g % 2, c, 0:width(g)], start=(c == 0), stop=(c == CC - 1))
                        last.then_inc(hidden, 1)
                    pe.wait_ge(relued, e * (SG * FB) + (g + 1) * FB)
                    for t in tiles:
                        if t >= 2:
                            pe.wait_ge(read, e * ST + t - 1)
                        for f in range(FB):
                            last = pe.matmul(PS[0:size(t), 5 + t % 2, 0:C],
                                             hT[:, f, 128 * (t % 4):128 * (t % 4) + size(t)], w2[:, f, :],
                                             start=(f == 0), stop=(f == FB - 1))
                        last.then_inc(made, 1)
                pe.wait_ge(expert_done, e + 1)

        @block.scalar
        def _(act):
            with act.Fori(0, EXP) as e:
                act.wait_ge(loaded, (e + 1) * 96)
                for g in range(SG):
                    root(act, rstd[:, 4 * g:min(4 * g + 4, ST)], spread, rooted, e * SG + g + 1)
                    for c in range(CC):
                        act.wait_ge(turned, e * (CC * SG) + g * CC + c + 1)
                        act.activation(xT[:, g % 2, c, 0:width(g)], PS[:, c, 0:width(g)], ACT.Copy).then_inc(copied, 1)
                    if g >= 1:
                        act.wait_ge(made, e * ST + 4 * g)
                    for f in range(FB):
                        n = g * FB + f
                        act.wait_ge(hidden, e * (SG * FB) + n + 1)
                        act.activation(hT[:, f, 0:width(g)], PS[:, 2 + n % 3, 0:width(g)], ACT.Relu,
                                       bias=b1[:, f:f + 1]).then_inc(relued, 1)
                act.wait_ge(expert_done, e + 1)

        @block.vector
        def _(dve):
            dve.memset(idle[:, :], 0.0)
            dve.memset(mv[:, :, :], 0.0)
            dve.memset(none[:, :], 0.0)
            dve.memset(tab[:, ST - 1, :], float(T)).then_inc(cleared, 1)
            with dve.Fori(0, EXP) as e:
                ch = Count(dve, chain, e * CHAIN)
                dve.wait_ge(loaded, (e + 1) * 96)
                dve.tensor_copy(tok[:, :], tab[:, :, 0]).then_inc(told, 1)

                def finish(t):
                    s = size(t)
                    y_, f_, n_, o_ = (v[0:s, t % 2, :] for v in (y, fin, nan, yf))
                    dve.wait_ge(made, e * ST + t + 1)
                    dve.tensor_tensor(y_, PS[0:s, 5 + t % 2, 0:C], b2b[0:s, :], ALU.add).then_inc(read, 1)
                    dve.wait_ge(read, e * ST + t + 1)
                    ch.after(dve.tensor_scalar(y_, y_, tab[0:s, t, 1:2], None, ALU.mult))
                    dve.tensor_scalar(f_, y_, 0.0, 0.0, ALU.mult, ALU.is_equal)
                    dve.tensor_tensor(n_, y_, y_, ALU.not_equal)
                    if t >= 2:
                        dve.wait_ge(scattered[t % 2], e * (8 * ST) + 16 * (t // 2))
                    ch.after(dve.tensor_scalar(o_, y_, -1.0e4, 1.0e4, ALU.max, ALU.min))
                    dve.tensor_copy(idle[:, 1:2], idle[:, 0:1])
                    ch.after(dve.copy_predicated(o_, n_, none[0:s, :]))
                    dve.tensor_copy(idle[:, 1:2], idle[:, 0:1])
                    ch.after(dve.copy_predicated(o_, f_, y_))
                    dve.tensor_tensor(o_, o_, xg[0:s, t, :], ALU.add).then_inc(finished, 1)

                for g in range(SG):
                    tiles = range(4 * g, min(4 * g + 4, ST))
                    for t in tiles:
                        s = size(t)
                        if t == 0:
                            dve.wait_ge(gathered, (e + 1) * (16 * ST))
                        last = dve.bn_stats(stats[0:s, t, :], xg[0:s, t, :])
                    ch.after(last)
                    dve.tensor_copy(idle[:, 1:2], idle[:, 0:1])
                    for t in tiles:
                        last = dve.bn_aggr(mv[0:size(t), t, :], stats[0:size(t), t, :])
                    ch.after(last)
                    inverse_root(dve, ch, rstd[:, 4 * g:tiles[-1] + 1], mv[:, 4 * g:tiles[-1] + 1, 1], 1e-5,
                                 spread, rooted, e * SG + g + 1)
                    for t in tiles:
                        s = size(t)
                        if g >= 1:
                            dve.wait_ge(turned, e * (CC * SG) + g * CC)
                        dve.tensor_scalar(xn[0:s, t % 4, :], xg[0:s, t, :], mv[0:s, t, 0:1], rstd[0:s, t:t + 1],
                                          ALU.subtract, ALU.mult).then_inc(normed, 1)
                    if g >= 1:
                        for t in range(4 * g - 4, 4 * g):
                            finish(t)
                for t in range(4 * SG - 4, ST):
                    finish(t)
                assert ch.n == CHAIN, ch.n
                dve.wait_ge(expert_done, e + 1)


STAGES = (layer0_bias_tables, layer0_project, layer0_attend, layer0_output, layer1_attend, layer1_output, route, experts)

SCRATCH = {
    "toeplitz": [W, NH * RPB, W],
    "bias": [NH, 5, TT, 8 * W],
    "qk0": [B, 2, 64, N],
    "v0": [B, N, C],
    "y0T": [2 * B, 128, N],
    "t0": [B, N, C],
    "q1": [2, 2 * B, 128, N],
    "k1": [2, 2 * B, 128, N],
    "v1": [2 * B, 128, KT, 128],
    "neg": [2, 4 * KT, 128],
    "y1T": [2 * B, 128, N],
    "t1": [T + 1, C],
    "logits": [TT, B * NT, EXP],
    "table": [SLOTS, 2],
}

INPUTS = {
    "x": "x", "L0_conv_Wq": "Wq0", "L0_conv_bq": "bq0", "L0_conv_Wk": "Wk0", "L0_conv_bk": "bk0",
    "L0_conv_Wv": "Wv0", "L0_conv_bv": "bv0", "L0_conv_rpb": "rpb", "L0_conv_Wp": "Wp0", "L0_conv_bp": "bp0",
    "L1_attn_w_qkv": "w_qkv", "L1_attn_b_qkv": "b_qkv", "L1_attn_w_out": "w_out", "L1_attn_b_out": "b_out",
    "L1_ffn_gate_w": "gate_w", "L1_ffn_gate_b": "gate_b", "L1_ffn_w1": "w1", "L1_ffn_b1": "b1",
    "L1_ffn_w2": "w2", "L1_ffn_b2": "b2",
}


def shape_constants():
    one = np.ones((128, 1), np.float32)
    group = C // 32
    return {
        "eye": np.eye(128, dtype=np.float32),
        "group_mean": np.kron(np.eye(128 // group, dtype=np.float32), np.full((group, group), 1.0 / group, np.float32)),
        "qk_scale": np.concatenate([one[:32] * np.float32(-HD ** -0.5), one[:32]]),
        "upper": np.triu(np.ones((TT, TT), np.float32)),
        "back": np.tile(np.arange(EXP, 0, -1, dtype=np.float32), (TT, 1)),
        "first": np.tile(np.arange(EXP, dtype=np.float32) * CAP, (TT, 1)),
        "token": np.arange(T, dtype=np.float32).reshape(B * NT, TT).T.copy(),
    }


def build(nc, A, S):
    A = dict(A)
    A["x"] = A["x"].rearrange("b h w c -> b (h w) c")
    A["out_rows"] = A["out"].rearrange("b h w c -> (b h w) c")
    A["out"] = A["out"].rearrange("b h w c -> b (h w) c")
    for stage in STAGES:
        stage(nc, A, S)


def kernel(**inputs):
    import concourse.bacc as bacc
    from concourse.bass_utils import run_bass_kernel_spmd

    nc = bacc.Bacc("TRN2", target_bir_lowering=False, num_devices=1)
    arrays, A = {}, {}
    given = {short: np.ascontiguousarray(inputs[name]) for name, short in INPUTS.items()}
    for short, a in {**given, **shape_constants()}.items():
        arrays["in_" + short] = a
        A[short] = nc.dram_tensor("in_" + short, a.shape, mybir.dt.from_np(a.dtype), kind="ExternalInput").ap()
    A["out"] = nc.dram_tensor("result", (B, H, W, C), F32, kind="ExternalOutput").ap()
    S = {n: nc.dram_tensor("scratch_" + n, s, F32, kind="Internal").ap() for n, s in SCRATCH.items()}
    build(nc, A, S)
    r = run_bass_kernel_spmd(nc, [arrays], core_ids=[0])
    return r.results[0]["result"]
```

```python
from contextlib import ExitStack

import numpy as np
import concourse.bass as bass
from concourse import mybir

F32 = mybir.dt.float32
F32R = mybir.dt.float32r
U32 = mybir.dt.uint32
U8 = mybir.dt.uint8
ALU = mybir.AluOpType
ACT = mybir.ActivationFunctionType
AX_X = mybir.AxisListType.X

B, H, W, C = 4, 56, 56, 256
N = H * W
T = B * N
TT = 112
NT = N // TT
GW = 4 * TT
NG = N // GW
CC = C // 128
NH, HD, LR = 8, 32, 4
K7 = 7
RPB = 2 * K7 - 1
SUB = W // K7
HT = N // NH
TR = HT // H
QT = 29
CASES = (1, -1, -3, -5, -7)
EXP, FF = 8, 1024
CAP = -(-5 * T // (4 * EXP))
SLOTS = EXP * CAP
FAR = 1.0e30
KT = (N + 127) // 128
KTAIL = N - 128 * (KT - 1)


def first_key_row(r):
    return min(max(2 * r - 4, 0), H - 8)


def case_of(r):
    return CASES.index(first_key_row(r) - (2 * r - 1))


def window_start(i, n):
    return min(max(i - K7 // 2, 0), n - K7)


class Count:

    def __init__(self, eng, sem, base):
        self.eng, self.sem, self.base, self.n = eng, sem, base, 0

    def after(self, instruction):
        self.n += 1
        instruction.then_inc(self.sem, 1)
        self.eng.wait_ge(self.sem, self.base + self.n)


def inverse_root(dve, ch, out, variance, eps, spread, rooted, n):
    dve.tensor_scalar(out, variance, eps, None, ALU.add).then_inc(spread, 1)
    dve.wait_ge(rooted, n)
    ch.after(dve.reciprocal(out, out))


def root(act, out, spread, rooted, n):
    act.wait_ge(spread, n)
    act.activation(out, out, ACT.Sqrt).then_inc(rooted, 1)


def layer0_project(nc, A, S):
    with ExitStack() as ctx:
        def sb(name, shape, dt=F32):
            return ctx.enter_context(nc.sbuf_tensor("p0_" + name, shape, dt))

        def sem(name):
            return ctx.enter_context(nc.semaphore("p0_" + name))

        idn = sb("idn", [TT, TT])
        blk = sb("blk", [128, 128])
        wqk = sb("wqk", [128, CC, 64])
        wv = sb("wv", [128, CC, C])
        bqk = sb("bqk", [64, 1])
        sqk = sb("sqk", [64, 1])
        bvb = sb("bvb", [TT, C])
        xs = sb("xs", [TT, NT, C])
        xT = sb("xT", [128, CC, N])
        stats = sb("stats", [128, CC, NG, 6])
        mv = sb("mv", [128, CC, 2])
        gm = sb("gm", [128, CC])
        dd = sb("dd", [128, CC])
        vv = sb("vv", [128, CC])
        rstd = sb("rstd", [128, CC])
        tmp = sb("tmp", [64, 2, GW])
        qkh = sb("qkh", [64, N], F32R)
        qkl = sb("qkl", [64, N], F32R)
        vs = sb("vs", [TT, NT, C])
        idle = sb("idle", [128, 2])
        far = sb("far", [128, 2 * GW * 5])
        rp = sb("rp", [NH * RPB, RPB])
        rn = sb("rn", [NH * RPB, RPB])
        PS = ctx.enter_context(nc.psum_tensor("p0_ps", [128, 8, 512], F32))

        consts, loaded, turned, copied = sem("consts"), sem("loaded"), sem("turned"), sem("copied")
        stat, grouped, normed, chain = sem("stat"), sem("grouped"), sem("normed"), sem("chain")
        qk_made, qk_read, qk_split = sem("qk_made"), sem("qk_read"), sem("qk_split")
        v_made, v_read, stored, image_done = sem("v_made"), sem("v_read"), sem("stored"), sem("image_done")
        spread, rooted = sem("spread"), sem("rooted")
        rpb_loaded, filled, negated = sem("rpb_loaded"), sem("far_filled"), sem("rpb_negated")
        tables_filled, placed, tiled = sem("tables_filled"), sem("rows_placed"), sem("tiles_placed")
        CHAIN = 5 + NG

        block = ctx.enter_context(nc.Block())

        @block.gpsimd
        def _(pool):
            pool.wait_ge(filled, 1)
            for h in range(0, NH, 2):
                pool.dma_start(S["toeplitz"][:, h * RPB:(h + 2) * RPB, :].rearrange("j r c -> j (r c)"),
                               far[0:W, 0:2 * RPB * W]).then_inc(tables_filled, 16)
            pool.dma_start(S["bias"].rearrange("h o p f -> p h o f")[:, 0:2],
                           far[0:TT, 0:2 * 5 * GW].rearrange("p (h o f) -> p h o f", h=2, o=5)).then_inc(tables_filled, 16)
            for h in range(2, NH, 2):
                pool.dma_start(S["bias"].rearrange("h o p f -> p h o f")[:, h:h + 2],
                               far[0:TT, 0:2 * 5 * GW].rearrange("p (h o f) -> p h o f", h=2, o=5)).then_inc(tables_filled, 16)
            pool.wait_ge(tables_filled, 16 * NH)
            pool.wait_ge(negated, 1)
            for j in range(W):
                c0 = window_start(j, W)
                pool.dma_start(S["toeplitz"][j, :, c0:c0 + K7], rn[:, c0 - j + K7 - 1:c0 - j + 2 * K7 - 1]).then_inc(placed, 16)
            pool.wait_ge(placed, 16 * W)
            n = 0
            for o in range(len(CASES)):
                r = next(r for r in range(QT) if case_of(r) == o)
                for ri in range(2):
                    i = 2 * r - 1 + ri
                    if not 0 <= i < H:
                        continue
                    kk = window_start(i, H) - first_key_row(r)
                    dr = window_start(i, H) - i + K7 - 1
                    for h in range(NH):
                        src = S["toeplitz"][:, h * RPB + dr:h * RPB + dr + K7, :].rearrange("(t s) r c -> s t (r c)", s=SUB)
                        dst = S["bias"][h, o].rearrange("(s r t) f -> s r t f", s=SUB, r=2)[:, ri, :, kk * W:(kk + K7) * W]
                        pool.dma_start(dst, src).then_inc(tiled, 16)
                        n += 1
            pool.wait_ge(tiled, 16 * n)

        @block.sync
        def _(sp):
            sp.dma_start(rp[:, :], A["rpb"].rearrange("h a b -> (h a) b")).then_inc(rpb_loaded, 16)
            for dst, src in ((idn[:, :], A["eye"][0:TT, 0:TT]), (blk[:, :], A["group_mean"]),
                             (wqk[:, :, 0:32], A["Wq0"].rearrange("(c p) n -> p c n", p=128)),
                             (wqk[:, :, 32:64], A["Wk0"].rearrange("(c p) n -> p c n", p=128)),
                             (wv[:, :, :], A["Wv0"].rearrange("(c p) n -> p c n", p=128)),
                             (bqk[0:32, :], A["bq0"].rearrange("(p a) -> p a", a=1)),
                             (bqk[32:64, :], A["bk0"].rearrange("(p a) -> p a", a=1)),
                             (sqk[:, :], A["qk_scale"]),
                             (bvb[:, :], A["bv0"].rearrange("(a n) -> a n", a=1).to_broadcast([TT, C]))):
                sp.dma_start(dst, src).then_inc(consts, 16)
            with sp.Fori(0, B) as b:
                sp.dma_start(xs[:, :, :], A["x"][b].rearrange("(j p) c -> p j c", p=TT)).then_inc(loaded, 16)
                sp.wait_ge(qk_split, (b + 1) * NG)
                sp.dma_start(S["qk0"][b, 0], qkh[:, :].bitcast(F32)).then_inc(stored, 16)
                sp.dma_start(S["qk0"][b, 1], qkl[:, :].bitcast(F32)).then_inc(stored, 16)
                sp.wait_ge(v_read, (b + 1) * NT)
                sp.dma_start(S["v0"][b].rearrange("(j p) c -> p j c", p=TT), vs[:, :, :]).then_inc(stored, 16)
                sp.wait_ge(stored, (b + 1) * 48)
                sp.sem_inc(image_done, 1)

        @block.tensor
        def _(pe):
            pe.wait_ge(consts, 144)
            with pe.Fori(0, B) as b:
                pe.wait_ge(loaded, (b + 1) * 16)
                for k in range(CC * NG):
                    g, c = divmod(k, CC)
                    if k >= 4:
                        pe.wait_ge(copied, b * (CC * NG) + k - 3)
                    for u in range(4):
                        last = pe.transpose(PS[:, k % 4, TT * u:TT * u + TT], xs[:, 4 * g + u, 128 * c:128 * c + 128],
                                            idn[:, :])
                    last.then_inc(turned, 1)
                for w, what in enumerate((mv[:, :, 0], vv[:, :])):
                    pe.wait_ge(stat, b * 2 + w + 1)
                    pe.matmul(PS[:, 4 + w, 0:CC], blk[:, :], what, start=True, stop=True).then_inc(grouped, 1)
                pe.wait_ge(normed, (b + 1) * CC)
                for g in range(NG):
                    if g >= 4:
                        pe.wait_ge(qk_read, b * NG + g - 3)
                    for c in range(CC):
                        last = pe.matmul(PS[0:64, g % 4, 0:GW], wqk[:, c, :], xT[:, c, GW * g:GW * g + GW],
                                         start=(c == 0), stop=(c == CC - 1))
                    last.then_inc(qk_made, 1)
                for j in range(NT):
                    if j >= 4:
                        pe.wait_ge(v_read, b * NT + j - 3)
                    for c in range(CC):
                        last = pe.matmul(PS[0:TT, 4 + j % 4, 0:C], xT[:, c, TT * j:TT * j + TT], wv[:, c, :],
                                         start=(c == 0), stop=(c == CC - 1))
                    last.then_inc(v_made, 1)
                pe.wait_ge(image_done, b + 1)

        @block.scalar
        def _(act):
            with act.Fori(0, B) as b:
                for k in range(CC * NG):
                    g, c = divmod(k, CC)
                    act.wait_ge(turned, b * (CC * NG) + k + 1)
                    act.activation(xT[:, c, GW * g:GW * g + GW], PS[:, k % 4, 0:GW], ACT.Copy).then_inc(copied, 1)
                root(act, rstd[:, :], spread, rooted, b + 1)
                act.wait_ge(image_done, b + 1)

        @block.vector
        def _(dve):
            dve.memset(idle[:, :], 0.0)
            dve.memset(far[:, :], FAR).then_inc(filled, 1)
            dve.wait_ge(rpb_loaded, 16)
            dve.tensor_scalar(rn[:, :], rp[:, :], -1.0, None, ALU.mult).then_inc(negated, 1)
            dve.wait_ge(consts, 144)
            with dve.Fori(0, B) as b:
                ch = Count(dve, chain, b * CHAIN)
                for k in range(CC * NG):
                    g, c = divmod(k, CC)
                    dve.wait_ge(copied, b * (CC * NG) + k + 1)
                    last = dve.bn_stats(stats[:, c, g, :], xT[:, c, GW * g:GW * g + GW])
                ch.after(last)
                dve.tensor_copy(idle[:, 1:2], idle[:, 0:1])
                for c in range(CC):
                    last = dve.bn_aggr(mv[:, c, :], stats[:, c, :, :].rearrange("p g s -> p (g s)"))
                last.then_inc(stat, 1)
                dve.wait_ge(grouped, b * 2 + 1)
                ch.after(dve.tensor_copy(gm[:, :], PS[:, 4, 0:CC]))
                ch.after(dve.tensor_tensor(dd[:, :], mv[:, :, 0], gm[:, :], ALU.subtract))
                ch.after(dve.tensor_tensor(dd[:, :], dd[:, :], dd[:, :], ALU.mult))
                dve.tensor_tensor(vv[:, :], dd[:, :], mv[:, :, 1], ALU.add).then_inc(stat, 1)
                dve.wait_ge(grouped, b * 2 + 2)
                inverse_root(dve, ch, rstd[:, :], PS[:, 5, 0:CC], 1e-5, spread, rooted, b + 1)
                for c in range(CC):
                    dve.tensor_scalar(xT[:, c, :], xT[:, c, :], gm[:, c:c + 1], rstd[:, c:c + 1],
                                      ALU.subtract, ALU.mult).then_inc(normed, 1)
                for g in range(NG):
                    dve.wait_ge(qk_made, b * NG + g + 1)
                    t = tmp[:, g % 2, :]
                    dve.tensor_scalar(t, PS[0:64, g % 4, 0:GW], bqk[:, 0:1], sqk[:, 0:1], ALU.add, ALU.mult)\
                       .then_inc(qk_read, 1)
                    dve.wait_ge(qk_read, b * NG + g + 1)
                    ch.after(dve.tensor_copy(qkh[:, GW * g:GW * g + GW], t))
                    dve.tensor_tensor(qkl[:, GW * g:GW * g + GW], t, qkh[:, GW * g:GW * g + GW].bitcast(F32),
                                      ALU.subtract).then_inc(qk_split, 1)
                for j in range(NT):
                    dve.wait_ge(v_made, b * NT + j + 1)
                    dve.tensor_tensor(vs[:, j, :], PS[0:TT, 4 + j % 4, 0:C], bvb[:, :], ALU.add).then_inc(v_read, 1)
                assert ch.n == CHAIN
                dve.wait_ge(image_done, b + 1)


def layer0_attend(nc, A, S):
    with ExitStack() as ctx:
        def sb(name, shape, dt=F32):
            return ctx.enter_context(nc.sbuf_tensor("n0_" + name, shape, dt))

        def sem(name):
            return ctx.enter_context(nc.semaphore("n0_" + name))

        PAD = TR
        KW = 8 * W
        U = 4 * QT
        NLOAD = 16 * (16 + 16 + SUB)
        INVERT, NORM, TURN, COPY, MIX, READ = 2, 3, 4, 5, 9, 14
        NSM, NP, NPT = 4, 6, 12
        BS, BT, BO = 0, 3, 6
        idn = sb("idn", [TT, TT])
        bias = sb("bias", [TT, 4, 5, KW])
        bnat = sb("bnat", [TT, 2, 5, KW])
        qn = sb("qn", [128, SUB, HT + 2 * PAD])
        qp = sb("qp", [128, QT * TT], F32R)
        kn = sb("kn", [128, SUB, HT], F32R)
        kp = sb("kp", [128, SUB, HT], F32R)
        vn = sb("vn", [TT, 4 * NT, HD])
        vt = sb("vt", [TT, 4 * NT, HD])
        sm = sb("sm", [TT, NSM, KW])
        P = sb("P", [TT, NP, KW])
        PTs = sb("PTs", [TT, NPT, KW])
        mx = sb("mx", [TT, 8])
        rs = sb("rs", [TT, 8])
        rc = sb("rc", [TT, 8])
        yT = sb("yT", [128, N])
        PS = ctx.enter_context(nc.psum_tensor("n0_ps", [128, 8, 512], F32))

        consts, zeroed, bias_done = sem("consts"), sem("zeroed"), sem("bias_done")
        bias_loaded = [sem("bias_loaded0"), sem("bias_loaded1")]
        loaded, queries_placed, keys_placed = sem("loaded"), sem("queries_placed"), sem("keys_placed")
        values_placed, scored, maxed = sem("values_placed"), sem("scored"), sem("maxed")
        exped, inverted, normed, turned = sem("exped"), sem("inverted"), sem("normed"), sem("turned")
        copied, mixed, out_read, stored = sem("copied"), sem("mixed"), sem("out_read"), sem("stored")
        steps = sem("steps")
        kv = [first_key_row(r) for r in range(QT)]

        block = ctx.enter_context(nc.Block())

        @block.sync
        def _(sp):
            def load(g, b, it):
                if it is not None:
                    sp.wait_ge(queries_placed, it)
                    sp.wait_ge(keys_placed, it)
                    sp.wait_ge(values_placed, it)
                for hh in range(4):
                    tok = g * (4 * HT) + hh * HT
                    for term in range(4):
                        rows = slice(32 * hh + 4 * term, 32 * hh + 4 * term + 4)
                        sp.dma_start(qn[rows, :, PAD:PAD + HT],
                                     S["qk0"][b, term // 2, 0:32, tok:tok + HT].rearrange("(s c) t -> c s t", c=LR))\
                          .then_inc(loaded, 16)
                        sp.dma_start(kn[rows, :, :].bitcast(F32),
                                     S["qk0"][b, (0, 1, 1, 0)[term], 32:64, tok:tok + HT]
                                     .rearrange("(s c) t -> c s t", c=LR)).then_inc(loaded, 16)
                for s in range(SUB):
                    src = S["v0"][b, g * (4 * HT):(g + 1) * (4 * HT), HD * s:HD * s + HD]
                    sp.dma_start(vn[14 * s:14 * s + 14, :, :], src.rearrange("(m t) d -> t m d", t=14))\
                      .then_inc(loaded, 16)

            def store(g, b):
                sp.wait_ge(out_read, (g * B + b + 1) * QT)
                sp.dma_start(S["y0T"][b * 2 + g], yT[:, :]).then_inc(stored, 16)

            def load_bias(g):
                for h in range(4):
                    if g > 0 or h >= 2:
                        sp.wait_ge(bias_done, g * 4 + h - 1)
                    sp.dma_start(bnat[:, h % 2, :, :], S["bias"][g * 4 + h].rearrange("o p f -> p o f"))\
                      .then_inc(bias_loaded[h % 2], 16)

            sp.sem_inc(stored, 16)
            sp.wait_ge(zeroed, 2)
            load(0, 0, None)
            sp.dma_start(idn[:, :], A["eye"][0:TT, 0:TT]).then_inc(consts, 16)
            load_bias(0)
            for g in range(2):
                with sp.Fori(0, B - 1) as b:
                    load(g, b + 1, g * B + b + 1)
                    store(g, b)
                if g == 0:
                    load(1, 0, B)
                store(g, B - 1)
                if g == 0:
                    load_bias(1)
            sp.wait_ge(stored, (2 * B + 1) * 16)

        @block.tensor
        def _(pe):
            pe.wait_ge(consts, 16)
            with pe.Fori(0, 2 * B) as it:
                pe.wait_ge(keys_placed, it + 1)
                pe.wait_ge(queries_placed, it + 1)
                for n in range(4 * QT + MIX):
                    if n < U:
                        r, hh = divmod(n, 4)
                        if n >= 3:
                            pe.wait_ge(maxed, it * U + n - 2)
                        rows = slice(32 * hh, 32 * hh + 16)
                        pe.matmul(PS[0:TT, BS + n % 3, 0:KW].rearrange("p (c s t) -> p c s t", c=4, s=SUB),
                                  qp[rows, TT * r:TT * r + TT],
                                  kp[rows, :, TR * kv[r]:TR * kv[r] + 56].rearrange("p s (c t) -> p c s t", c=4),
                                  start=True, stop=True).then_inc(scored, 1)
                    if TURN <= n < U + TURN:
                        m = n - TURN
                        pe.wait_ge(normed, it * U + m + 1)
                        if m >= 3:
                            pe.wait_ge(copied, it * U + m - 2)
                        for c in range(4):
                            last = pe.transpose(PS[0:TT, BT + m % 3, TT * c:TT * c + TT],
                                                P[:, m % NP, TT * c:TT * c + TT], idn[:, :])
                        last.then_inc(turned, 1)
                    if n >= MIX:
                        r, c = divmod(n - MIX, 4)
                        if c == 0:
                            pe.wait_ge(copied, it * U + 4 * r + 4)
                            if r == 0:
                                pe.wait_ge(values_placed, it + 1)
                            if r >= 2:
                                pe.wait_ge(out_read, it * QT + r - 1)
                        for hh in range(4):
                            last = pe.matmul(PS[32 * hh:32 * hh + 32, BO + r % 2, 0:TT],
                                             vt[:, NT * hh + kv[r] // 2 + c, :],
                                             PTs[:, (4 * r + hh) % NPT, TT * c:TT * c + TT],
                                             start=(c == 0), stop=(c == 3))
                        if c == 3:
                            last.then_inc(mixed, 1)
                pe.wait_ge(out_read, (it + 1) * QT)

        @block.vector
        def _(dve):
            def read_out(it, r):
                dve.wait_ge(mixed, it * QT + r + 1)
                if r == 0:
                    dve.wait_ge(stored, (it + 1) * 16)
                t0, t1 = (7, 14) if r == 0 else (0, 7) if r == QT - 1 else (0, 14)
                p0 = W * (2 * r - 1) + SUB * t0
                dve.tensor_copy(yT[:, p0:p0 + SUB * (t1 - t0)].rearrange("p (t s) -> p s t", s=SUB),
                                PS[:, BO + r % 2, 0:TT].rearrange("p (s t) -> p s t", s=SUB)[:, :, t0:t1])\
                   .then_inc(out_read, 1)

            dve.memset(qn[:, :, :], 0.0).then_inc(zeroed, 1)
            dve.memset(kn[:, :, :].bitcast(F32), 0.0).then_inc(zeroed, 1)
            with dve.Fori(0, 2) as g:
                for h in range(4):
                    dve.wait_ge(bias_loaded[h % 2], g * 32 + (h // 2 + 1) * 16)
                    dve.tensor_copy(bias[:, h, :, :].rearrange("p o (c s t) -> p (o c) s t", c=4, s=SUB),
                                    bnat[:, h % 2, :, :].rearrange("p o (c t s) -> p (o c) s t", c=4, s=SUB))\
                       .then_inc(bias_done, 1)
                dve.wait_ge(bias_done, (g + 1) * 4)
                dve.sem_inc(steps, 1)
                with dve.Fori(0, B) as b:
                    it = g * B + b
                    dve.wait_ge(loaded, (it + 1) * NLOAD)
                    dve.tensor_copy(qp[:, :].rearrange("p (r s t) -> p r s t", r=QT, s=SUB),
                                    qn[:, :, :].rearrange("p s (r t) -> p r s t", r=QT)).then_inc(queries_placed, 1)
                    for n in range(4 * (QT - 1) + READ + 1):
                        if n < U:
                            r, hh = divmod(n, 4)
                            if n >= NSM:
                                dve.wait_ge(exped, it * U + n - NSM + 1)
                            dve.wait_ge(scored, it * U + n + 1)
                            dve.sem_inc(steps, 1)
                            dve.tensor_tensor_reduce(out=sm[:, n % NSM, :], in0=PS[0:TT, BS + n % 3, 0:KW],
                                                     in1=bias[:, hh, case_of(r), :], scale=1.0, scalar=3.0e38,
                                                     op0=ALU.add, op1=ALU.min, accum_out=mx[:, n % 8:n % 8 + 1])\
                               .then_inc(maxed, 1)
                        if NORM <= n < U + NORM:
                            m = n - NORM
                            dve.wait_ge(inverted, it * U + m + 1)
                            dve.tensor_scalar(P[:, m % NP, :], P[:, m % NP, :], rc[:, m % 8:m % 8 + 1], None,
                                              ALU.mult).then_inc(normed, 1)
                        if INVERT <= n < U + INVERT:
                            m = n - INVERT
                            dve.wait_ge(exped, it * U + m + 1)
                            dve.reciprocal(rc[:, m % 8:m % 8 + 1], rs[:, m % 8:m % 8 + 1]).then_inc(inverted, 1)
                        if n >= READ and (n - READ) % 4 == 0:
                            read_out(it, (n - READ) // 4)

        @block.scalar
        def _(act):
            with act.Fori(0, 2 * B) as it:
                act.wait_ge(loaded, (it + 1) * NLOAD)
                act.activation(vt[:, :, :], vn[:, :, :], ACT.Copy).then_inc(values_placed, 1)
                for n in range(U + COPY):
                    if n < U:
                        act.wait_ge(maxed, it * U + n + 1)
                        if n >= NP:
                            act.wait_ge(turned, it * U + n - NP + 1)
                        act.activation(P[:, n % NP, :], sm[:, n % NSM, :], ACT.Exp, bias=mx[:, n % 8:n % 8 + 1],
                                       scale=-1.0, accum_out=rs[:, n % 8:n % 8 + 1]).then_inc(exped, 1)
                    if n >= COPY:
                        m = n - COPY
                        act.wait_ge(turned, it * U + m + 1)
                        if m >= NPT and m % 4 == 0:
                            act.wait_ge(mixed, it * QT + (m - NPT) // 4 + 1)
                        act.activation(PTs[:, m % NPT, :], PS[0:TT, BT + m % 3, 0:KW], ACT.Copy).then_inc(copied, 1)
                act.wait_ge(mixed, (it + 1) * QT)

        @block.gpsimd
        def _(pool):
            with pool.Fori(0, 2 * B) as it:
                pool.wait_ge(loaded, (it + 1) * NLOAD)
                pool.sem_inc(steps, 1)
                pool.tensor_copy(kp[:, :, :], kn[:, :, :]).then_inc(keys_placed, 1)
                pool.wait_ge(scored, (it + 1) * U)


def layer0_output(nc, A, S):
    with ExitStack() as ctx:
        def sb(name, shape, dt=F32):
            return ctx.enter_context(nc.sbuf_tensor("o0_" + name, shape, dt))

        def sem(name):
            return ctx.enter_context(nc.semaphore("o0_" + name))

        QB = 4
        idn = sb("idn", [TT, TT])
        wp = sb("wp", [128, CC, C])
        wqkv = sb("wqkv", [128, CC, 3 * C])
        bqk = sb("bqk", [128, QB])
        bpb = sb("bpb", [TT, C])
        bvb = sb("bvb", [128, C])
        yT = sb("yT", [128, CC, N])
        ts = sb("ts", [TT, NT, C])
        xn = sb("xn", [TT, 4, C])
        xT = sb("xT", [128, CC, N])
        stats = sb("stats", [TT, NT, 6])
        mv = sb("mv", [TT, NT, 2])
        rstd = sb("rstd", [TT, NT])
        tmp = sb("tmp", [128, 2, GW])
        high = sb("high", [128, 2, N], F32R)
        low = sb("low", [128, 2, N], F32R)
        vs = sb("vs", [128, KT, C])
        idle = sb("idle", [TT, 2])
        spread, rooted = sem("spread"), sem("rooted")
        steps = sem("steps")
        PS = ctx.enter_context(nc.psum_tensor("o0_ps", [128, 8, 512], F32))

        consts, loaded, made, summed, normed = sem("consts"), sem("loaded"), sem("made"), sem("summed"), sem("normed")
        turned, copied, chain = sem("turned"), sem("copied"), sem("chain")
        qk_made, qk_read, qk_split = sem("qk_made"), sem("qk_read"), sem("qk_split")
        v_made, v_read = sem("v_made"), sem("v_read")
        part_stored = [sem("part_stored0"), sem("part_stored1")]
        v_stored, t_stored, image_done = sem("v_stored"), sem("t_stored"), sem("image_done")
        CHAIN = 4 + QB * NG
        block = ctx.enter_context(nc.Block())

        @block.sync
        def _(sp):
            sp.dma_start(bqk[:, :], A["b_qkv"][0:2 * C].rearrange("(q p) -> p q", p=128),
                         allow_slow_non_contiguous=True).then_inc(consts, 16)
            for dst, src in ((idn[:, :], A["eye"][0:TT, 0:TT]),
                             (wp[:, :, :], A["Wp0"].rearrange("(c p) n -> p c n", p=128)),
                             (wqkv[:, :, :], A["w_qkv"].rearrange("(c p) n -> p c n", p=128)),
                             (bpb[:, :], A["bp0"].rearrange("(a n) -> a n", a=1).to_broadcast([TT, C])),
                             (bvb[:, :], A["b_qkv"][2 * C:3 * C].rearrange("(a n) -> a n", a=1).to_broadcast([128, C]))):
                sp.dma_start(dst, src).then_inc(consts, 16)
            with sp.Fori(0, B) as b:
                sp.dma_start(yT[:, :, :], S["y0T"][bass.ds(b * 2, 2)].rearrange("c p n -> p c n")).then_inc(loaded, 16)
                sp.dma_start(ts[:, :, :], A["x"][b].rearrange("(j p) c -> p j c", p=TT)).then_inc(loaded, 16)
                sp.wait_ge(summed, (b + 1) * NT)
                sp.dma_start(S["t0"][b].rearrange("(j p) c -> p j c", p=TT), ts[:, :, :]).then_inc(t_stored, 16)
                for q in range(QB):
                    sp.wait_ge(qk_split, b * (QB * NG) + (q + 1) * NG)
                    sp.sem_inc(steps, 1)
                    for part, src in ((0, high), (1, low)):
                        sp.dma_start(S["q1" if q < 2 else "k1"][part, b * 2 + q % 2],
                                     src[:, q % 2, :].bitcast(F32)).then_inc(part_stored[q % 2], 16)
                sp.wait_ge(v_read, (b + 1) * KT)
                sp.sem_inc(steps, 1)
                for g in range(2):
                    sp.dma_start(S["v1"][b * 2 + g, :, 0:KT - 1, :], vs[:, 0:KT - 1, 128 * g:128 * g + 128])\
                      .then_inc(v_stored, 16)
                    sp.dma_start(S["v1"][b * 2 + g, 0:KTAIL, KT - 1, :],
                                 vs[0:KTAIL, KT - 1, 128 * g:128 * g + 128]).then_inc(v_stored, 16)
                for w in range(2):
                    sp.wait_ge(part_stored[w], (b + 1) * (QB * 16))
                    sp.sem_inc(steps, 1)
                sp.wait_ge(v_stored, (b + 1) * 64)
                sp.sem_inc(steps, 1)
                sp.wait_ge(t_stored, (b + 1) * 16)
                sp.sem_inc(image_done, 1)

        @block.tensor
        def _(pe):
            pe.wait_ge(consts, 96)
            with pe.Fori(0, B) as b:
                pe.wait_ge(loaded, (b + 1) * 32)
                for j in range(NT):
                    if j >= 4:
                        pe.wait_ge(summed, b * NT + j - 3)
                    for c in range(CC):
                        last = pe.matmul(PS[0:TT, j % 4, 0:C], yT[:, c, TT * j:TT * j + TT], wp[:, c, :],
                                         start=(c == 0), stop=(c == CC - 1))
                    last.then_inc(made, 1)
                for g in range(NG):
                    pe.wait_ge(normed, b * NT + 4 * g + 4)
                    if g >= 2:
                        pe.wait_ge(copied, b * (CC * NG) + 2 * g - 2)
                    for c in range(CC):
                        for u in range(4):
                            last = pe.transpose(PS[:, 4 + (2 * g + c) % 4, TT * u:TT * u + TT],
                                                xn[:, u, 128 * c:128 * c + 128], idn[:, :])
                        last.then_inc(turned, 1)
                pe.wait_ge(copied, (b + 1) * (CC * NG))
                for n in range(QB * NG):
                    q, g = divmod(n, NG)
                    if n >= 4:
                        pe.wait_ge(qk_read, b * (QB * NG) + n - 3)
                    for c in range(CC):
                        last = pe.matmul(PS[:, n % 4, 0:GW], wqkv[:, c, 128 * q:128 * q + 128],
                                         xT[:, c, GW * g:GW * g + GW], start=(c == 0), stop=(c == CC - 1))
                    last.then_inc(qk_made, 1)
                for j in range(KT):
                    rows = 128 if j < KT - 1 else KTAIL
                    if j >= 4:
                        pe.wait_ge(v_read, b * KT + j - 3)
                    for c in range(CC):
                        last = pe.matmul(PS[0:rows, 4 + j % 4, 0:C], xT[:, c, 128 * j:128 * j + rows],
                                         wqkv[:, c, 2 * C:3 * C], start=(c == 0), stop=(c == CC - 1))
                    last.then_inc(v_made, 1)
                pe.wait_ge(image_done, b + 1)

        @block.scalar
        def _(act):
            with act.Fori(0, B) as b:
                root(act, rstd[:, :], spread, rooted, b + 1)
                for k in range(CC * NG):
                    g, c = divmod(k, CC)
                    act.wait_ge(turned, b * (CC * NG) + k + 1)
                    act.activation(xT[:, c, GW * g:GW * g + GW], PS[:, 4 + k % 4, 0:GW], ACT.Copy).then_inc(copied, 1)
                act.wait_ge(image_done, b + 1)

        @block.vector
        def _(dve):
            dve.memset(idle[:, :], 0.0)
            dve.wait_ge(consts, 96)
            with dve.Fori(0, B) as b:
                ch = Count(dve, chain, b * CHAIN)
                dve.wait_ge(loaded, (b + 1) * 32)
                for j in range(NT):
                    last = dve.tensor_tensor(ts[:, j, :], ts[:, j, :], bpb[:, :], ALU.add)
                ch.after(last)
                for j in range(NT):
                    dve.wait_ge(made, b * NT + j + 1)
                    dve.tensor_tensor(ts[:, j, :], PS[0:TT, j % 4, 0:C], ts[:, j, :], ALU.add).then_inc(summed, 1)
                    if j >= 1:
                        dve.wait_ge(summed, b * NT + j)
                        dve.bn_stats(stats[:, j - 1, :], ts[:, j - 1, :])
                dve.wait_ge(summed, (b + 1) * NT)
                ch.after(dve.bn_stats(stats[:, NT - 1, :], ts[:, NT - 1, :]))
                dve.tensor_copy(idle[:, 1:2], idle[:, 0:1])
                for j in range(NT):
                    last = dve.bn_aggr(mv[:, j, :], stats[:, j, :])
                ch.after(last)
                inverse_root(dve, ch, rstd[:, :], mv[:, :, 1], 1e-5, spread, rooted, b + 1)
                for j in range(NT):
                    if j >= 4:
                        dve.wait_ge(turned, b * (CC * NG) + 2 * (j // 4))
                    dve.tensor_scalar(xn[:, j % 4, :], ts[:, j, :], mv[:, j, 0:1], rstd[:, j:j + 1],
                                      ALU.subtract, ALU.mult).then_inc(normed, 1)
                for n in range(QB * NG):
                    q, g = divmod(n, NG)
                    dve.wait_ge(qk_made, b * (QB * NG) + n + 1)
                    t = tmp[:, n % 2, :]
                    dve.tensor_scalar(t, PS[:, n % 4, 0:GW], bqk[:, q:q + 1], float(C) ** -0.5 if q < 2 else 1.0,
                                      ALU.add, ALU.mult).then_inc(qk_read, 1)
                    if q >= 2 and g == 0:
                        dve.wait_ge(part_stored[q % 2], b * (QB * 16) + 32)
                    dve.wait_ge(qk_read, b * (QB * NG) + n + 1)
                    at = slice(GW * g, GW * g + GW)
                    ch.after(dve.tensor_copy(high[:, q % 2, at], t))
                    dve.tensor_tensor(low[:, q % 2, at], t, high[:, q % 2, at].bitcast(F32), ALU.subtract)\
                       .then_inc(qk_split, 1)
                for j in range(KT):
                    rows = 128 if j < KT - 1 else KTAIL
                    dve.wait_ge(v_made, b * KT + j + 1)
                    dve.tensor_tensor(vs[0:rows, j, :], PS[0:rows, 4 + j % 4, 0:C], bvb[0:rows, :], ALU.add)\
                       .then_inc(v_read, 1)
                assert ch.n == CHAIN
                dve.wait_ge(image_done, b + 1)


def layer1_attend(nc, A, S):
    with ExitStack() as ctx:
        def sb(name, shape, dt=F32):
            return ctx.enter_context(nc.sbuf_tensor("a1_" + name, shape, dt))

        def sem(name):
            return ctx.enter_context(nc.semaphore("a1_" + name))

        QUADS = 2 * B
        STEPS = NG * KT
        MX = 4 * KT * NG
        HMX = KT * NG
        PAIRS = KT // 2
        SUMS = PAIRS + 1
        HS = 4 * STEPS
        LAG = 5
        RING, MAXES = 5, 3
        HEAD_STEPS = 42
        idn = sb("idn", [128, 128])
        ones = sb("ones", [128, HD])
        qp = sb("qp", [98, 4, N], F32R)
        kp = sb("kp", [98, 4, N], F32R)
        hq = sb("hq", [96, N], F32R)
        hk = sb("hk", [96, N], F32R)
        vt = sb("vt", [128, KT, 128])
        tops = sb("tops", [128, 4 * KT, NG])
        top = sb("top", [128, 4 * KT])
        neg = sb("neg", [4 * KT, 128])
        negh = sb("negh", [4 * KT, 128], F32R)
        negl = sb("negl", [4 * KT, 128], F32R)
        P = sb("P", [128, 2 * RING, 2, GW])
        added2 = sb("added2", [128, 6, 2, GW])
        sums = sb("sums", [128, GW])
        y = sb("y", [128, 2, GW])
        yo = sb("yo", [128, 2, GW])
        PS = ctx.enter_context(nc.psum_tensor("a1_ps", [128, 8, 512], F32))
        MAX, MIX, SUM = 3, 6, 7

        consts, cleared, loaded, head_loaded = sem("consts"), sem("cleared"), sem("loaded"), sem("head_loaded")
        keyed, topped, chain, top_turned = sem("keyed"), sem("topped"), sem("chain"), sem("top_turned")
        neg_stored, neg_loaded = sem("neg_stored"), sem("neg_loaded")
        scored, exped, added, mixed, summed = sem("scored"), sem("exped"), sem("added"), sem("mixed"), sem("summed")
        taken, sums_taken = sem("taken"), sem("sums_taken")
        inverted, divided = sem("inverted"), sem("divided")
        stored = [sem("stored0"), sem("stored1")]
        steps = sem("steps")
        CHAIN = 5
        KGROUPS = [(5 * u, min(5 * u + 5, KT)) for u in range(KT // 5)]
        LOADS = 3 * NG + 3 * len(KGROUPS) + len(KGROUPS) + 1

        def rows_of(t):
            return 128 if t < KT - 1 else KTAIL

        def sum_number(j, u):
            return SUMS * j + u + 1 + (2 * u + 1 + LAG >= KT)

        LAST_SUM = len([u for u in range(PAIRS) if 2 * u + 1 + LAG < KT]) + 1

        def work(n):
            return 4 * n + 2 * (n // 2)

        def maxima_by(n):
            hh = min(n // HEAD_STEPS, 3)
            first, end = HEAD_STEPS * hh + 1, HEAD_STEPS * hh + HEAD_STEPS - 3
            done = work(min(max(n, first), end)) - work(first)
            return HMX * hh + HMX * done // (work(end) - work(first))

        block = ctx.enter_context(nc.Block())

        @block.sync
        def _(sp):
            def load_q(m, j):
                for term in range(3):
                    sp.dma_start(qp[32 * term:32 * term + 32, :, GW * j:GW * j + GW].bitcast(F32),
                                 S["q1"][(0, 0, 1)[term], m].rearrange("(h d) n -> d h n", d=HD)
                                 [:, :, GW * j:GW * j + GW]).then_inc(loaded, 16)

            def load_kv(m, u):
                t0, t1 = KGROUPS[u]
                c0, c1 = 128 * t0, min(128 * t1, N)
                for term in range(3):
                    sp.dma_start(kp[32 * term:32 * term + 32, :, c0:c1].bitcast(F32),
                                 S["k1"][(0, 1, 0)[term], m].rearrange("(h d) n -> d h n", d=HD)[:, :, c0:c1])\
                      .then_inc(loaded, 16)
                full = min(t1, KT - 1)
                sp.dma_start(vt[:, t0:full, :], S["v1"][m, :, t0:full, :]).then_inc(loaded, 16)
                if t1 == KT:
                    sp.dma_start(vt[0:KTAIL, KT - 1, :], S["v1"][m, 0:KTAIL, KT - 1, :]).then_inc(loaded, 16)

            def move_neg(m):
                sp.wait_ge(chain, (m + 1) * CHAIN)
                sp.dma_start(S["neg"][0], negh[:, :].bitcast(F32)).then_inc(neg_stored, 16)
                sp.dma_start(S["neg"][1], negl[:, :].bitcast(F32)).then_inc(neg_stored, 16)
                sp.wait_ge(neg_stored, (m + 1) * 32)
                sp.dma_start(qp[96:98, :, :].bitcast(F32),
                             S["neg"].rearrange("u (h t) p -> u h (t p)", h=4)[:, :, 0:N]).then_inc(neg_loaded, 16)

            def store_y(q, j):
                sp.wait_ge(divided, q * NG + j + 1)
                sp.dma_start(S["y1T"][q, :, GW * j:GW * j + GW], yo[:, j % 2, :]).then_inc(stored[j % 2], 16)

            def quad(q, more):
                m = q + 1
                for n in range(STEPS + 1):
                    if more and n in (1, HEAD_STEPS, 2 * HEAD_STEPS, 3 * HEAD_STEPS):
                        hh = n // HEAD_STEPS
                        sp.wait_ge(keyed, m * MX + HMX * hh)
                        for term in range(3):
                            rows = slice(32 * term, 32 * term + 32)
                            head = slice(HD * hh, HD * hh + HD)
                            sp.dma_start(hq[rows, :].bitcast(F32), S["q1"][(0, 0, 1)[term], m, head, :])\
                              .then_inc(head_loaded, 16)
                            sp.dma_start(hk[rows, :].bitcast(F32), S["k1"][(0, 1, 0)[term], m, head, :])\
                              .then_inc(head_loaded, 16)
                    if more and n > 0 and n % KT == 0:
                        sp.wait_ge(scored, q * HS + 4 * n)
                        load_q(m, n // KT - 1)
                    if n > KT and n % KT == 11:
                        store_y(q, n // KT - 1)
                    if more and n > STEPS - KT and n % 5 == 0:
                        sp.wait_ge(mixed, q * STEPS + n)
                        load_kv(m, (n - (STEPS - KT)) // 5 - 1)
                if more:
                    move_neg(m)
                store_y(q, NG - 1)

            sp.dma_start(idn[:, :], A["eye"]).then_inc(consts, 16)
            for j in range(NG):
                load_q(0, j)
            for u in range(len(KGROUPS)):
                load_kv(0, u)
            move_neg(0)
            with sp.Fori(0, QUADS - 1) as q:
                quad(q, True)
            quad(QUADS - 1, False)
            for w in range(2):
                sp.wait_ge(stored[w], QUADS * 16 * ((NG + 1 - w) // 2))

        @block.tensor
        def _(pe):
            def product_for_maximum(m, i, q_of, k_of):
                hh, t, k = i // HMX, i // NG % KT, i % NG
                if i >= MAXES:
                    pe.wait_ge(topped, m * MX + i - MAXES + 1)
                if q_of(0) is hq and i % HMX == 0:
                    pe.wait_ge(head_loaded, (m - 1) * (4 * 96) + (hh + 1) * 96)
                pe.matmul(PS[0:rows_of(t), MAX + i % MAXES, 0:GW], q_of(hh)[:, 128 * t:128 * t + rows_of(t)],
                          k_of(hh)[:, GW * k:GW * k + GW], start=True, stop=True).then_inc(keyed, 1)

            def turn_maxima(m):
                pe.wait_ge(chain, m * CHAIN + 2)
                pe.transpose(PS[0:4 * KT, MAX + 1, 0:128], top[:, :], idn[:, :]).then_inc(top_turned, 1)

            def mix(q, n):
                j, t = divmod(n, KT)
                rows = rows_of(t)
                pe.wait_ge(exped, q * HS + 4 * n + 4)
                if t == 0 and j >= 1:
                    pe.wait_ge(taken, q * NG + j)
                if rows < 128:
                    pe.sem_inc(steps, 1)
                for hh in range(4):
                    last = pe.matmul(PS[HD * hh:HD * hh + HD, MIX, 0:GW], vt[0:rows, t, HD * hh:HD * hh + HD],
                                     P[0:rows, (2 * n + hh // 2) % (2 * RING), hh % 2, :], start=(t == 0), stop=(t == KT - 1))
                last.then_inc(mixed, 1)
                if t == KT - 1:
                    for hh in range(4):
                        last = pe.matmul(PS[HD * hh:HD * hh + HD, SUM, 0:GW], ones[0:rows, :],
                                         P[0:rows, (2 * n + hh // 2) % (2 * RING), hh % 2, :], start=False, stop=False)
                    last.then_inc(summed, 1)

            def sum_pair(q, j, u):
                pe.wait_ge(added, q * (2 * PAIRS * NG) + 2 * (PAIRS * j + u) + 2)
                if u == 0 and j >= 1:
                    pe.wait_ge(sums_taken, q * NG + j)
                for hh in range(4):
                    last = pe.matmul(PS[HD * hh:HD * hh + HD, SUM, 0:GW], ones[:, :],
                                     added2[:, (2 * (PAIRS * j + u) + hh // 2) % 6, hh % 2, :],
                                     start=(u == 0), stop=(u == PAIRS - 1))
                last.then_inc(summed, 1)

            def quad(q, more):
                m = q + 1
                pe.wait_ge(loaded, m * (16 * LOADS))
                pe.wait_ge(neg_loaded, m * 16)
                i = 0
                for n in range(STEPS + LAG):
                    due = maxima_by(n) if more else 0
                    parts = []
                    if n < STEPS:
                        parts += [("scores", 0, 2), ("scores", 2, 3), ("scores", 3, 4)]
                    if 1 <= n < STEPS + 1:
                        parts += [("mix", 0, 0)]
                    if n >= LAG and (n - LAG) % KT % 2 == 1:
                        parts += [("sum", 0, 0)]
                    for at, (what, h0, h1) in enumerate(parts):
                        if what == "scores":
                            j, t = divmod(n, KT)
                            for hh in range(h0, h1):
                                i_s = 4 * n + hh
                                if i_s >= 3:
                                    pe.wait_ge(exped, q * HS + i_s - 2)
                                pe.matmul(PS[0:rows_of(t), i_s % 3, 0:GW],
                                          kp[0:98, hh, 128 * t:128 * t + rows_of(t)],
                                          qp[0:98, hh, GW * j:GW * j + GW], start=True, stop=True).then_inc(scored, 1)
                        elif what == "mix":
                            mix(q, n - 1)
                        else:
                            sum_pair(q, (n - LAG) // KT, (n - LAG) % KT // 2)
                        until = i + (due - i + len(parts) - 1 - at) // (len(parts) - at)
                        while i < until:
                            product_for_maximum(m, i, lambda hh: hq, lambda hh: hk)
                            i += 1
                    if more and n == STEPS - 5:
                        assert i == MX
                        turn_maxima(m)
                pe.wait_ge(taken, m * NG)
                pe.wait_ge(sums_taken, m * NG)

            pe.wait_ge(consts, 16)
            pe.wait_ge(cleared, 3)
            pe.wait_ge(loaded, 16 * LOADS)
            for i in range(MX):
                product_for_maximum(0, i, lambda hh: qp[0:96, hh, :], lambda hh: kp[0:96, hh, :])
            turn_maxima(0)
            with pe.Fori(0, QUADS - 1) as q:
                quad(q, True)
            quad(QUADS - 1, False)

        @block.vector
        def _(dve):
            def maximum(m, i):
                hh, t, k = i // HMX, i // NG % KT, i % NG
                dve.wait_ge(keyed, m * MX + i + 1)
                dve.tensor_reduce(tops[0:rows_of(t), KT * hh + t, k:k + 1], PS[0:rows_of(t), MAX + i % MAXES, 0:GW],
                                  AX_X, ALU.max).then_inc(topped, 1)

            def negate(m):
                ch = Count(dve, chain, m * CHAIN)
                dve.wait_ge(topped, (m + 1) * MX)
                ch.after(dve.tensor_reduce(top[:, :], tops[:, :, :], AX_X, ALU.max))
                ch.after(dve.tensor_scalar(top[:, :], top[:, :], -1.0, None, ALU.mult))

            def split(m):
                ch = Count(dve, chain, m * CHAIN + 2)
                dve.wait_ge(top_turned, m + 1)
                ch.after(dve.tensor_copy(neg[:, :], PS[0:4 * KT, MAX + 1, 0:128]))
                ch.after(dve.tensor_copy(negh[:, :], neg[:, :]))
                ch.after(dve.tensor_tensor(negl[:, :], neg[:, :], negh[:, :].bitcast(F32), ALU.subtract))

            def invert(q, j, part):
                cols = slice(GW // 4 * part, GW // 4 * (part + 1))
                if part == 0:
                    dve.wait_ge(sums_taken, q * NG + j + 1)
                dve.reciprocal(sums[:, cols], sums[:, cols]).then_inc(inverted, 1)

            def divide(q, j):
                dve.wait_ge(taken, q * NG + j + 1)
                if j >= 2:
                    dve.wait_ge(stored[j % 2], q * (16 * ((NG + 1 - j % 2) // 2)) + 16 * (j // 2))
                dve.wait_ge(inverted, q * (4 * NG) + 4 * (j + 1))
                dve.tensor_tensor(yo[:, j % 2, :], y[:, j % 2, :], sums[:, :], ALU.mult).then_inc(divided, 1)

            def quad(q, more):
                m = q + 1
                i = 0
                for n in range(STEPS):
                    while more and i < maxima_by(n):
                        maximum(m, i)
                        i += 1
                    if more and i == MX and n == STEPS - 6:
                        negate(m)
                    if more and n == STEPS - 4:
                        split(m)
                    if n > KT and 6 <= n % KT < 10:
                        invert(q, n // KT - 1, n % KT - 6)
                    if n > KT and n % KT == 10:
                        divide(q, n // KT - 1)
                for part in range(4):
                    invert(q, NG - 1, part)
                divide(q, NG - 1)
                for w in range(2):
                    dve.wait_ge(stored[w], m * (16 * ((NG + 1 - w) // 2)))
                dve.wait_ge(divided, m * NG)

            dve.memset(tops[:, :, :], 0.0).then_inc(cleared, 1)
            dve.memset(ones[:, :], 1.0).then_inc(cleared, 1)
            dve.memset(kp[96:98, :, :].bitcast(F32), 1.0).then_inc(cleared, 1)
            for i in range(MX):
                maximum(0, i)
            negate(0)
            split(0)
            with dve.Fori(0, QUADS - 1) as q:
                quad(q, True)
            quad(QUADS - 1, False)

        @block.scalar
        def _(act):
            def take(q, j):
                act.wait_ge(mixed, q * STEPS + KT * (j + 1))
                if j >= 2:
                    act.wait_ge(divided, q * NG + j - 1)
                act.activation(y[:, j % 2, :], PS[:, MIX, 0:GW], ACT.Copy).then_inc(taken, 1)

            def take_sums(q, j):
                act.wait_ge(summed, q * (SUMS * NG) + SUMS * (j + 1))
                if j >= 1:
                    act.wait_ge(divided, q * NG + j)
                act.activation(sums[:, :], PS[:, SUM, 0:GW], ACT.Copy).then_inc(sums_taken, 1)

            def quad(q):
                for n in range(STEPS):
                    t = n % KT
                    for hh in range(4):
                        pair = hh // 2
                        if n >= RING and hh % 2 == 0:
                            j0, t0 = divmod(n - RING, KT)
                            if pair == 0:
                                act.wait_ge(mixed, q * STEPS + n - RING + 1)
                                if t0 == KT - 1:
                                    act.wait_ge(summed, q * (SUMS * NG) + SUMS * j0 + LAST_SUM)
                            if t0 < KT - 1:
                                act.wait_ge(added, q * (2 * PAIRS * NG) + 2 * (PAIRS * j0 + t0 // 2) + pair + 1)
                        act.wait_ge(scored, q * HS + 4 * n + hh + 1)
                        act.activation(P[0:rows_of(t), (2 * n + pair) % (2 * RING), hh % 2, :],
                                       PS[0:rows_of(t), (4 * n + hh) % 3, 0:GW], ACT.Exp).then_inc(exped, 1)
                    if t == 0 and n > 0:
                        take(q, n // KT - 1)
                    if t == LAG - 1 and n > KT:
                        take_sums(q, n // KT - 1)
                take(q, NG - 1)
                take_sums(q, NG - 1)
                act.wait_ge(mixed, (q + 1) * STEPS)
                act.wait_ge(summed, (q + 1) * (SUMS * NG))
                act.wait_ge(divided, (q + 1) * NG)

            with act.Fori(0, QUADS) as q:
                quad(q)

        @block.gpsimd
        def _(pool):
            with pool.Fori(0, QUADS) as q:
                for j in range(NG):
                    for u in range(PAIRS):
                        for pair in range(2):
                            n = KT * j + 2 * u
                            a = 2 * (PAIRS * j + u) + pair
                            if pair == 0 and a >= 6:
                                before = PAIRS * j + u - 3
                                pool.wait_ge(summed, q * (SUMS * NG) + sum_number(before // PAIRS, before % PAIRS))
                            pool.wait_ge(exped, q * HS + 4 * (n + 1) + 2 * pair + 2)
                            pool.tensor_tensor(added2[:, a % 6, :, :], P[:, (2 * n + pair) % (2 * RING), :, :],
                                               P[:, (2 * n + 2 + pair) % (2 * RING), :, :], ALU.add).then_inc(added, 1)
                pool.wait_ge(summed, (q + 1) * (SUMS * NG))


def layer1_output(nc, A, S):
    with ExitStack() as ctx:
        def sb(name, shape, dt=F32):
            return ctx.enter_context(nc.sbuf_tensor("o1_" + name, shape, dt))

        def sem(name):
            return ctx.enter_context(nc.semaphore("o1_" + name))

        idn = sb("idn", [TT, TT])
        wo = sb("wo", [128, CC, C])
        gw = sb("gw", [128, CC, EXP])
        bob = sb("bob", [TT, C])
        gbb = sb("gbb", [TT, EXP])
        yT = sb("yT", [128, CC, N])
        ts = sb("ts", [TT, NT, C])
        xn = sb("xn", [TT, 4, C])
        xT = sb("xT", [128, CC, N])
        stats = sb("stats", [TT, NT, 6])
        mv = sb("mv", [TT, NT, 2])
        rstd = sb("rstd", [TT, NT])
        lg = sb("lg", [TT, NT, EXP])
        zero = sb("zero", [1, C])
        idle = sb("idle", [TT, 2])
        spread, rooted = sem("spread"), sem("rooted")
        PS = ctx.enter_context(nc.psum_tensor("o1_ps", [128, 8, 512], F32))

        consts, loaded, made, summed, normed = sem("consts"), sem("loaded"), sem("made"), sem("summed"), sem("normed")
        turned, copied, chain, gated, gate_read = sem("turned"), sem("copied"), sem("chain"), sem("gated"), sem("gate_read")
        zeroed, zero_stored, stored, image_done = sem("zeroed"), sem("zero_stored"), sem("stored"), sem("image_done")
        CHAIN = 4
        block = ctx.enter_context(nc.Block())

        @block.sync
        def _(sp):
            for dst, src in ((idn[:, :], A["eye"][0:TT, 0:TT]),
                             (wo[:, :, :], A["w_out"].rearrange("(c p) n -> p c n", p=128)),
                             (gw[:, :, :], A["gate_w"].rearrange("(c p) n -> p c n", p=128)),
                             (bob[:, :], A["b_out"].rearrange("(a n) -> a n", a=1).to_broadcast([TT, C])),
                             (gbb[:, :], A["gate_b"].rearrange("(a n) -> a n", a=1).to_broadcast([TT, EXP]))):
                sp.dma_start(dst, src).then_inc(consts, 16)
            sp.wait_ge(zeroed, 1)
            sp.dma_start(S["t1"][T:T + 1, :], zero[:, :]).then_inc(zero_stored, 16)
            sp.wait_ge(zero_stored, 16)
            with sp.Fori(0, B) as b:
                sp.dma_start(yT[:, :, :], S["y1T"][bass.ds(b * 2, 2)].rearrange("c p n -> p c n")).then_inc(loaded, 16)
                sp.dma_start(ts[:, :, :], S["t0"][b].rearrange("(j p) c -> p j c", p=TT)).then_inc(loaded, 16)
                sp.wait_ge(summed, (b + 1) * NT)
                sp.dma_start(S["t1"][bass.ds(b * N, N), :].rearrange("(j p) c -> p j c", p=TT), ts[:, :, :])\
                  .then_inc(stored, 16)
                sp.dma_start(A["out"][b].rearrange("(j p) c -> p j c", p=TT), ts[:, :, :]).then_inc(stored, 16)
                sp.wait_ge(gate_read, (b + 1) * NT)
                sp.dma_start(S["logits"][:, bass.ds(b * NT, NT), :], lg[:, :, :]).then_inc(stored, 16)
                sp.wait_ge(stored, (b + 1) * 48)
                sp.sem_inc(image_done, 1)

        @block.tensor
        def _(pe):
            pe.wait_ge(consts, 80)
            with pe.Fori(0, B) as b:
                pe.wait_ge(loaded, (b + 1) * 32)
                for j in range(NT):
                    if j >= 4:
                        pe.wait_ge(summed, b * NT + j - 3)
                    for c in range(CC):
                        last = pe.matmul(PS[0:TT, j % 4, 0:C], yT[:, c, TT * j:TT * j + TT], wo[:, c, :],
                                         start=(c == 0), stop=(c == CC - 1))
                    last.then_inc(made, 1)
                for g in range(NG):
                    pe.wait_ge(normed, b * NT + 4 * g + 4)
                    if g >= 2:
                        pe.wait_ge(copied, b * (CC * NG) + 2 * g - 2)
                    for c in range(CC):
                        for u in range(4):
                            last = pe.transpose(PS[:, 4 + (2 * g + c) % 4, TT * u:TT * u + TT],
                                                xn[:, u, 128 * c:128 * c + 128], idn[:, :])
                        last.then_inc(turned, 1)
                pe.wait_ge(copied, (b + 1) * (CC * NG))
                for j in range(NT):
                    if j >= 4:
                        pe.wait_ge(gate_read, b * NT + j - 3)
                    for c in range(CC):
                        last = pe.matmul(PS[0:TT, j % 4, 0:EXP], xT[:, c, TT * j:TT * j + TT], gw[:, c, :],
                                         start=(c == 0), stop=(c == CC - 1))
                    last.then_inc(gated, 1)
                pe.wait_ge(image_done, b + 1)

        @block.scalar
        def _(act):
            with act.Fori(0, B) as b:
                root(act, rstd[:, :], spread, rooted, b + 1)
                for k in range(CC * NG):
                    g, c = divmod(k, CC)
                    act.wait_ge(turned, b * (CC * NG) + k + 1)
                    act.activation(xT[:, c, GW * g:GW * g + GW], PS[:, 4 + k % 4, 0:GW], ACT.Copy).then_inc(copied, 1)
                act.wait_ge(image_done, b + 1)

        @block.vector
        def _(dve):
            dve.memset(zero[:, :], 0.0).then_inc(zeroed, 1)
            dve.memset(idle[:, :], 0.0)
            dve.wait_ge(consts, 80)
            with dve.Fori(0, B) as b:
                ch = Count(dve, chain, b * CHAIN)
                dve.wait_ge(loaded, (b + 1) * 32)
                for j in range(NT):
                    last = dve.tensor_tensor(ts[:, j, :], ts[:, j, :], bob[:, :], ALU.add)
                ch.after(last)
                for j in range(NT):
                    dve.wait_ge(made, b * NT + j + 1)
                    dve.tensor_tensor(ts[:, j, :], PS[0:TT, j % 4, 0:C], ts[:, j, :], ALU.add).then_inc(summed, 1)
                    if j >= 1:
                        dve.wait_ge(summed, b * NT + j)
                        dve.bn_stats(stats[:, j - 1, :], ts[:, j - 1, :])
                dve.wait_ge(summed, (b + 1) * NT)
                ch.after(dve.bn_stats(stats[:, NT - 1, :], ts[:, NT - 1, :]))
                dve.tensor_copy(idle[:, 1:2], idle[:, 0:1])
                for j in range(NT):
                    last = dve.bn_aggr(mv[:, j, :], stats[:, j, :])
                ch.after(last)
                inverse_root(dve, ch, rstd[:, :], mv[:, :, 1], 1e-5, spread, rooted, b + 1)
                for j in range(NT):
                    if j >= 4:
                        dve.wait_ge(turned, b * (CC * NG) + 2 * (j // 4))
                    dve.tensor_scalar(xn[:, j % 4, :], ts[:, j, :], mv[:, j, 0:1], rstd[:, j:j + 1],
                                      ALU.subtract, ALU.mult).then_inc(normed, 1)
                for j in range(NT):
                    dve.wait_ge(gated, b * NT + j + 1)
                    dve.tensor_tensor(lg[:, j, :], PS[0:TT, j % 4, 0:EXP], gbb[:, :], ALU.add).then_inc(gate_read, 1)
                assert ch.n == CHAIN
                dve.wait_ge(image_done, b + 1)


def route(nc, A, S):
    with ExitStack() as ctx:
        def sb(name, shape, dt=F32):
            return ctx.enter_context(nc.sbuf_tensor("r_" + name, shape, dt))

        def sem(name):
            return ctx.enter_context(nc.semaphore("r_" + name))

        J = B * NT
        HALF = J // 2 * EXP
        lg = sb("lg", [TT, J, EXP])
        e1 = sb("e1", [TT, J, EXP])
        e2 = sb("e2", [TT, J, EXP])
        hot = sb("hot", [TT, J, EXP])
        back = sb("back", [TT, EXP])
        first = sb("first", [TT, EXP])
        upper = sb("upper", [TT, TT])
        ones = sb("ones", [TT, TT])
        top = sb("top", [TT, J])
        place = sb("place", [TT, J])
        prob = sb("prob", [TT, J])
        pos = sb("pos", [TT, J])
        kept = sb("kept", [TT, J])
        slot = sb("slot", [TT, J])
        slotu = sb("slotu", [TT, J], U32)
        before = sb("before", [TT, EXP, J])
        zeros = sb("zeros", [TT, J])
        token = sb("token", [TT, J])
        rows = sb("rows", [TT, J, 2])
        empty = sb("empty", [112, SLOTS // 112, 2])
        PS = ctx.enter_context(nc.psum_tensor("r_ps", [128, 4, 512], F32))
        loaded, chain, told, counted, shifted = sem("loaded"), sem("chain"), sem("told"), sem("counted"), sem("shifted")
        exped, table_cleared, scattered = sem("exped"), sem("table_cleared"), sem("scattered")
        emptied, placed = sem("emptied"), sem("placed")
        block = ctx.enter_context(nc.Block())

        def over_experts(x):
            return x.unsqueeze(2).to_broadcast([TT, J, EXP])

        def over_tokens(x):
            return x.unsqueeze(1).to_broadcast([TT, J, EXP])

        @block.sync
        def _(sp):
            for dst, src in ((lg[:, :, :], S["logits"]), (back[:, :], A["back"]), (first[:, :], A["first"]),
                             (upper[:, :], A["upper"]), (token[:, :], A["token"])):
                sp.dma_start(dst, src).then_inc(loaded, 16)
            sp.wait_ge(emptied, 2)
            sp.dma_start(S["table"].rearrange("(p a) b -> p a b", p=112), empty[:, :, :]).then_inc(table_cleared, 16)
            sp.wait_ge(table_cleared, 16)

        @block.gpsimd
        def _(pool):
            pool.memset(empty[:, :, 0], float(T)).then_inc(emptied, 1)
            pool.memset(empty[:, :, 1], 0.0).then_inc(emptied, 1)
            pool.wait_ge(table_cleared, 16)
            pool.wait_ge(placed, 1)
            for j in range(J):
                pool.indirect_dma_start(out=S["table"], out_offset=bass.IndirectOffsetOnAxis(ap=slotu[:, j:j + 1], axis=0),
                                        in_=rows[:, j, :], in_offset=None, bounds_check=SLOTS - 1,
                                        oob_is_err=False).then_inc(scattered, 16)
            pool.wait_ge(scattered, 16 * J)

        @block.scalar
        def _(act):
            act.wait_ge(shifted, 1)
            act.activation(e2[:, :, :], e2[:, :, :], ACT.Exp).then_inc(exped, 1)

        @block.tensor
        def _(pe):
            pe.wait_ge(told, 1)
            for half in range(2):
                cols = hot[:, :, :].rearrange("p j e -> p (j e)")[:, half * HALF:half * HALF + HALF]
                pe.matmul(PS[0:TT, half, 0:HALF], upper[:, :], cols, start=True, stop=True).then_inc(counted, 1)
                pe.matmul(PS[0:TT, 2 + half, 0:HALF], ones[:, :], cols, start=True, stop=True).then_inc(counted, 1)

        @block.vector
        def _(dve):
            ch = Count(dve, chain, 0)
            ch.after(dve.memset(ones[:, :], 1.0))
            ch.after(dve.memset(zeros[:, :], 0.0))
            dve.wait_ge(loaded, 80)
            ch.after(dve.tensor_reduce(top[:, :], lg[:, :, :], AX_X, ALU.max))
            ch.after(dve.tensor_tensor(e2[:, :, :], lg[:, :, :], over_experts(top[:, :]), ALU.subtract))
            ch.after(dve.tensor_scalar(e1[:, :, :], e2[:, :, :], 0.0, None, ALU.is_ge))
            dve.sem_inc(shifted, 1)
            ch.after(dve.tensor_tensor(e1[:, :, :], e1[:, :, :], over_tokens(back[:, :]), ALU.mult))
            ch.after(dve.tensor_reduce(place[:, :], e1[:, :, :], AX_X, ALU.max))
            dve.tensor_tensor(hot[:, :, :], over_tokens(back[:, :]), over_experts(place[:, :]), ALU.is_equal)\
               .then_inc(told, 1)
            dve.wait_ge(exped, 1)
            ch.after(dve.tensor_reduce(prob[:, :], e2[:, :, :], AX_X, ALU.add))
            dve.wait_ge(counted, 4)
            for half in range(2):
                last = dve.tensor_copy(e1[:, half * (J // 2):(half + 1) * (J // 2), :],
                                       PS[0:TT, 2 + half, 0:HALF].rearrange("p (j e) -> p j e", e=EXP))
            ch.after(last)
            for e in range(EXP):
                last = dve.tensor_tensor_scan(out=before[:, e, :], data0=e1[:, :, e], data1=zeros[:, :], initial=0.0,
                                              op0=ALU.add, op1=ALU.add)
            ch.after(last)
            ch.after(dve.tensor_tensor(e1[:, :, :], before[:, :, :].rearrange("p e j -> p j e"), e1[:, :, :],
                                       ALU.subtract))
            for half in range(2):
                part = e1[:, half * (J // 2):(half + 1) * (J // 2), :]
                last = dve.tensor_tensor(part, PS[0:TT, half, 0:HALF].rearrange("p (j e) -> p j e", e=EXP), part,
                                         ALU.add)
            ch.after(last)
            ch.after(dve.tensor_tensor(e2[:, :, :], e1[:, :, :], hot[:, :, :], ALU.mult))
            ch.after(dve.tensor_reduce(pos[:, :], e2[:, :, :], AX_X, ALU.add))
            ch.after(dve.tensor_tensor(e2[:, :, :], hot[:, :, :], over_tokens(first[:, :]), ALU.mult))
            ch.after(dve.tensor_reduce(slot[:, :], e2[:, :, :], AX_X, ALU.add))
            ch.after(dve.tensor_scalar(kept[:, :], pos[:, :], float(CAP), float(2 * SLOTS), ALU.is_gt, ALU.mult))
            ch.after(dve.tensor_tensor(slot[:, :], slot[:, :], pos[:, :], ALU.add))
            ch.after(dve.tensor_tensor(slot[:, :], slot[:, :], kept[:, :], ALU.add))
            ch.after(dve.tensor_scalar(slotu[:, :], slot[:, :], -1.0, None, ALU.add))
            ch.after(dve.reciprocal(rows[:, :, 1], prob[:, :]))
            dve.tensor_copy(rows[:, :, 0], token[:, :]).then_inc(placed, 1)


def experts(nc, A, S):
    with ExitStack() as ctx:
        def sb(name, shape, dt=F32):
            return ctx.enter_context(nc.sbuf_tensor("e_" + name, shape, dt))

        def sem(name):
            return ctx.enter_context(nc.semaphore("e_" + name))

        FB = FF // 128
        ST = (CAP + 127) // 128
        STAIL = CAP - 128 * (ST - 1)
        SG = (ST + 3) // 4
        idn = sb("idn", [128, 128])
        w1 = sb("w1", [128, 2, CC, FF])
        w2 = sb("w2", [128, 2, FB, C])
        b1 = sb("b1", [128, 2, FB])
        b2b = sb("b2b", [128, 2, C])
        tab = sb("tab", [128, 2, ST, 2])
        tok = sb("tok", [128, 2, ST], U32)
        xg = sb("xg", [128, 2, ST, C])
        xn = sb("xn", [128, 4, C])
        stats = sb("stats", [128, ST, 6])
        mv = sb("mv", [128, ST, 2])
        rstd = sb("rstd", [128, ST])
        xT = sb("xT", [128, 2, CC, 512])
        hT = sb("hT", [128, FB, 512])
        y = sb("y", [128, 2, C])
        none = sb("none", [128, C])
        fin = sb("fin", [128, 2, C], U8)
        nan = sb("nan", [128, 2, C], U8)
        yf = sb("yf", [128, 2, C])
        idle = sb("idle", [128, 2])
        spread, rooted = sem("spread"), sem("rooted")
        PS = ctx.enter_context(nc.psum_tensor("e_ps", [128, 8, 512], F32))
        consts, cleared, told, gathered = sem("consts"), sem("cleared"), sem("told"), sem("gathered")
        loaded = [sem("loaded0"), sem("loaded1")]
        chain, normed, turned, copied = sem("chain"), sem("normed"), sem("turned"), sem("copied")
        hidden, relued, made, finished = sem("hidden"), sem("relued"), sem("made"), sem("finished")
        read = sem("read")
        scattered = [sem("scattered0"), sem("scattered1")]
        emptied = sem("emptied")
        steps = sem("steps")
        CHAIN = 3 * SG + 4 * ST

        def size(t):
            return 128 if t < ST - 1 else STAIL

        def width(g):
            return min(512, CAP - 512 * g)

        block = ctx.enter_context(nc.Block())

        def for_experts(engine, expert):
            with engine.Fori(0, EXP // 2 - 1) as i:
                expert(i, 0, True)
                expert(i, 1, True)
            expert(EXP // 2 - 1, 0, True)
            expert(EXP // 2 - 1, 1, False)

        @block.sync
        def _(sp):
            def load(e, p):
                sp.dma_start(tab[:, p, 0:ST - 1, :],
                             S["table"][bass.ds(e * CAP, 128 * (ST - 1)), :].rearrange("(t p) b -> p t b", p=128))\
                  .then_inc(loaded[p], 16)
                sp.dma_start(tab[0:STAIL, p, ST - 1, :], S["table"][bass.ds(e * CAP + 128 * (ST - 1), STAIL), :])\
                  .then_inc(loaded[p], 16)
                sp.dma_start(w1[:, p, :, :], A["w1"][e].rearrange("(c p) n -> p c n", p=128)).then_inc(loaded[p], 16)
                sp.dma_start(w2[:, p, :, :], A["w2"][e].rearrange("(c p) n -> p c n", p=128)).then_inc(loaded[p], 16)
                sp.dma_start(b1[:, p, :], A["b1"][e].rearrange("(c p) -> p c", p=128),
                             allow_slow_non_contiguous=True).then_inc(loaded[p], 16)
                sp.dma_start(b2b[:, p, :], A["b2"][bass.ds(e, 1), :].to_broadcast([128, C])).then_inc(loaded[p], 16)

            sp.sem_inc(emptied, 1)
            sp.dma_start(idn[:, :], A["eye"]).then_inc(consts, 16)
            sp.wait_ge(cleared, 1)
            load(0, 0)
            load(1, 1)
            with sp.Fori(0, EXP // 2 - 1) as i:
                for p in range(2):
                    for w in scattered:
                        sp.wait_ge(w, (2 * i + p + 1) * (8 * ST))
                        sp.sem_inc(steps, 1)
                    sp.sem_inc(emptied, 1)
                    load(2 * i + p + 2, p)
            for e in (EXP - 2, EXP - 1):
                for w in scattered:
                    sp.wait_ge(w, (e + 1) * (8 * ST))
                sp.sem_inc(emptied, 1)

        @block.gpsimd
        def _(pool):
            def gather(e, p):
                pool.wait_ge(told, e + 1)
                pool.sem_inc(steps, 1)
                for t in range(ST):
                    pool.indirect_dma_start(out=xg[0:size(t), p, t, :], out_offset=None, in_=S["t1"],
                                            in_offset=bass.IndirectOffsetOnAxis(ap=tok[0:size(t), p, t:t + 1], axis=0))\
                        .then_inc(gathered, 16)

            def expert(i, p, more):
                e = 2 * i + p
                if more:
                    gather(e + 1, 1 - p)
                for t in range(ST):
                    pool.wait_ge(finished, e * ST + t + 1)
                    pool.sem_inc(steps, 1)
                    pool.indirect_dma_start(out=A["out_rows"],
                                            out_offset=bass.IndirectOffsetOnAxis(ap=tok[0:size(t), p, t:t + 1], axis=0),
                                            in_=yf[0:size(t), t % 2, :], in_offset=None, bounds_check=T - 1,
                                            oob_is_err=False).then_inc(scattered[t % 2], 16)

            gather(0, 0)
            for_experts(pool, expert)

        @block.tensor
        def _(pe):
            def turn(e, g):
                tiles = range(4 * g, min(4 * g + 4, ST))
                pe.wait_ge(normed, e * ST + tiles[-1] + 1)
                for c in range(CC):
                    if g >= 1:
                        pe.wait_ge(copied, e * (CC * SG) + (g - 1) * CC + c + 1)
                    for t in tiles:
                        last = pe.transpose(PS[:, c, 128 * (t % 4):128 * (t % 4) + size(t)],
                                            xn[0:size(t), t % 4, 128 * c:128 * c + 128],
                                            idn[0:size(t), 0:size(t)])
                    last.then_inc(turned, 1)

            def expert(i, p, more):
                e = 2 * i + p
                pe.wait_ge(loaded[p], (i + 1) * 96)
                turn(e, 0)
                for g in range(SG):
                    tiles = range(4 * g, min(4 * g + 4, ST))
                    pe.wait_ge(copied, e * (CC * SG) + (g + 1) * CC)
                    for f in range(FB):
                        n = g * FB + f
                        if n >= 3:
                            pe.wait_ge(relued, e * (SG * FB) + n - 2)
                        for c in range(CC):
                            last = pe.matmul(PS[:, 2 + n % 3, 0:width(g)], w1[:, p, c, 128 * f:128 * f + 128],
                                             xT[:, g % 2, c, 0:width(g)], start=(c == 0), stop=(c == CC - 1))
                        last.then_inc(hidden, 1)
                    if g < SG - 1:
                        turn(e, g + 1)
                    pe.wait_ge(relued, e * (SG * FB) + (g + 1) * FB)
                    for t in tiles:
                        pe.wait_ge(read, e * ST + t + 1)
                        for f in range(FB):
                            last = pe.matmul(PS[0:size(t), 5 + t % 2, 0:C],
                                             hT[:, f, 128 * (t % 4):128 * (t % 4) + size(t)], w2[:, p, f, :],
                                             start=(f == 0), stop=(f == FB - 1))
                        last.then_inc(made, 1)

            pe.wait_ge(consts, 16)
            for_experts(pe, expert)

        @block.scalar
        def _(act):
            def expert(i, p, more):
                e = 2 * i + p
                act.wait_ge(loaded[p], (i + 1) * 96)
                for g in range(SG):
                    root(act, rstd[:, 4 * g:min(4 * g + 4, ST)], spread, rooted, e * SG + g + 1)
                    for c in range(CC):
                        act.wait_ge(turned, e * (CC * SG) + g * CC + c + 1)
                        act.activation(xT[:, g % 2, c, 0:width(g)], PS[:, c, 0:width(g)], ACT.Copy).then_inc(copied, 1)
                    if g >= 1:
                        act.wait_ge(made, e * ST + 4 * g)
                    for f in range(FB):
                        n = g * FB + f
                        act.wait_ge(hidden, e * (SG * FB) + n + 1)
                        act.activation(hT[:, f, 0:width(g)], PS[:, 2 + n % 3, 0:width(g)], ACT.Relu,
                                       bias=b1[:, p, f:f + 1]).then_inc(relued, 1)
                act.wait_ge(made, (e + 1) * ST)

            for_experts(act, expert)

        @block.vector
        def _(dve):
            dve.memset(idle[:, :], 0.0)
            dve.memset(mv[:, :, :], 0.0)
            dve.memset(none[:, :], 0.0)
            dve.memset(tab[:, :, ST - 1, :], float(T)).then_inc(cleared, 1)
            dve.sem_inc(read, 2)

            def tell(i, p):
                dve.wait_ge(loaded[p], (i + 1) * 96)
                dve.tensor_copy(tok[:, p, :], tab[:, p, :, 0]).then_inc(told, 1)

            def expert(i, p, more):
                e = 2 * i + p
                ch = Count(dve, chain, e * CHAIN)

                def finish(t):
                    s = size(t)
                    y_, f_, n_, o_ = (v[0:s, t % 2, :] for v in (y, fin, nan, yf))
                    dve.wait_ge(made, e * ST + t + 1)
                    dve.tensor_tensor(y_, PS[0:s, 5 + t % 2, 0:C], b2b[0:s, p, :], ALU.add).then_inc(read, 1)
                    dve.wait_ge(read, e * ST + t + 3)
                    ch.after(dve.tensor_scalar(y_, y_, tab[0:s, p, t, 1:2], None, ALU.mult))
                    dve.tensor_scalar(f_, y_, 0.0, 0.0, ALU.mult, ALU.is_equal)
                    dve.tensor_tensor(n_, y_, y_, ALU.not_equal)
                    if t >= 2:
                        dve.wait_ge(scattered[t % 2], e * (8 * ST) + 16 * (t // 2))
                    else:
                        dve.wait_ge(emptied, e + 1)
                    ch.after(dve.tensor_scalar(o_, y_, -1.0e4, 1.0e4, ALU.max, ALU.min))
                    dve.tensor_copy(idle[:, 1:2], idle[:, 0:1])
                    ch.after(dve.copy_predicated(o_, n_, none[0:s, :]))
                    dve.tensor_copy(idle[:, 1:2], idle[:, 0:1])
                    ch.after(dve.copy_predicated(o_, f_, y_))
                    dve.tensor_tensor(o_, o_, xg[0:s, p, t, :], ALU.add).then_inc(finished, 1)

                for g in range(SG):
                    tiles = range(4 * g, min(4 * g + 4, ST))
                    for t in tiles:
                        s = size(t)
                        if t == 0:
                            dve.wait_ge(gathered, (e + 1) * (16 * ST))
                        last = dve.bn_stats(stats[0:s, t, :], xg[0:s, p, t, :])
                    ch.after(last)
                    dve.tensor_copy(idle[:, 1:2], idle[:, 0:1])
                    for t in tiles:
                        last = dve.bn_aggr(mv[0:size(t), t, :], stats[0:size(t), t, :])
                    ch.after(last)
                    inverse_root(dve, ch, rstd[:, 4 * g:tiles[-1] + 1], mv[:, 4 * g:tiles[-1] + 1, 1], 1e-5,
                                 spread, rooted, e * SG + g + 1)
                    for t in tiles:
                        s = size(t)
                        if g >= 1:
                            dve.wait_ge(turned, e * (CC * SG) + g * CC)
                        dve.tensor_scalar(xn[0:s, t % 4, :], xg[0:s, p, t, :], mv[0:s, t, 0:1], rstd[0:s, t:t + 1],
                                          ALU.subtract, ALU.mult).then_inc(normed, 1)
                    if g == 1 and more:
                        tell(i + p, 1 - p)
                    if g >= 1:
                        for t in range(4 * g - 4, 4 * g):
                            finish(t)
                for t in range(4 * SG - 4, ST):
                    finish(t)
                assert ch.n == CHAIN, ch.n

            tell(0, 0)
            for_experts(dve, expert)


STAGES = (layer0_project, layer0_attend, layer0_output, layer1_attend, layer1_output, route, experts)

SCRATCH = {
    "toeplitz": [W, NH * RPB, W],
    "bias": [NH, 5, TT, 8 * W],
    "qk0": [B, 2, 64, N],
    "v0": [B, N, C],
    "y0T": [2 * B, 128, N],
    "t0": [B, N, C],
    "q1": [2, 2 * B, 128, N],
    "k1": [2, 2 * B, 128, N],
    "v1": [2 * B, 128, KT, 128],
    "neg": [2, 4 * KT, 128],
    "y1T": [2 * B, 128, N],
    "t1": [T + 1, C],
    "logits": [TT, B * NT, EXP],
    "table": [SLOTS, 2],
}

INPUTS = {
    "x": "x", "L0_conv_Wq": "Wq0", "L0_conv_bq": "bq0", "L0_conv_Wk": "Wk0", "L0_conv_bk": "bk0",
    "L0_conv_Wv": "Wv0", "L0_conv_bv": "bv0", "L0_conv_rpb": "rpb", "L0_conv_Wp": "Wp0", "L0_conv_bp": "bp0",
    "L1_attn_w_qkv": "w_qkv", "L1_attn_b_qkv": "b_qkv", "L1_attn_w_out": "w_out", "L1_attn_b_out": "b_out",
    "L1_ffn_gate_w": "gate_w", "L1_ffn_gate_b": "gate_b", "L1_ffn_w1": "w1", "L1_ffn_b1": "b1",
    "L1_ffn_w2": "w2", "L1_ffn_b2": "b2",
}


def shape_constants():
    one = np.ones((128, 1), np.float32)
    group = C // 32
    return {
        "eye": np.eye(128, dtype=np.float32),
        "group_mean": np.kron(np.eye(128 // group, dtype=np.float32), np.full((group, group), 1.0 / group, np.float32)),
        "qk_scale": np.concatenate([one[:32] * np.float32(-HD ** -0.5), one[:32]]),
        "upper": np.triu(np.ones((TT, TT), np.float32)),
        "back": np.tile(np.arange(EXP, 0, -1, dtype=np.float32), (TT, 1)),
        "first": np.tile(np.arange(EXP, dtype=np.float32) * CAP, (TT, 1)),
        "token": np.arange(T, dtype=np.float32).reshape(B * NT, TT).T.copy(),
    }


def build(nc, A, S):
    A = dict(A)
    A["x"] = A["x"].rearrange("b h w c -> b (h w) c")
    A["out_rows"] = A["out"].rearrange("b h w c -> (b h w) c")
    A["out"] = A["out"].rearrange("b h w c -> b (h w) c")
    for stage in STAGES:
        stage(nc, A, S)


def kernel(**inputs):
    import concourse.bacc as bacc
    from concourse.bass_utils import run_bass_kernel_spmd

    nc = bacc.Bacc("TRN2", target_bir_lowering=False, num_devices=1)
    arrays, A = {}, {}
    given = {short: np.ascontiguousarray(inputs[name]) for name, short in INPUTS.items()}
    for short, a in {**given, **shape_constants()}.items():
        arrays["in_" + short] = a
        A[short] = nc.dram_tensor("in_" + short, a.shape, mybir.dt.from_np(a.dtype), kind="ExternalInput").ap()
    A["out"] = nc.dram_tensor("result", (B, H, W, C), F32, kind="ExternalOutput").ap()
    S = {n: nc.dram_tensor("scratch_" + n, s, F32, kind="Internal").ap() for n, s in SCRATCH.items()}
    build(nc, A, S)
    r = run_bass_kernel_spmd(nc, [arrays], core_ids=[0])
    return r.results[0]["result"]
```
